# Optimizing a Trainium2 kernel written in Bass

```python
import numpy as np
import jax
import jax.numpy as jnp

def _softmax(x, axis=-1):
    return jax.nn.softmax(x, axis=axis)

def _gelu(x):
    return jax.nn.gelu(x, approximate=True)

def _silu(x):
    return jax.nn.silu(x)

def _sigmoid(x):
    return jax.nn.sigmoid(x)

def _layernorm(x, axis=-1, eps=1e-05):
    m = jnp.mean(x, axis=axis, keepdims=True)
    v = jnp.var(x, axis=axis, keepdims=True)
    return (x - m) / jnp.sqrt(v + eps)

def _scatter_add(tgt, idx, src, axis=0):
    return tgt.at[idx].add(src)

def _segment_sum(src, seg, n):
    return jax.ops.segment_sum(src, seg, n)
kernel_name = 'mk_gps_d1_gnn_r8_70839d'

def setup_inputs(seed: int=0):
    np.random.seed(seed)
    _w = jnp.asarray

    def _rec_inputs():
        import jax
        import jax.numpy as jnp
        _gk = jax.random.key(seed)
        x = -0.0003713 + 1 * jax.random.normal(jax.random.fold_in(_gk, 1), (6250, 256), jnp.float32)
        src = jax.random.randint(jax.random.fold_in(_gk, 2), (200000,), 0, 6250, jnp.int32)
        dst = jax.random.randint(jax.random.fold_in(_gk, 3), (200000,), 0, 6250, jnp.int32)
        _o = jnp.argsort(dst, stable=True)
        src = src[_o]
        dst = dst[_o]
        return (x, src, dst)
    x, src, dst = _rec_inputs()

    def _L0_gnn_setup():
        import jax, jax.numpy as jnp
        import numpy as np
        N_NODES = 6250
        N_EDGES = 100000
        D = 256

        def _mean_aggregate(x, src, tgt, num_nodes):
            summed = jax.ops.segment_sum(x[src], tgt, num_segments=num_nodes)
            count = jax.ops.segment_sum(jnp.ones((src.shape[0],), x.dtype), tgt, num_segments=num_nodes)
            return summed / jnp.maximum(count, 1.0)[:, None]

        def _sage_conv(x, src, tgt, W_l, b, W_r):
            agg = _mean_aggregate(x, src, tgt, x.shape[0])
            return agg @ W_l + b + x @ W_r
        key = jax.random.key(seed)
        ks = jax.random.split(key, 8)
        s = 1.0 / np.sqrt(D)
        x = jax.random.normal(ks[0], (N_NODES, D), dtype=jnp.float32)
        edge_index = jax.random.randint(ks[1], (2, N_EDGES), 0, N_NODES, dtype=jnp.int64)
        return {'x': x, 'edge_index': edge_index, 'W1_l': jax.random.normal(ks[2], (D, D), dtype=jnp.float32) * s, 'b1': jnp.zeros((D,), dtype=jnp.float32), 'W1_r': jax.random.normal(ks[3], (D, D), dtype=jnp.float32) * s, 'W2_l': jax.random.normal(ks[4], (D, D), dtype=jnp.float32) * s, 'b2': jnp.zeros((D,), dtype=jnp.float32), 'W2_r': jax.random.normal(ks[5], (D, D), dtype=jnp.float32) * s}
    _L0_gnn_all = _L0_gnn_setup()
    _L0_gnn_in = {k: v for k, v in _L0_gnn_all.items() if k in ('W1_l', 'b1', 'W1_r', 'W2_l', 'b2', 'W2_r')}
    del _L0_gnn_all

    def _L0_mix_setup():
        import jax, jax.numpy as jnp
        import numpy as np
        NHEAD = 8
        ATT_EPS = 1e-06
        LN_EPS = 1e-05

        def _layernorm(x, g, b):
            mu = jnp.mean(x, axis=-1, keepdims=True)
            var = jnp.mean(jnp.square(x - mu), axis=-1, keepdims=True)
            return (x - mu) * jax.lax.rsqrt(var + LN_EPS) * g + b
        key = jax.random.key(seed)
        ks = jax.random.split(key, 7)
        N, L, C = (4, 2048, 256)
        s = 1.0 / np.sqrt(C)
        return {'x': jax.random.normal(ks[0], (N, L, C), jnp.float32), 'Wq': jax.random.normal(ks[1], (C, C), jnp.float32) * s, 'Wk': jax.random.normal(ks[2], (C, C), jnp.float32) * s, 'Wv': jax.random.normal(ks[3], (C, C), jnp.float32) * s, 'Wm': jax.random.normal(ks[4], (C, C), jnp.float32) * s, 'W1': jax.random.normal(ks[5], (2 * C, 2 * C), jnp.float32) * (1.0 / np.sqrt(2 * C)), 'W2': jax.random.normal(ks[6], (2 * C, C), jnp.float32) * (1.0 / np.sqrt(2 * C)), 'g1': jnp.ones((C,), jnp.float32), 'b1': jnp.zeros((C,), jnp.float32), 'g2': jnp.ones((C,), jnp.float32), 'b2': jnp.zeros((C,), jnp.float32)}
    _L0_mix_all = _L0_mix_setup()
    _L0_mix_in = {k: v for k, v in _L0_mix_all.items() if k in ('Wq', 'Wk', 'Wv', 'Wm', 'W1', 'W2', 'g1', 'b1', 'g2', 'b2')}
    del _L0_mix_all

    def _L0_ffn_setup():
        import jax, jax.numpy as jnp
        import numpy as np
        E = 8
        K = 2
        D = 256
        H = 512
        DOUT = 256
        EPS = 1e-05
        key = jax.random.key(seed)
        ks = jax.random.split(key, 9)
        s = 0.02
        return {'x': jax.random.normal(ks[0], (4, 1024, D), jnp.float32), 'gamma': 1.0 + 0.05 * jax.random.normal(ks[1], (D,), jnp.float32), 'beta': 0.05 * jax.random.normal(ks[2], (D,), jnp.float32), 'Wr': 0.01 * jax.random.normal(ks[3], (D, E), jnp.float32), 'br': jnp.zeros((E,), jnp.float32), 'W1': s * jax.random.normal(ks[4], (E, D, H), jnp.float32), 'b1': s * jax.random.normal(ks[5], (E, H), jnp.float32), 'W2': s * jax.random.normal(ks[6], (E, H, DOUT), jnp.float32), 'b2': s * jax.random.normal(ks[7], (E, DOUT), jnp.float32)}
    _L0_ffn_all = _L0_ffn_setup()
    _L0_ffn_in = {k: v for k, v in _L0_ffn_all.items() if k in ('gamma', 'beta', 'Wr', 'br', 'W1', 'b1', 'W2', 'b2')}
    del _L0_ffn_all
    return {'x': x, 'src': src, 'dst': dst, 'L0_gnn_W1_l': _L0_gnn_in['W1_l'], 'L0_gnn_b1': _L0_gnn_in['b1'], 'L0_gnn_W1_r': _L0_gnn_in['W1_r'], 'L0_gnn_W2_l': _L0_gnn_in['W2_l'], 'L0_gnn_b2': _L0_gnn_in['b2'], 'L0_gnn_W2_r': _L0_gnn_in['W2_r'], 'L0_mix_Wq': _L0_mix_in['Wq'], 'L0_mix_Wk': _L0_mix_in['Wk'], 'L0_mix_Wv': _L0_mix_in['Wv'], 'L0_mix_Wm': _L0_mix_in['Wm'], 'L0_mix_W1': _L0_mix_in['W1'], 'L0_mix_W2': _L0_mix_in['W2'], 'L0_mix_g1': _L0_mix_in['g1'], 'L0_mix_b1': _L0_mix_in['b1'], 'L0_mix_g2': _L0_mix_in['g2'], 'L0_mix_b2': _L0_mix_in['b2'], 'L0_ffn_gamma': _L0_ffn_in['gamma'], 'L0_ffn_beta': _L0_ffn_in['beta'], 'L0_ffn_Wr': _L0_ffn_in['Wr'], 'L0_ffn_br': _L0_ffn_in['br'], 'L0_ffn_W1': _L0_ffn_in['W1'], 'L0_ffn_b1': _L0_ffn_in['b1'], 'L0_ffn_W2': _L0_ffn_in['W2'], 'L0_ffn_b2': _L0_ffn_in['b2']}

def reference(x, src, dst, L0_gnn_W1_l, L0_gnn_b1, L0_gnn_W1_r, L0_gnn_W2_l, L0_gnn_b2, L0_gnn_W2_r, L0_mix_Wq, L0_mix_Wk, L0_mix_Wv, L0_mix_Wm, L0_mix_W1, L0_mix_W2, L0_mix_g1, L0_mix_b1, L0_mix_g2, L0_mix_b2, L0_ffn_gamma, L0_ffn_beta, L0_ffn_Wr, L0_ffn_br, L0_ffn_W1, L0_ffn_b1, L0_ffn_W2, L0_ffn_b2):
    import jax
    import jax.numpy as jnp

    def _L0_gnn_ref(x, edge_index, W1_l, b1, W1_r, W2_l, b2, W2_r):
        import jax, jax.numpy as jnp
        import numpy as np
        N_NODES = 6250
        N_EDGES = 100000
        D = 256

        def _mean_aggregate(x, src, tgt, num_nodes):
            summed = jax.ops.segment_sum(x[src], tgt, num_segments=num_nodes)
            count = jax.ops.segment_sum(jnp.ones((src.shape[0],), x.dtype), tgt, num_segments=num_nodes)
            return summed / jnp.maximum(count, 1.0)[:, None]

        def _sage_conv(x, src, tgt, W_l, b, W_r):
            agg = _mean_aggregate(x, src, tgt, x.shape[0])
            return agg @ W_l + b + x @ W_r
        src, tgt = (edge_index[0], edge_index[1])
        h = jax.nn.relu(_sage_conv(x, src, tgt, W1_l, b1, W1_r))
        return _sage_conv(h, src, tgt, W2_l, b2, W2_r)

    def _L0_mix_ref(x, Wq, Wk, Wv, Wm, W1, W2, g1, b1, g2, b2):
        import jax, jax.numpy as jnp
        import numpy as np
        NHEAD = 8
        ATT_EPS = 1e-06
        LN_EPS = 1e-05

        def _layernorm(x, g, b):
            mu = jnp.mean(x, axis=-1, keepdims=True)
            var = jnp.mean(jnp.square(x - mu), axis=-1, keepdims=True)
            return (x - mu) * jax.lax.rsqrt(var + LN_EPS) * g + b
        N, L, C = x.shape
        H = NHEAD
        D = C // H
        q = (x @ Wq).reshape(N, L, H, D)
        k = (x @ Wk).reshape(N, L, H, D)
        v = (x @ Wv).reshape(N, L, H, D)
        Q = jax.nn.elu(q) + 1.0
        K = jax.nn.elu(k) + 1.0
        v = v / L
        KV = jnp.einsum('nshd,nshv->nhdv', K, v)
        Z = 1.0 / (jnp.einsum('nlhd,nhd->nlh', Q, K.sum(axis=1)) + ATT_EPS)
        msg = jnp.einsum('nlhd,nhdv,nlh->nlhv', Q, KV, Z) * L
        msg = msg.reshape(N, L, C) @ Wm
        msg = _layernorm(msg, g1, b1)
        h = jnp.concatenate([x, msg], axis=-1) @ W1
        h = jax.nn.relu(h) @ W2
        msg = _layernorm(h, g2, b2)
        return x + msg

    def _L0_ffn_ref(x, gamma, beta, Wr, br, W1, b1, W2, b2):
        import jax, jax.numpy as jnp
        import numpy as np
        E = 8
        K = 2
        D = 256
        H = 512
        DOUT = 256
        EPS = 1e-05
        mu = jnp.mean(x, axis=-1, keepdims=True)
        var = jnp.mean(jnp.square(x - mu), axis=-1, keepdims=True)
        xn = (x - mu) * jax.lax.rsqrt(var + EPS) * gamma + beta
        logits = jnp.einsum('bsd,de->bse', xn, Wr) + br
        top_vals, top_idx = jax.lax.top_k(logits, K)
        w = jax.nn.softmax(top_vals, axis=-1)
        w_full = jnp.einsum('bsk,bske->bse', w, jax.nn.one_hot(top_idx, E, dtype=w.dtype))
        y = jnp.zeros(x.shape[:-1] + (DOUT,), x.dtype)
        for e in range(E):
            h = jax.nn.gelu(jnp.einsum('bsd,dh->bsh', xn, W1[e]) + b1[e], approximate=False)
            y_e = jnp.einsum('bsh,hd->bsd', h, W2[e]) + b2[e]
            y = y + y_e * w_full[..., e, None]
        return y
    edge_index = jnp.stack([src, dst])
    xn = _layernorm(x, axis=-1)
    x = x + _L0_gnn_ref(xn, edge_index, L0_gnn_W1_l, L0_gnn_b1, L0_gnn_W1_r, L0_gnn_W2_l, L0_gnn_b2, L0_gnn_W2_r) + _L0_mix_ref(xn[None], L0_mix_Wq, L0_mix_Wk, L0_mix_Wv, L0_mix_Wm, L0_mix_W1, L0_mix_W2, L0_mix_g1, L0_mix_b1, L0_mix_g2, L0_mix_b2)[0]
    x = x + _L0_ffn_ref(_layernorm(x, axis=-1)[None], L0_ffn_gamma, L0_ffn_beta, L0_ffn_Wr, L0_ffn_br, L0_ffn_W1, L0_ffn_b1, L0_ffn_W2, L0_ffn_b2)[0]
    return x

_drawn_inputs = setup_inputs


def setup_inputs(seed=0):
    import zlib

    import numpy as np

    out = dict(_drawn_inputs(seed))
    spreads = {'L0_gnn_b1': (0.0, 0.1),
     'L0_gnn_b2': (0.0, 0.1),
     'L0_mix_g1': (1.0, 0.2),
     'L0_mix_b1': (0.0, 0.282),
     'L0_mix_g2': (1.0, 0.2),
     'L0_mix_b2': (0.0, 0.1),
     'L0_ffn_br': (0.0, 0.353)}
    factors = {'L0_ffn_gamma': 8.0,
     'L0_ffn_beta': 8.0,
     'L0_ffn_Wr': 3.822,
     'L0_ffn_b1': 24.784,
     'L0_ffn_b2': 8.0}
    for name, (base, spread) in spreads.items():
        noise = np.random.default_rng([zlib.crc32(name.encode()), seed]).standard_normal(out[name].shape)
        drawn = base * np.exp(spread * noise) if base else spread * noise
        out[name] = jnp.asarray(drawn.astype(out[name].dtype))
    for name, factor in factors.items():
        out[name] = (out[name] * factor).astype(out[name].dtype)
    return out
```

```python
from contextlib import ExitStack

import concourse.bass as bass
from concourse import mybir

F32 = mybir.dt.float32
F16 = mybir.dt.float16
F8 = mybir.dt.float8e4
I32 = mybir.dt.int32
U32 = mybir.dt.uint32
ALU = mybir.AluOpType
ACT = mybir.ActivationFunctionType

P = 128
N_NODES, N_EDGES, D = 6250, 200000, 256
KD = D // P
TILES = -(-N_NODES // P)
NPAD = TILES * P
SUP = 7
SUPERS = TILES // SUP
R = SUP * P
NB = 2
NW = R // NB
LN_EPS = 1e-5
ATT_EPS = 1e-6
HEADS, HD = 8, 32
EXPERTS, HID = 8, 512
HB = HID // P

GN = 8
GROUPS = P // GN
CHUNKS = 3
GE = CHUNKS * P
EROW = 32
WROWS = GE // EROW
GC = GN * TILES
ROW = 400
ROWS = N_EDGES // ROW
STILES = -(-(TILES * GROUPS + 1) // P)
EP = 125
ELEN = N_EDGES // EP
LO_SCALE = 2048.0
FAR = -1.0e6

ONEHOTS = 4
BANKS = 4
SPLIT = (0, TILES // 2, TILES)


def program(nc, t_in, out):
    with ExitStack() as ctx:
        def sem(name):
            return ctx.enter_context(nc.semaphore(name))

        def dram(name, shape, dt):
            return nc.dram_tensor(name, shape, dt).ap()

        d = dict(
            edges=dram("edges", [(N_EDGES + GE) // EROW, 2 * EROW], F32),
            adj=dram("adj", [TILES, P, TILES * P // 4], I32),
            xnt=dram("xnt", [TILES, P, KD, P], F32),
            acc=dram("acc", [NPAD, D], F32),
        )

        def sb(stack, name, shape, dt):
            return stack.enter_context(nc.sbuf_tensor(name, shape, dt))

        keep = dict(
            ident=sb(ctx, "ident", [P, P], F32),
            eps=sb(ctx, "eps", [P, 1], F32),
            kvacc=sb(ctx, "kvacc", [P, KD, P + 1], F32),
            rdeg=sb(ctx, "rdeg", [P, TILES], F32),
            unscale=sb(ctx, "unscale", [P, 2], F32),
            turn=sem("turn"),
        )
        with ExitStack() as graph:
            keep["window"] = sb(graph, "window", [P, STILES, WROWS], I32)
            with ExitStack() as mem:
                edge_phase(nc, sem, mem, d, t_in, keep)
            keep["gathered"] = sb(graph, "gathered", [P, STILES, GE, 2], F32)
            keep["yh"] = sb(graph, "yh", [P, TILES, D + 2], F16)
            keep["yl"] = sb(graph, "yl", [P, TILES, D], F16)
            keep["w2lr"] = sb(graph, "w2lr", [P, KD, 2 * D], F32)
            keep["w1r"] = sb(graph, "w1r", [P, KD, D], F32)
            keep["b1"] = sb(graph, "b1", [P, D], F32)
            keep["b2"] = sb(graph, "b2", [P, D], F32)
            with ExitStack() as mem:
                norm_phase(nc, sem, mem, d, t_in, keep)
            with ExitStack() as mem:
                count_phase(nc, sem, mem, d, keep)
            with ExitStack() as mem:
                keep["y2h"] = sb(mem, "y2h", [P, TILES, D], F16)
                keep["y2l"] = sb(mem, "y2l", [P, TILES, D], F16)
                layer1_phase(nc, sem, mem, d, keep)
                layer2_phase(nc, sem, mem, d, keep)
        with ExitStack() as mem:
            mix_phase(nc, sem, mem, d, t_in, keep, out)


def edge_phase(nc, sem, mem, d, t_in, keep):
    def sb(name, shape, dt):
        return mem.enter_context(nc.sbuf_tensor(name, shape, dt))

    src, dst = t_in["src"], t_in["dst"]
    src_i = sb("src_i", [EP, ELEN], I32)
    dst_i = sb("dst_i", [EP, ELEN], I32)
    lo_i = sb("lo_i", [EP, ELEN], I32)
    pair = sb("pair", [EP, ELEN, 2], F32)
    pad = sb("pad", [P, CHUNKS, 2], F32)
    first_i = sb("first_i", [1, ROWS], I32)
    first_f = sb("first_f", [1, ROWS], F32)
    ones_row = sb("ones_row", [1, P], F32)
    firsts = sb("firsts", [P, ROWS], F32)
    bound = sb("bound", [P, STILES], F32)
    below = sb("below", [P, STILES], F32)
    row_i = sb("row_i", [P, STILES], I32)
    rows_i = sb("rows_i", [P, STILES, ROW], I32)
    rows_f = sb("rows_f", [P, STILES, ROW], F32)
    scratch = sb("scratch", [P, STILES, ROWS], F32)
    within = sb("within", [P, STILES], F32)
    start_f = sb("start_f", [P, STILES], F32)
    start_i = sb("start_i", [P, STILES], I32)
    row0 = sb("row0", [P, STILES], F32)
    steps = sb("steps", [P, STILES, WROWS], F32)
    spread = mem.enter_context(nc.psum_tensor("spread", [P, 512], F32))

    e_dst, e_src, e_first = sem("e_dst"), sem("e_src"), sem("e_first")
    e_const = sem("e_const")
    e_split = sem("e_split")
    e_firstf, e_spread = sem("e_firstf"), sem("e_spread")
    e_search = sem("e_search")
    e_rowi, e_rows = sem("e_rowi"), sem("e_rows")
    e_stored = sem("e_stored")
    dst_rows = dst.rearrange("(r n) -> r n", n=ROW)

    with nc.Block() as block:
        @block.sync
        def _(sp):
            with nc.allow_non_contiguous_dma(reason="one element of each row"):
                sp.dma_start(first_i[:], dst.rearrange("(r n) -> n r", n=ROW)[0:1, :]).then_inc(e_first, 16)
            sp.dma_start(dst_i[:], dst.rearrange("(p n) -> p n", p=EP)).then_inc(e_dst, 16)
            sp.dma_start(src_i[:], src.rearrange("(p n) -> p n", p=EP)).then_inc(e_src, 16)
            sp.wait_ge(e_const, 1)
            flat = d["edges"].rearrange("r (n c) -> (r n) c", c=2)
            sp.dma_start(flat[N_EDGES:N_EDGES + GE, :].rearrange("(p n) c -> p n c", p=P), pad[:]).then_inc(e_stored, 16)
            sp.wait_ge(e_split, 5)
            sp.dma_start(flat[0:N_EDGES, :].rearrange("(p n) c -> p n c", p=EP), pair[:])\
              .then_inc(e_stored, 16)
            sp.wait_ge(e_stored, 32)

        @block.gpsimd
        def _(pool):
            nc.gpsimd.memset(pad[:, :, 0:1], 0.0)
            nc.gpsimd.memset(pad[:, :, 1:2], FAR).then_inc(e_const, 1)
            nc.gpsimd.memset(ones_row[:], 1.0).then_inc(e_const, 1)
            nc.gpsimd.iota(bound[:], [[GN * P, STILES]], base=0, channel_multiplier=GN,
                           allow_small_or_imprecise_dtypes=True).then_inc(e_const, 1)
            nc.gpsimd.memset(keep["eps"][:], LN_EPS).then_inc(e_const, 1)
            nc.gpsimd.memset(keep["kvacc"][:], 0.0).then_inc(e_const, 1)
            nc.gpsimd.memset(keep["ident"][:], 0.0).then_inc(e_const, 1)
            nc.gpsimd.iota(steps[:], [[0, STILES], [1, WROWS]], base=0, channel_multiplier=0,
                           allow_small_or_imprecise_dtypes=True).then_inc(e_const, 1)
            pool.wait_ge(e_const, 6)
            nc.gpsimd.affine_select(out=keep["ident"][:], in_=keep["ident"][:], compare_op=ALU.not_equal,
                                    fill=1.0, base=0, pattern=[[-1, P]], channel_multiplier=1).then_inc(e_const, 1)
            pool.wait_ge(e_rowi, 1)
            for r in range(STILES):
                pool.indirect_dma_start(rows_i[:, r, :], None, dst_rows,
                                        bass.IndirectOffsetOnAxis(ap=row_i[:, r:r + 1], axis=0)).then_inc(e_rows, 16)
            pool.wait_ge(e_const, 8)
            pool.wait_ge(e_rows, 16 * STILES)

        @block.tensor
        def _(pe):
            pe.wait_ge(e_const, 2)
            pe.wait_ge(e_firstf, 1)
            nc.tensor.matmul(spread[:, 0:ROWS], ones_row[:], first_f[:], start=True, stop=True).then_inc(e_spread, 1)

        @block.vector
        def _(dve):
            dve.wait_ge(e_first, 16)
            nc.vector.tensor_copy(first_f[:], first_i[:]).then_inc(e_firstf, 1)
            dve.wait_ge(e_const, 3)
            dve.wait_ge(e_spread, 1)
            nc.vector.tensor_copy(firsts[:], spread[:, 0:ROWS]).then_inc(e_search, 1)
            dve.wait_ge(e_search, 1)
            for r in range(STILES):
                last = nc.vector.tensor_scalar(scratch[:, r, :], firsts[:], bound[:, r:r + 1], 0.0,
                                               ALU.is_lt, ALU.add, accum_out=below[:, r:r + 1])
            last.then_inc(e_search, 1)
            dve.wait_ge(e_search, 2)
            nc.vector.tensor_scalar(below[:], below[:], -1.0, 0.0, ALU.add, ALU.max).then_inc(e_search, 1)
            dve.wait_ge(e_search, 3)
            nc.vector.tensor_copy(row_i[:], below[:]).then_inc(e_rowi, 1)
            dve.wait_ge(e_src, 16)
            dve.wait_ge(e_dst, 16)
            nc.vector.tensor_scalar(lo_i[:], src_i[:], P - 1, None, ALU.bitwise_and).then_inc(e_split, 1)
            dve.wait_ge(e_split, 1)
            nc.vector.tensor_scalar(src_i[:], src_i[:], 7, None, ALU.logical_shift_right).then_inc(e_split, 1)
            nc.vector.tensor_scalar(dst_i[:], dst_i[:], TILES, None, ALU.mult).then_inc(e_split, 1)
            nc.vector.tensor_copy(pair[:, :, 0], lo_i[:]).then_inc(e_split, 1)
            dve.wait_ge(e_split, 4)
            nc.vector.tensor_tensor(pair[:, :, 1], src_i[:], dst_i[:], ALU.add).then_inc(e_split, 1)
            dve.wait_ge(e_rows, 16 * STILES)
            nc.vector.tensor_copy(rows_f[:], rows_i[:]).then_inc(e_search, 1)
            dve.wait_ge(e_search, 4)
            for r in range(STILES):
                last = nc.vector.tensor_scalar(scratch[:, r, 0:ROW], rows_f[:, r, :], bound[:, r:r + 1], 0.0,
                                               ALU.is_lt, ALU.add, accum_out=within[:, r:r + 1])
            last.then_inc(e_search, 1)
            dve.wait_ge(e_search, 5)
            nc.vector.scalar_tensor_tensor(start_f[:], below[:], float(ROW), within[:], ALU.mult, ALU.add)\
              .then_inc(e_search, 1)
            dve.wait_ge(e_search, 6)
            nc.vector.tensor_copy(start_i[:], start_f[:]).then_inc(e_search, 1)
            dve.wait_ge(e_search, 7)
            nc.vector.tensor_scalar(start_i[:], start_i[:], 5, None, ALU.logical_shift_right).then_inc(e_search, 1)
            dve.wait_ge(e_search, 8)
            nc.vector.tensor_copy(row0[:], start_i[:]).then_inc(e_search, 1)
            dve.wait_ge(e_search, 9)
            dve.wait_ge(e_const, 7)
            nc.vector.tensor_tensor(keep["window"][:], steps[:], row0[:].unsqueeze(2).to_broadcast([P, STILES, WROWS]),
                                    ALU.add).then_inc(e_search, 1)
            dve.wait_ge(e_search, 10)


def norm_phase(nc, sem, mem, d, t_in, keep):
    def sb(name, shape, dt):
        return mem.enter_context(nc.sbuf_tensor(name, shape, dt))

    def ps(name):
        return mem.enter_context(nc.psum_tensor(name, [P, 512], F32))

    ident, eps, kvacc, yh, yl = (keep[k] for k in ("ident", "eps", "kvacc", "yh", "yl"))
    w2lr, w1r, b1, b2, unscale = (keep[k] for k in ("w2lr", "w1r", "b1", "b2", "unscale"))
    xb = sb("xb", [P, SUP, D], F32)
    xn = sb("xn", [P, SUP, D], F32)
    xr = sb("xr", [P, SUP, D], F32)
    xnt = sb("xnt_sb", [P, KD, R], F32)
    wyk = sb("wyk", [P, KD, 2 * D], F32)
    wv = sb("wv", [P, KD, D], F32)
    stats = sb("stats", [P, SUP, 6], F32)
    meanvar = sb("meanvar", [P, SUP, 2], F32)
    std = sb("std", [P, SUP], F32)
    rstd = sb("rstd", [P, SUP], F32)
    kmin = sb("kmin", [P, 2, D], F32)
    kexp = sb("kexp", [P, 2, D], F32)
    kbuf = sb("kbuf", [P, SUP, D], F32)
    vbuf = sb("vbuf", [P, SUP, KD, P + 1], F32)
    valid = sb("valid", [P, TILES], F32)
    ones = sb("ones", [P, P], F32)
    squares = sb("squares", [P, 4, KD * D], F32)
    sumsq = sb("sumsq", [P, 4], F32)
    norms = sb("norms", [P, 4], F32)
    bnd = sb("bnd", [P, 2], F32)
    tmp = sb("tmp", [P, 2], F32)
    scale = sb("scale", [P, 2], F32)
    rscale = sb("rscale", [P, 2], F32)
    pt = [ps(f"pt{i}") for i in range(2)]
    pyk = [ps(f"pyk{i}") for i in range(2)]
    pv = [ps(f"pv{i}") for i in range(2)]
    pkv = ps("pkv")

    n_w, n_b = sem("n_w"), sem("n_b")
    n_gather = sem("n_gather")
    n_const = sem("n_const")
    n_sq, n_norm, n_sc = sem("n_sq"), sem("n_norm"), sem("n_sc")
    n_sums = sem("n_sums")
    n_x, n_xfree = sem("n_x"), sem("n_xfree")
    n_stats, n_var, n_std, n_rstd, n_xn = (sem(f"n_{k}") for k in ("stats", "var", "std", "rstd", "xn"))
    n_xr, n_xrfree, n_xrst = sem("n_xr"), sem("n_xrfree"), sem("n_xrst")
    n_tr, n_xnt, n_xntst, n_xntfree = sem("n_tr"), sem("n_xnt"), sem("n_xntst"), sem("n_xntfree")
    n_yk, n_ykfree = sem("n_yk"), sem("n_ykfree")
    n_yh, n_v, n_kmin, n_kexp, n_k = (sem(f"n_{k}") for k in ("yh", "v", "kmin", "kexp", "k"))
    n_yl, n_ones = sem("n_yl"), sem("n_ones")
    n_kv, n_kvacc = sem("n_kv"), sem("n_kvacc")

    kb = lambda w: w.rearrange("(k p) n -> p k n", p=P)
    x_s = t_in["x"].rearrange("(s j p) f -> s p j f", p=P, j=SUP)
    acc_s = d["acc"].rearrange("(s j p) f -> s p j f", p=P, j=SUP)
    xnt_s = d["xnt"].rearrange("(s j) p k c -> s p k j c", j=SUP)

    with nc.Block() as block:
        @block.sync
        def _(sp):
            sp.dma_start(wyk[:, :, 0:D], kb(t_in["gnn_W1_l"])).then_inc(n_w, 16)
            sp.dma_start(wyk[:, :, D:2 * D], kb(t_in["mix_Wk"])).then_inc(n_w, 16)
            sp.dma_start(wv[:], kb(t_in["mix_Wv"])).then_inc(n_w, 16)
            sp.dma_start(w1r[:], kb(t_in["gnn_W1_r"])).then_inc(n_w, 16)
            sp.dma_start(w2lr[:, :, 0:D], kb(t_in["gnn_W2_l"])).then_inc(n_w, 16)
            sp.dma_start(w2lr[:, :, D:2 * D], kb(t_in["gnn_W2_r"])).then_inc(n_w, 16)
            sp.dma_start(b1[:], t_in["gnn_b1"].unsqueeze(0).to_broadcast([P, D])).then_inc(n_b, 16)
            sp.dma_start(b2[:], t_in["gnn_b2"].unsqueeze(0).to_broadcast([P, D])).then_inc(n_b, 16)
            sp.sem_inc(n_xrfree, 1)
            sp.sem_inc(n_xntfree, 1)
            with sp.Fori(0, SUPERS) as s:
                sp.wait_ge(n_xfree, s + 1)
                sp.dma_start(xb[:], x_s[bass.ds(s, 1)].rearrange("o p j f -> (o p) j f")).then_inc(n_x, 16)
                sp.wait_ge(n_xr, s + 1)
                sp.dma_start(acc_s[bass.ds(s, 1)].rearrange("o p j f -> (o p) j f"), xr[:]).then_inc(n_xrst, 16)
                sp.wait_ge(n_xnt, 4 * s + 4)
                for k in range(KD):
                    sp.dma_start(xnt_s[bass.ds(s, 1), :, k].rearrange("o p j c -> (o p) j c"),
                                 xnt[:, k, :].rearrange("p (j c) -> p j c", j=SUP)).then_inc(n_xntst, 16)
                sp.wait_ge(n_xrst, 16 * s + 16)
                sp.sem_inc(n_xrfree, 1)
                sp.wait_ge(n_xntst, 32 * s + 32)
                sp.sem_inc(n_xntfree, 1)

        @block.gpsimd
        def _(pool):
            nc.gpsimd.memset(ones[:], 1.0).then_inc(n_const, 1)
            nc.gpsimd.memset(valid[:], 1.0).then_inc(n_const, 1)
            nc.gpsimd.memset(yh[:, :, D:D + 2], 1.0).then_inc(n_const, 1)
            pool.wait_ge(n_const, 3)
            nc.gpsimd.affine_select(out=valid[:], in_=valid[:], compare_op=ALU.is_ge, fill=0.0,
                                    base=N_NODES - 1, pattern=[[-P, TILES]], channel_multiplier=-1).then_inc(n_const, 1)
            pool.wait_ge(n_const, 4)
            pool.sem_inc(n_xfree, 1)
            for r in range(STILES):
                for k in range(WROWS):
                    pool.indirect_dma_start(keep["gathered"][:, r, k * EROW:(k + 1) * EROW, :].rearrange("p n c -> p (n c)"),
                                            None, d["edges"],
                                            bass.IndirectOffsetOnAxis(ap=keep["window"][:, r, k:k + 1], axis=0))\
                        .then_inc(n_gather, 16)
            with pool.Fori(0, SUPERS) as s:
                pool.wait_ge(n_xn, s + 1)
                pool.wait_ge(n_xrfree, s + 1)
                nc.gpsimd.tensor_tensor(xr[:], xb[:], xn[:], ALU.add).then_inc(n_xr, 1)
                pool.wait_ge(n_xr, s + 1)
                pool.sem_inc(n_xfree, 1)
            pool.wait_ge(n_gather, 16 * STILES * WROWS)

        @block.scalar
        def _(act):
            act.wait_ge(n_w, 96)
            act.wait_ge(n_b, 32)
            for i, w in enumerate((wyk[:, :, 0:D], w1r[:], w2lr[:, :, 0:D])):
                nc.scalar.activation(squares[:, i, :].rearrange("p (k n) -> p k n", k=KD), w, ACT.Square,
                                     accum_out=sumsq[:, i:i + 1]).then_inc(n_sq, 1)
            nc.scalar.activation(squares[:, 3, 0:D], b1[:], ACT.Square, accum_out=sumsq[:, 3:4]).then_inc(n_sq, 1)
            act.wait_ge(n_sums, 1)
            act.wait_ge(n_sq, 4)
            nc.scalar.activation(norms[:, 0:3], pt[0][:, 0:3], ACT.Sqrt).then_inc(n_norm, 1)
            nc.scalar.activation(norms[:, 3:4], sumsq[:, 3:4], ACT.Sqrt).then_inc(n_norm, 1)
            with act.Fori(0, SUPERS) as s:
                act.wait_ge(n_var, s + 1)
                nc.scalar.activation(std[:], meanvar[:, :, 1], ACT.Sqrt, bias=eps[:]).then_inc(n_std, 1)
                act.wait_ge(n_xntfree, s + 1)
                for b in range(4):
                    k, half = b // 2, b % 2
                    act.wait_ge(n_tr, 4 * s + b + 1)
                    w = (4, 3)[half] * P
                    nc.scalar.activation(xnt[:, k, half * 4 * P:half * 4 * P + w], pt[half][:, 0:w], ACT.Copy)\
                      .then_inc(n_xnt, 1)
                for j in range(SUP):
                    act.wait_ge(n_yk, s * SUP + (j + 1))
                    nc.scalar.activation(yh[:, bass.ds(s * SUP + j, 1), 0:D].rearrange("p o f -> p (o f)"),
                                         pyk[j % 2][:, 0:D], ACT.Copy, scale=1.0 / LO_SCALE).then_inc(n_yh, 1)
                    nc.scalar.activation(vbuf[:, j, :, 0:P],
                                         pv[j % 2][:, 0:D].rearrange("p (k f) -> p k f", k=KD),
                                         ACT.Copy).then_inc(n_v, 1)
                    act.wait_ge(n_kmin, s * SUP + (j + 1))
                    nc.scalar.activation(kexp[:, j % 2, :], kmin[:, j % 2, :], ACT.Exp).then_inc(n_kexp, 1)

        @block.vector
        def _(dve):
            dve.wait_ge(n_norm, 2)
            top = float(D) ** 0.5
            nc.vector.tensor_tensor(tmp[:, 0:1], norms[:, 0:1], norms[:, 1:2], ALU.add).then_inc(n_sc, 1)
            nc.vector.tensor_scalar(bnd[:, 0:1], norms[:, 0:1], top, None, ALU.mult).then_inc(n_sc, 1)
            dve.wait_ge(n_sc, 2)
            nc.vector.scalar_tensor_tensor(tmp[:, 1:2], tmp[:, 0:1], top, norms[:, 3:4], ALU.mult, ALU.add)\
              .then_inc(n_sc, 1)
            dve.wait_ge(n_sc, 3)
            nc.vector.tensor_tensor(bnd[:, 1:2], tmp[:, 1:2], norms[:, 2:3], ALU.mult).then_inc(n_sc, 1)
            dve.wait_ge(n_sc, 4)
            nc.vector.tensor_scalar(bnd[:], bnd[:], 1e-20, None, ALU.max).then_inc(n_sc, 1)
            dve.wait_ge(n_sc, 5)
            nc.vector.reciprocal(scale[:], bnd[:]).then_inc(n_sc, 1)
            dve.wait_ge(n_sc, 6)
            nc.vector.tensor_scalar(scale[:], scale[:], 2.0 ** 15 * LO_SCALE, None, ALU.mult).then_inc(n_sc, 1)
            dve.wait_ge(n_sc, 7)
            nc.vector.tensor_scalar(scale[:].bitcast(I32), scale[:].bitcast(I32), 0x7F800000, None,
                                    ALU.bitwise_and).then_inc(n_sc, 1)
            dve.wait_ge(n_sc, 8)
            nc.vector.reciprocal(rscale[:], scale[:]).then_inc(n_sc, 1)
            nc.vector.tensor_scalar(wyk[:, :, 0:D], wyk[:, :, 0:D], scale[:, 0:1], None, ALU.mult).then_inc(n_sc, 1)
            nc.vector.tensor_scalar(w2lr[:, :, 0:D], w2lr[:, :, 0:D], scale[:, 1:2], None, ALU.mult).then_inc(n_sc, 1)
            dve.wait_ge(n_sc, 11)
            nc.vector.tensor_scalar(unscale[:], rscale[:], LO_SCALE, None, ALU.mult).then_inc(n_sc, 1)
            dve.wait_ge(n_const, 4)
            dve.sem_inc(n_ykfree, 2)
            with dve.Fori(0, SUPERS) as s:
                dve.wait_ge(n_x, 16 * s + 16)
                for j in range(SUP):
                    last = nc.vector.bn_stats(stats[:, j, :], xb[:, j, :])
                last.then_inc(n_stats, 1)
                dve.wait_ge(n_stats, s + 1)
                dve.sem_inc(keep["turn"], 1)
                for j in range(SUP):
                    last = nc.vector.bn_aggr(meanvar[:, j, :], stats[:, j, :])
                last.then_inc(n_var, 1)
                dve.wait_ge(n_std, s + 1)
                nc.vector.reciprocal(rstd[:], std[:]).then_inc(n_rstd, 1)
                dve.wait_ge(n_rstd, s + 1)
                for j in range(SUP):
                    last = nc.vector.tensor_scalar(xn[:, j, :], xb[:, j, :], meanvar[:, j, 0:1], rstd[:, j:j + 1],
                                                   ALU.subtract, ALU.mult)
                last.then_inc(n_xn, 1)
                nc.vector.tensor_copy(vbuf[:, :, :, P:P + 1].rearrange("p j k o -> p j (k o)"),
                                      valid[:, bass.ds(s * SUP, SUP)].unsqueeze(2).to_broadcast([P, SUP, KD]))\
                  .then_inc(n_ones, 1)
                for j in range(SUP):
                    dve.wait_ge(n_yk, s * SUP + (j + 1))
                    dve.wait_ge(n_yh, s * SUP + (j + 1))
                    nc.vector.tensor_scalar(kmin[:, j % 2, :], pyk[j % 2][:, D:2 * D], 0.0, None, ALU.min)\
                      .then_inc(n_kmin, 1)
                    nc.vector.scalar_tensor_tensor(yl[:, bass.ds(s * SUP + j, 1), :].rearrange("p o f -> p (o f)"),
                                                   yh[:, bass.ds(s * SUP + j, 1), 0:D].rearrange("p o f -> p (o f)"),
                                                   -LO_SCALE, pyk[j % 2][:, 0:D], ALU.mult, ALU.add).then_inc(n_yl, 1)
                    dve.wait_ge(n_kexp, s * SUP + (j + 1))
                    nc.vector.scalar_tensor_tensor(kbuf[:, j, :], pyk[j % 2][:, D:2 * D], 0.0, kexp[:, j % 2, :],
                                                   ALU.max, ALU.add).then_inc(n_ykfree, 1)
                dve.wait_ge(n_kv, s + 1)
                nc.vector.tensor_tensor(kvacc[:], pkv[:, 0:KD * (P + 1)].rearrange("p (k n) -> p k n", k=KD),
                                        kvacc[:], ALU.add).then_inc(n_kvacc, 1)
                dve.wait_ge(n_kvacc, s + 1)

        @block.tensor
        def _(pe):
            pe.wait_ge(n_const, 1)
            pe.wait_ge(n_sq, 4)
            nc.tensor.matmul(pt[0][:, 0:3], ones[:], sumsq[:, 0:3], start=True, stop=True).then_inc(n_sums, 1)
            pe.wait_ge(n_sc, 11)
            with pe.Fori(0, SUPERS) as s:
                pe.wait_ge(n_xn, s + 1)
                for b in range(4):
                    k, half = b // 2, b % 2
                    if b >= 2:
                        pe.wait_ge(n_xnt, s * 4 + (b - 1))
                    for j in range(4 * half, min(4 * half + 4, SUP)):
                        last = nc.tensor.transpose(pt[half][:, (j % 4) * P:(j % 4 + 1) * P],
                                                   xn[:, j, k * P:(k + 1) * P], ident[:])
                    last.then_inc(n_tr, 1)
                pe.wait_ge(n_xnt, 4 * s + 4)
                for j in range(SUP):
                    pe.wait_ge(n_ykfree, s * SUP + (j + 1))
                    for k in range(KD):
                        nc.tensor.matmul(pyk[j % 2][:], xnt[:, k, j * P:(j + 1) * P], wyk[:, k, :],
                                         start=(k == 0), stop=(k == KD - 1))
                    for k in range(KD):
                        last = nc.tensor.matmul(pv[j % 2][:, 0:D], xnt[:, k, j * P:(j + 1) * P],
                                                wv[:, k, :], start=(k == 0), stop=(k == KD - 1))
                    last.then_inc(n_yk, 1)
                pe.wait_ge(n_ykfree, s * SUP + (SUP + 2))
                pe.wait_ge(n_v, s * SUP + SUP)
                pe.wait_ge(n_ones, s + 1)
                for k in range(KD):
                    for j in range(SUP):
                        last = nc.tensor.matmul(pkv[:, k * (P + 1):(k + 1) * (P + 1)], kbuf[:, j, k * P:(k + 1) * P],
                                                vbuf[:, j, k, :], start=(j == 0), stop=(j == SUP - 1))
                last.then_inc(n_kv, 1)


def count_phase(nc, sem, mem, d, keep):
    def sb(name, shape, dt):
        return mem.enter_context(nc.sbuf_tensor(name, shape, dt))

    ident, gathered = keep["ident"], keep["gathered"]
    lo_all = sb("lo_all", [P, STILES * P, CHUNKS], F16)
    key_all = sb("key_all", [P, STILES * P, CHUNKS], F32)
    iota_key = sb("iota_key", [P, GC], F16)
    iota_lo = sb("iota_lo", [P, P, GROUPS * CHUNKS], F16)
    keybase = sb("keybase", [P, STILES * P, CHUNKS], F32)
    lo = sb("lo", [P, GROUPS * CHUNKS], F16)
    key = sb("key", [P, GROUPS, CHUNKS], F32)
    hot_key = sb("hot_key", [P, ONEHOTS, CHUNKS, GC], F16)
    hot_lo = [sb(f"hot_lo{i}", [P, P, GROUPS * CHUNKS], F16) for i in range(2)]
    counts = [sb(f"counts{i}", [P, TILES, P], F8) for i in range(2)]
    pc = [mem.enter_context(nc.psum_tensor(f"pc{i}", [P, 512], F32)) for i in range(BANKS)]

    c_const = sem("c_const")
    c_turned, c_taken = sem("c_turned"), sem("c_taken")
    c_keys = sem("c_keys")
    c_hot = sem("c_hot")
    c_group = sem("c_group")
    c_evac = sem("c_evac")
    c_countsfree = [sem(f"c_countsfree{i}") for i in range(2)]
    c_stored = [sem(f"c_stored{i}") for i in range(2)]

    with nc.Block() as block:
        @block.sync
        def _(sp):
            pass

        @block.gpsimd
        def _(pool):
            iota = lambda *a, **k: nc.gpsimd.iota(*a, allow_small_or_imprecise_dtypes=True, **k)
            iota(iota_key[:], [[1, GC]], base=0, channel_multiplier=0).then_inc(c_const, 1)
            iota(iota_lo[:], [[1, P], [0, GROUPS * CHUNKS]], base=0, channel_multiplier=0).then_inc(c_const, 1)
            iota(keybase[:], [[GC, STILES * P], [0, CHUNKS]], base=0, channel_multiplier=0).then_inc(c_const, 1)
            for b in range(2):
                pool.sem_inc(c_countsfree[b], 1)

            def store(t, b, turn):
                pool.wait_ge(c_evac, t * GROUPS + (BANKS + GROUPS))
                pool.dma_start(d["adj"][bass.ds(t, 1)].rearrange("o p c -> (o p) c"),
                               counts[b][:].rearrange("p a b -> p (a b)").bitcast(I32)).then_inc(c_stored[b], 16)
                pool.wait_ge(c_stored[b], turn * 16)
                pool.sem_inc(c_countsfree[b], 1)
            with pool.Fori(0, TILES // 2) as i:
                store(i * 2, 0, i + 1)
                store(i * 2 + 1, 1, i + 1)
            store(TILES - 1, 0, TILES // 2 + 1)

        @block.vector
        def _(dve):
            dve.wait_ge(c_const, 3)
            for r in range(STILES):
                dve.wait_ge(c_turned, r + 1)
                here = slice(r * P, (r + 1) * P)
                nc.vector.tensor_copy(lo_all[:, here, :], pc[2 * (r % 2)][:, 0:GE].rearrange("p (c g) -> p g c", g=P))
                nc.vector.tensor_tensor(key_all[:, here, :], pc[2 * (r % 2) + 1][:, 0:GE].rearrange("p (c g) -> p g c", g=P),
                                        keybase[:, here, :], ALU.subtract).then_inc(c_taken, 1)
            dve.wait_ge(c_taken, STILES)

            def onehots(t, b):
                nc.vector.tensor_copy(lo[:], lo_all[:, bass.ds(t * GROUPS, GROUPS), :].rearrange("p g c -> p (g c)"))\
                  .then_inc(c_keys, 1)
                nc.vector.tensor_copy(key[:], key_all[:, bass.ds(t * GROUPS, GROUPS), :]).then_inc(c_keys, 1)
                dve.wait_ge(c_keys, t * 2 + 2)
                nc.vector.tensor_tensor(hot_lo[b][:], iota_lo[:],
                                        lo[:].unsqueeze(1).to_broadcast([P, P, GROUPS * CHUNKS]), ALU.is_equal)
                for g in range(GROUPS):
                    dve.wait_ge(c_group, t * GROUPS + (g + 1))
                    for c in range(CHUNKS):
                        last = nc.vector.tensor_scalar(hot_key[:, g % ONEHOTS, c, :], iota_key[:], key[:, g, c:c + 1],
                                                       None, ALU.is_equal)
                    last.then_inc(c_hot, 1)
                dve.wait_ge(c_hot, t * GROUPS + GROUPS)
            with dve.Fori(0, TILES // 2) as i:
                onehots(i * 2, 0)
                onehots(i * 2 + 1, 1)
            onehots(TILES - 1, 0)

        @block.tensor
        def _(pe):
            for r in range(STILES):
                if r >= 2:
                    pe.wait_ge(c_taken, r - 1)
                for c in range(CHUNKS):
                    for i in range(2):
                        last = nc.tensor.transpose(pc[2 * (r % 2) + i][:, c * P:(c + 1) * P],
                                                   gathered[:, r, c * P:(c + 1) * P, i], ident[:])
                last.then_inc(c_turned, 1)
            pe.wait_ge(c_taken, STILES)
            pe.sem_inc(c_group, ONEHOTS)

            def multiply(t, b):
                for g in range(GROUPS):
                    pe.wait_ge(c_hot, t * GROUPS + (g + 1))
                    pe.wait_ge(c_evac, t * GROUPS + (g + 1))
                    for c in range(CHUNKS):
                        last = nc.tensor.matmul(pc[g % BANKS][:, 0:GC], hot_lo[b][:, :, g * CHUNKS + c],
                                                hot_key[:, g % ONEHOTS, c, :], start=(c == 0), stop=(c == CHUNKS - 1))
                    last.then_inc(c_group, 1)
            with pe.Fori(0, TILES // 2) as i:
                multiply(i * 2, 0)
                multiply(i * 2 + 1, 1)
            multiply(TILES - 1, 0)

        @block.scalar
        def _(act):
            act.sem_inc(c_evac, BANKS)

            def evacuate(t, b, turn):
                act.wait_ge(c_countsfree[b], turn)
                for g in range(GROUPS):
                    act.wait_ge(c_group, t * GROUPS + (ONEHOTS + g + 1))
                    act.sem_inc(keep["turn"], 1)
                    nc.scalar.activation(counts[b][:, :, g * GN:(g + 1) * GN].rearrange("p h n -> p n h"),
                                         pc[g % BANKS][:, 0:GC].rearrange("p (n h) -> p n h", n=GN),
                                         ACT.Copy, saturate=False).then_inc(c_evac, 1)
            with act.Fori(0, TILES // 2) as i:
                evacuate(i * 2, 0, i + 1)
                evacuate(i * 2 + 1, 1, i + 1)
            evacuate(TILES - 1, 0, TILES // 2 + 1)


def aggregate(pe, nc, keep, s, part, q, ph, pl, yh, yl, cols, t):
    pe.wait_ge(s["part"][q], t * 16 + 16)
    pe.wait_ge(s["bankfree"][q], t + 1)
    pe.sem_inc(keep["turn"], 1)
    h0, h1 = SPLIT[q], SPLIT[q + 1]
    for h in range(h0, h1):
        nc.tensor.matmul(ph[q][:, 0:cols], part[q][:, h - h0, :], yh[:, h, 0:cols], start=(h == h0), stop=(h == h1 - 1))
        last = nc.tensor.matmul(pl[q][:, 0:D], part[q][:, h - h0, :], yl[:, h, :], start=(h == h0), stop=(h == h1 - 1))
    last.then_inc(s["summed"][q], 1)


def load_parts(sp, s, d, part, t):
    for q in range(2):
        sp.wait_ge(s["summed"][q], t + 1)
        sp.dma_start(part[q][:].rearrange("p h n -> p (h n)").bitcast(I32),
                     d["adj"][bass.ds(t, 1), :, SPLIT[q] * P // 4:SPLIT[q + 1] * P // 4].rearrange("o p c -> (o p) c"))\
          .then_inc(s["part"][q], 16)


def aggregation_semaphores(sem, p):
    pair = lambda n: [sem(f"{p}_{n}{q}") for q in range(2)]
    return dict(part=pair("part"), summed=pair("summed"), bankfree=pair("bankfree"),
                comb=sem(f"{p}_comb"))


def combine(dve, nc, s, ph, pl, first, total, cols, t):
    dve.wait_ge(s["summed"][0], t + 2)
    nc.vector.tensor_copy(first[:, 0:cols], ph[0][:, 0:cols]).then_inc(s["comb"], 1)
    dve.wait_ge(s["comb"], t * 4 + 1)
    nc.vector.scalar_tensor_tensor(first[:, 0:D], pl[0][:, 0:D], 1.0 / LO_SCALE, first[:, 0:D], ALU.mult, ALU.add)\
      .then_inc(s["comb"], 1)
    dve.wait_ge(s["comb"], t * 4 + 2)
    dve.sem_inc(s["bankfree"][0], 1)
    dve.wait_ge(s["summed"][1], t + 2)
    nc.vector.tensor_tensor(total[:, 0:cols], ph[1][:, 0:cols], first[:, 0:cols], ALU.add).then_inc(s["comb"], 1)
    dve.wait_ge(s["comb"], t * 4 + 3)
    nc.vector.scalar_tensor_tensor(total[:, 0:D], pl[1][:, 0:D], 1.0 / LO_SCALE, total[:, 0:D], ALU.mult, ALU.add)\
      .then_inc(s["comb"], 1)
    dve.wait_ge(s["comb"], t * 4 + 4)
    dve.sem_inc(s["bankfree"][1], 1)


def layer1_phase(nc, sem, mem, d, keep):
    def sb(name, shape, dt):
        return mem.enter_context(nc.sbuf_tensor(name, shape, dt))

    ident, yh, yl, y2h, y2l, w1r, w2lr, b1, b2, rdeg, unscale = (keep[k] for k in (
        "ident", "yh", "yl", "y2h", "y2l", "w1r", "w2lr", "b1", "b2", "rdeg", "unscale"))
    keep["part"] = part = [sb(f"part{q}", [P, SPLIT[q + 1] - SPLIT[q], P], F8) for q in range(2)]
    keep["first"] = first = sb("first", [P, D + 1], F32)
    keep["total"] = total = sb("total", [P, D + 1], F32)
    keep["acc_in"] = acc_in = sb("acc_in", [P, D], F32)
    keep["acc_out"] = acc_out = sb("acc_out", [P, D], F32)
    xt = sb("xt", [P, KD, P], F32)
    rsum = sb("rsum", [P, 2], F32)
    h0 = sb("h0", [P, D], F32)
    h = sb("h", [P, D], F32)
    ht = sb("ht", [P, KD, P], F32)
    ps = lambda n: mem.enter_context(nc.psum_tensor(n, [P, 512], F32))
    keep["ph"] = ph = [ps("ph0"), ps("ph1")]
    keep["pl"] = pl = [ps("pl0"), ps("pl1")]
    pr, ptr, py2 = ps("pr"), ps("ptr"), ps("py2")

    s = aggregation_semaphores(sem, "g")
    g_xt, g_root, g_acc, g_accfree = sem("g_xt"), sem("g_root"), sem("g_acc"), sem("g_accfree")
    g_h, g_tr, g_ht, g_y2, g_y2h = sem("g_h"), sem("g_tr"), sem("g_ht"), sem("g_y2"), sem("g_y2h")
    g_step = sem("g_step")
    g_y2free, g_out, g_outfree, g_stored = sem("g_y2free"), sem("g_out"), sem("g_outfree"), sem("g_stored")
    g_pre, g_tail = sem("g_pre"), sem("g_tail")

    with nc.Block() as block:
        @block.sync
        def _(sp):
            def load_tile(t):
                load_parts(sp, s, d, part, t)
                sp.wait_ge(g_root, t + 1)
                sp.dma_start(xt[:], d["xnt"][bass.ds(t, 1)].rearrange("o p k c -> (o p) k c")).then_inc(g_xt, 16)

            def load_acc(t):
                sp.wait_ge(g_accfree, t + 1)
                sp.dma_start(acc_in[:], d["acc"][bass.ds(t * P, P), :]).then_inc(g_acc, 16)
            load_tile(0)
            with sp.Fori(1, TILES) as t:
                load_tile(t)
                load_acc(t - 1)
            load_acc(TILES - 1)

        @block.gpsimd
        def _(pool):
            pool.sem_inc(g_outfree, 1)
            with pool.Fori(0, TILES) as t:
                pool.wait_ge(g_out, t + 1)
                pool.dma_start(d["acc"][bass.ds(t * P, P), :], acc_out[:]).then_inc(g_stored, 16)
                pool.wait_ge(g_stored, t * 16 + 16)
                pool.sem_inc(g_outfree, 1)

        @block.tensor
        def _(pe):
            for q in range(2):
                pe.sem_inc(s["summed"][q], 1)
            pe.sem_inc(g_root, 1)

            def tail_transpose(t):
                pe.wait_ge(g_h, t + 1)
                for k in range(KD):
                    last = nc.tensor.transpose(ptr[:, k * P:(k + 1) * P], h[:, k * P:(k + 1) * P], ident[:])
                last.then_inc(g_tr, 1)

            def tail_project(t):
                pe.wait_ge(g_ht, t + 1)
                pe.wait_ge(g_y2free, t + 1)
                for k in range(KD):
                    last = nc.tensor.matmul(py2[:], ht[:, k, :], w2lr[:, k, :], start=(k == 0), stop=(k == KD - 1))
                last.then_inc(g_y2, 1)

            def root(t):
                pe.wait_ge(g_xt, t * 16 + 16)
                for k in range(KD):
                    last = nc.tensor.matmul(pr[:, 0:D], xt[:, k, :], w1r[:, k, :], start=(k == 0), stop=(k == KD - 1))
                last.then_inc(g_root, 1)

            def sums(t, q):
                aggregate(pe, nc, keep, s, part, q, ph, pl, yh, yl, D + 2, t)
            sums(0, 0)
            root(0)
            sums(0, 1)
            with pe.Fori(1, TILES) as t:
                sums(t, 0)
                tail_transpose(t - 1)
                root(t)
                sums(t, 1)
                tail_project(t - 1)
            tail_transpose(TILES - 1)
            tail_project(TILES - 1)

        @block.scalar
        def _(act):
            with act.Fori(0, TILES) as t:
                act.wait_ge(g_tr, t + 1)
                nc.scalar.activation(ht[:].rearrange("p k c -> p (k c)"), ptr[:, 0:D], ACT.Copy).then_inc(g_ht, 1)
                act.wait_ge(g_y2, t + 1)
                nc.scalar.activation(y2h[:, bass.ds(t, 1), :].rearrange("p o f -> p (o f)"), py2[:, 0:D],
                                     ACT.Copy, scale=1.0 / LO_SCALE).then_inc(g_y2h, 1)

        @block.vector
        def _(dve):
            for q in range(2):
                dve.sem_inc(s["bankfree"][q], 1)
            dve.sem_inc(g_accfree, 1)
            dve.sem_inc(g_y2free, 1)

            def head(t):
                combine(dve, nc, s, ph, pl, first, total, D + 1, t)
                nc.vector.tensor_scalar(rsum[:, 0:1], total[:, D:D + 1], 1.0, None, ALU.max).then_inc(g_step, 1)
                dve.wait_ge(g_step, t * 5 + 1)
                nc.vector.reciprocal(rsum[:, 1:2], rsum[:, 0:1]).then_inc(g_step, 1)
                dve.wait_ge(g_step, t * 5 + 2)
                nc.vector.tensor_scalar(rsum[:, 0:1], rsum[:, 1:2], unscale[:, 0:1], None, ALU.mult).then_inc(g_step, 1)
                nc.vector.tensor_scalar(rdeg[:, bass.ds(t, 1)], rsum[:, 1:2], unscale[:, 1:2], None, ALU.mult)\
                  .then_inc(g_step, 1)
                dve.wait_ge(g_step, t * 5 + 4)
                dve.wait_ge(g_root, t + 2)
                nc.vector.scalar_tensor_tensor(h0[:], total[:, 0:D], rsum[:, 0:1], b1[:], ALU.mult, ALU.add)\
                  .then_inc(g_step, 1)
                dve.wait_ge(g_step, t * 5 + 5)
                nc.vector.tensor_tensor(h0[:], pr[:, 0:D], h0[:], ALU.add).then_inc(g_pre, 1)
                dve.wait_ge(g_pre, t + 1)
                nc.vector.tensor_scalar(h[:], h0[:], 0.0, None, ALU.max).then_inc(g_h, 1)

            def tail(t):
                dve.wait_ge(g_y2h, t + 1)
                nc.vector.scalar_tensor_tensor(y2l[:, bass.ds(t, 1), :].rearrange("p o f -> p (o f)"),
                                               y2h[:, bass.ds(t, 1), :].rearrange("p o f -> p (o f)"),
                                               -LO_SCALE, py2[:, 0:D], ALU.mult, ALU.add).then_inc(g_tail, 1)
                dve.wait_ge(g_acc, t * 16 + 16)
                dve.wait_ge(g_outfree, t + 1)
                nc.vector.tensor_tensor(acc_out[:], py2[:, D:2 * D], acc_in[:], ALU.add).then_inc(g_tail, 1)
                dve.wait_ge(g_tail, t * 2 + 2)
                dve.sem_inc(g_accfree, 1)
                dve.sem_inc(g_y2free, 1)
                nc.vector.tensor_tensor(acc_out[:], acc_out[:], b2[:], ALU.add).then_inc(g_out, 1)
                dve.wait_ge(g_out, t + 1)
            head(0)
            with dve.Fori(1, TILES) as t:
                head(t)
                tail(t - 1)
            tail(TILES - 1)


def layer2_phase(nc, sem, mem, d, keep):
    y2h, y2l, rdeg = keep["y2h"], keep["y2l"], keep["rdeg"]
    part, first, total, ph, pl = (keep[k] for k in ("part", "first", "total", "ph", "pl"))
    acc_in, acc_out = keep["acc_in"], keep["acc_out"]
    s = aggregation_semaphores(sem, "h")
    h_acc, h_accfree, h_out, h_outfree, h_stored = (sem(f"h_{k}") for k in ("acc", "accfree", "out", "outfree", "stored"))

    with nc.Block() as block:
        @block.sync
        def _(sp):
            with sp.Fori(0, TILES) as t:
                load_parts(sp, s, d, part, t)
                sp.wait_ge(h_accfree, t + 1)
                sp.dma_start(acc_in[:], d["acc"][bass.ds(t * P, P), :]).then_inc(h_acc, 16)

        @block.gpsimd
        def _(pool):
            pool.sem_inc(h_outfree, 1)
            with pool.Fori(0, TILES) as t:
                pool.wait_ge(h_out, t + 1)
                pool.dma_start(d["acc"][bass.ds(t * P, P), :], acc_out[:]).then_inc(h_stored, 16)
                pool.wait_ge(h_stored, t * 16 + 16)
                pool.sem_inc(h_outfree, 1)

        @block.tensor
        def _(pe):
            for q in range(2):
                pe.sem_inc(s["summed"][q], 1)
            with pe.Fori(0, TILES) as t:
                for q in range(2):
                    aggregate(pe, nc, keep, s, part, q, ph, pl, y2h, y2l, D, t)

        @block.vector
        def _(dve):
            for q in range(2):
                dve.sem_inc(s["bankfree"][q], 1)
            dve.sem_inc(h_accfree, 1)
            with dve.Fori(0, TILES) as t:
                combine(dve, nc, s, ph, pl, first, total, D, t)
                dve.wait_ge(h_acc, t * 16 + 16)
                dve.wait_ge(h_outfree, t + 1)
                nc.vector.scalar_tensor_tensor(acc_out[:], total[:, 0:D], rdeg[:, bass.ds(t, 1)], acc_in[:],
                                               ALU.mult, ALU.add).then_inc(h_out, 1)
                dve.wait_ge(h_out, t + 1)
                dve.sem_inc(h_accfree, 1)

        @block.scalar
        def _(act):
            pass


def mix_phase(nc, sem, mem, d, t_in, keep, out):
    def sb(name, shape, dt=F32):
        return mem.enter_context(nc.sbuf_tensor(name, shape, dt))

    ident, eps, kvacc = keep["ident"], keep["eps"], keep["kvacc"]
    NV = EXPERTS * HB + 4 * KD
    wq, wm = sb("wq", [P, KD, D]), sb("wm", [P, KD, D])
    w1, w2 = sb("w1", [P, 2 * KD, 2 * D]), sb("w2", [P, 2 * KD, D])
    we1, we2 = sb("we1", [P, EXPERTS, KD, HID]), sb("we2", [P, EXPERTS, HB, D])
    wr = sb("wr", [P, KD, EXPERTS])
    be2 = sb("be2", [EXPERTS, D])
    g2, b2 = sb("mix_g2", [P, D]), sb("mix_b2", [P, D])
    br = sb("br", [P, EXPERTS])
    rows = sb("vec_rows", [NV, P])
    cols = sb("vec_cols", [P, NV])
    G1, B1, GAMMA, BETA = (EXPERTS * HB + i * KD for i in range(4))
    betab = sb("betab", [P, KD, P])
    ones = sb("ones2", [P, P])
    bdkv, bdks = sb("bdkv", [P, KD, P]), sb("bdks", [P, KD, P])
    c1 = sb("c1", [P, 2 * D // P])
    ce = sb("ce", [P, EXPERTS * HB])
    lb = sb("lb", [P, EXPERTS])
    iota8 = sb("iota8", [P, SUP, EXPERTS])
    xt, qt, msgt, m1t, x2t = (sb(n, [P, KD, R]) for n in ("m_xt", "qt", "msgt", "m1t", "x2t"))
    qmin, qexp, den = sb("qmin", [P, 2, NW]), sb("qexp", [P, 2, NW]), sb("den", [P, 2, NW])
    rden = sb("rden", [P, 2, NW])
    nrm = sb("nrm", [P, SUP, D])
    h1t = sb("h1t", [P, 2 * D // P, R])
    acc, x2, yacc = (sb(n, [P, SUP, D]) for n in ("m_acc", "x2", "yacc"))
    hot = [h1t, sb("hidt", [P, HB, R])]
    stats, mv = sb("m_stats", [P, SUP, 6]), sb("m_mv", [P, SUP, 2])
    std, rstd, rstd2, var2 = (sb(n, [P, SUP]) for n in ("m_std", "m_rstd", "m_rstd2", "m_var2"))
    lg, top = sb("lg", [P, SUP, EXPERTS]), sb("top", [P, SUP, 8])
    idx, idxf = sb("idx", [P, SUP, 8], U32), sb("idxf", [P, SUP, 8])
    gap, wgt = sb("gap", [P, SUP]), sb("wgt", [P, SUP, 2])
    pick = sb("pick", [P, 2, SUP, EXPERTS])
    wfull = sb("wfull", [P, SUP, EXPERTS])
    wt = sb("wt", [EXPERTS, R])
    bank = [mem.enter_context(nc.psum_tensor(f"bank{i}", [P, 512], F32)) for i in range(8)]

    m_w, m_row = sem("m_w"), sem("m_row")
    m_const, m_cols, m_colst, m_fold, m_scaled, m_bd, m_setup = (sem(f"m_{k}") for k in (
        "const", "cols", "colst", "fold", "scaled", "bd", "setup"))
    m_x, m_accin, m_accb, m_accfree = sem("m_x"), sem("m_accin"), sem("m_accb"), sem("m_accfree")
    m_q, m_qmin, m_qexp, m_qt = sem("m_q"), sem("m_qmin"), sem("m_qexp"), sem("m_qt")
    m_att, m_den, m_msg = sem("m_att"), sem("m_den"), sem("m_msg")
    m_m1, m_tr1, m_m1t = sem("m_m1"), sem("m_tr1"), sem("m_m1t")
    m_h1, m_h1t, m_h2, m_x2 = sem("m_h1"), sem("m_h1t"), sem("m_h2"), sem("m_x2")
    m_tr2, m_x2t = sem("m_tr2"), sem("m_x2t")
    m_lg, m_route, m_gap, m_exp, m_wfull = (sem(f"m_{k}") for k in ("lg", "route", "gap", "exp", "wfull"))
    m_wtp, m_wt, m_yb, m_y0 = sem("m_wtp"), sem("m_wt"), sem("m_yb"), sem("m_y0")
    m_hid, m_hidt, m_y, m_yacc = sem("m_hid"), sem("m_hidt"), sem("m_y"), sem("m_yacc")
    m_out, m_stored, m_yfree = sem("m_out"), sem("m_stored"), sem("m_yfree")
    ln = [{k: sem(f"m_ln{i}_{k}") for k in ("stats", "var", "std", "rstd", "done") + ("step",) * (i == 2)} for i in range(3)]

    kb = lambda w: w.rearrange("(k p) n -> p k n", p=P)
    acc_s = d["acc"].rearrange("(s j p) f -> s p j f", p=P, j=SUP)
    out_s = out.rearrange("(s j p) f -> s p j f", p=P, j=SUP)
    xnt_s = d["xnt"].rearrange("(s j) p k c -> s p k j c", j=SUP)
    tile_cols = lambda b, j: b[j // 2][:, (j % 2) * D:(j % 2 + 1) * D]
    row_vec = lambda v, n: v.rearrange("(k p) -> k p", p=P)

    with nc.Block() as block:
        @block.sync
        def _(sp):
            r = 0
            for v, n in ((t_in["ffn_b1"].rearrange("e (m p) -> (e m) p", p=P), EXPERTS * HB),
                         (row_vec(t_in["mix_g1"], KD), KD), (row_vec(t_in["mix_b1"], KD), KD),
                         (row_vec(t_in["ffn_gamma"], KD), KD), (row_vec(t_in["ffn_beta"], KD), KD)):
                sp.dma_start(rows[r:r + n, :], v).then_inc(m_row, 16)
                r += n
            sp.dma_start(w1[:], kb(t_in["mix_W1"])).then_inc(m_w, 16)
            sp.dma_start(wr[:], kb(t_in["ffn_Wr"])).then_inc(m_w, 16)
            sp.dma_start(br[:], t_in["ffn_br"].unsqueeze(0).to_broadcast([P, EXPERTS])).then_inc(m_w, 16)
            for e in range(EXPERTS):
                sp.dma_start(we1[:, e], kb(t_in["ffn_W1"][e])).then_inc(m_w, 16)
            sp.dma_start(wq[:], kb(t_in["mix_Wq"])).then_inc(m_w, 16)
            sp.dma_start(wm[:], kb(t_in["mix_Wm"])).then_inc(m_w, 16)
            sp.dma_start(w2[:], kb(t_in["mix_W2"])).then_inc(m_w, 16)
            sp.dma_start(g2[:], t_in["mix_g2"].unsqueeze(0).to_broadcast([P, D])).then_inc(m_w, 16)
            sp.dma_start(b2[:], t_in["mix_b2"].unsqueeze(0).to_broadcast([P, D])).then_inc(m_w, 16)
            sp.dma_start(be2[:], t_in["ffn_b2"]).then_inc(m_w, 16)
            for e in range(EXPERTS):
                sp.dma_start(we2[:, e], kb(t_in["ffn_W2"][e])).then_inc(m_w, 16)
            sp.sem_inc(m_yfree, 1)
            with sp.Fori(0, SUPERS) as s:
                sp.wait_ge(m_h1, s * 8 + 1)
                for k in range(KD):
                    sp.dma_start(xt[:, k, :].rearrange("p (j c) -> p j c", j=SUP),
                                 xnt_s[bass.ds(s, 1), :, k].rearrange("o p j c -> (o p) j c")).then_inc(m_x, 16)
                sp.wait_ge(m_accfree, s + 1)
                sp.dma_start(acc[:], acc_s[bass.ds(s, 1)].rearrange("o p j f -> (o p) j f")).then_inc(m_accin, 16)
                sp.wait_ge(m_yacc, s * (EXPERTS * SUP) + EXPERTS * SUP)
                sp.dma_start(out_s[bass.ds(s, 1)].rearrange("o p j f -> (o p) j f"), yacc[:]).then_inc(m_stored, 16)
                sp.wait_ge(m_stored, s * 16 + 16)
                sp.sem_inc(m_yfree, 1)

        @block.gpsimd
        def _(pool):
            nc.gpsimd.memset(bdkv[:], 0.0).then_inc(m_const, 1)
            nc.gpsimd.memset(bdks[:], 0.0).then_inc(m_const, 1)
            nc.gpsimd.memset(ones[:], 1.0).then_inc(m_const, 1)
            nc.gpsimd.iota(iota8[:], [[0, SUP], [1, EXPERTS]], base=0, channel_multiplier=0,
                           allow_small_or_imprecise_dtypes=True).then_inc(m_const, 1)
            pool.wait_ge(m_w, 16 * (3 + EXPERTS + 6 + EXPERTS))
            with pool.Fori(0, SUPERS) as s:
                pool.wait_ge(m_accin, s * 16 + 16)
                nc.gpsimd.tensor_tensor(acc[:], acc[:], b2[:].unsqueeze(1).to_broadcast([P, SUP, D]), ALU.add)\
                  .then_inc(m_accb, 1)

        @block.scalar
        def _(act):
            act.wait_ge(m_cols, 1)
            nc.scalar.activation(cols[:], bank[0][:, 0:NV], ACT.Copy).then_inc(m_colst, 1)

            def stdev(l, src, s, per, k):
                act.wait_ge(ln[l]["var"], s * per + (k + 1))
                nc.scalar.activation(std[:], src, ACT.Sqrt, bias=eps[:]).then_inc(ln[l]["std"], 1)
            with act.Fori(0, SUPERS) as s:
                for i in range(4):
                    act.wait_ge(m_qmin, s * 4 + (i + 1))
                    nc.scalar.activation(qexp[:, i % 2, :], qmin[:, i % 2, :], ACT.Exp).then_inc(m_qexp, 1)
                stdev(0, mv[:, :, 1], s, 1, 0)
                for b in range(4):
                    k, half, w = b // 2, b % 2, (4, 3)[b % 2] * P
                    act.wait_ge(m_tr1, s * 4 + (b + 1))
                    nc.scalar.activation(m1t[:, k, half * 4 * P:half * 4 * P + w], bank[4 + b][:, 0:w], ACT.Copy)\
                      .then_inc(m_m1t, 1)
                for i in range(8):
                    m, n = i // 2, i % 2
                    act.wait_ge(m_h1, s * 8 + (i + 2))
                    nc.scalar.activation(h1t[:, m, n * NW:(n + 1) * NW], bank[i % 4][:, 0:NW], ACT.Relu,
                                         bias=c1[:, m:m + 1]).then_inc(m_h1t, 1)
                stdev(1, mv[:, :, 1], s, 1, 0)
                stdev(2, mv[:, :, 1], s, 2, 0)
                stdev(2, var2[:], s, 2, 1)
                for b in range(4):
                    k, half, w = b // 2, b % 2, (4, 3)[b % 2] * P
                    act.wait_ge(m_tr2, s * 4 + (b + 1))
                    nc.scalar.activation(x2t[:, k, half * 4 * P:half * 4 * P + w], bank[b][:, 0:w], ACT.Copy)\
                      .then_inc(m_x2t, 1)
                act.wait_ge(m_gap, s + 1)
                nc.scalar.activation(gap[:], gap[:], ACT.Exp).then_inc(m_exp, 1)
                def gelu(e):
                    for i in range(8):
                        m, n = i // 2, i % 2
                        act.wait_ge(m_hid, s * (8 * EXPERTS) + (8 * e + i + 1))
                        nc.scalar.activation(hot[e % 2][:, m, n * NW:(n + 1) * NW], bank[i % 4][:, 0:NW], ACT.Gelu,
                                             bias=ce[:, e * HB + m:e * HB + m + 1]).then_inc(m_hidt, 1)
                gelu(0)
                for b in range(2):
                    act.wait_ge(m_wtp, s * 2 + (b + 1))
                    w = (4, 3)[b] * P
                    nc.scalar.activation(wt[:, b * 4 * P:b * 4 * P + w], bank[5 + b][0:EXPERTS, 0:w], ACT.Copy)\
                      .then_inc(m_wt, 1)
                for e in range(1, EXPERTS):
                    gelu(e)

        @block.tensor
        def _(pe):
            pe.wait_ge(m_row, 80)
            nc.tensor.transpose(bank[0][:, 0:NV], rows[:], ident[0:NV, 0:NV]).then_inc(m_cols, 1)
            pe.wait_ge(m_colst, 1)
            pe.wait_ge(m_bd, 1)
            pe.wait_ge(m_w, 16 * (3 + EXPERTS + 6 + EXPERTS))
            for m in range(2 * D // P):
                for k in range(KD):
                    nc.tensor.matmul(bank[1][:, m:m + 1], w1[:, KD + k, m * P:(m + 1) * P], cols[:, B1 + k:B1 + k + 1],
                                     start=(k == 0), stop=(k == KD - 1))
            for e in range(EXPERTS):
                for m in range(HB):
                    for k in range(KD):
                        nc.tensor.matmul(bank[2][:, e * HB + m:e * HB + m + 1], we1[:, e, k, m * P:(m + 1) * P],
                                         cols[:, BETA + k:BETA + k + 1], start=(k == 0), stop=(k == KD - 1))
            for k in range(KD):
                last = nc.tensor.matmul(bank[3][:, 0:EXPERTS], betab[:, k, :], wr[:, k, :],
                                        start=(k == 0), stop=(k == KD - 1))
            last.then_inc(m_fold, 1)
            pe.wait_ge(m_setup, 1)
            pe.sem_inc(m_h1, 1)
            with pe.Fori(0, SUPERS) as s:
                pe.wait_ge(m_x, s * 32 + 32)
                for i in range(4):
                    m, n = i // 2, i % 2
                    for k in range(KD):
                        last = nc.tensor.matmul(bank[i][:, 0:NW], wq[:, k, m * P:(m + 1) * P],
                                                xt[:, k, n * NW:(n + 1) * NW], start=(k == 0), stop=(k == KD - 1))
                    last.then_inc(m_q, 1)
                for i in range(4):
                    m, n = i // 2, i % 2
                    pe.wait_ge(m_qt, s * 4 + (i + 1))
                    if i >= 2:
                        pe.wait_ge(m_msg, s * 4 + (i - 1))
                    nc.tensor.matmul(bank[4 + 2 * (i % 2)][:, 0:NW], bdkv[:, m, :], qt[:, m, n * NW:(n + 1) * NW],
                                     start=True, stop=True)
                    nc.tensor.matmul(bank[5 + 2 * (i % 2)][:, 0:NW], bdks[:, m, :], qt[:, m, n * NW:(n + 1) * NW],
                                     start=True, stop=True).then_inc(m_att, 1)
                pe.wait_ge(m_msg, s * 4 + 4)
                for j in range(SUP):
                    for k in range(KD):
                        last = nc.tensor.matmul(tile_cols(bank[0:4], j), msgt[:, k, j * P:(j + 1) * P], wm[:, k, :],
                                                start=(k == 0), stop=(k == KD - 1))
                last.then_inc(m_m1, 1)
                pe.wait_ge(ln[0]["done"], s + 1)
                for b in range(4):
                    k, half = b // 2, b % 2
                    for j in range(4 * half, min(4 * half + 4, SUP)):
                        last = nc.tensor.transpose(bank[4 + b][:, (j % 4) * P:(j % 4 + 1) * P],
                                                   nrm[:, j, k * P:(k + 1) * P], ident[:])
                    last.then_inc(m_tr1, 1)
                pe.wait_ge(m_m1t, s * 4 + 4)
                for i in range(8):
                    m, n = i // 2, i % 2
                    if i >= 4:
                        pe.wait_ge(m_h1t, s * 8 + (i - 3))
                    for k in range(2 * KD):
                        src = xt if k < KD else m1t
                        last = nc.tensor.matmul(bank[i % 4][:, 0:NW], w1[:, k, m * P:(m + 1) * P],
                                                src[:, k % KD, n * NW:(n + 1) * NW],
                                                start=(k == 0), stop=(k == 2 * KD - 1))
                    last.then_inc(m_h1, 1)
                pe.wait_ge(m_h1t, s * 8 + 8)
                for j in range(SUP):
                    for k in range(2 * KD):
                        last = nc.tensor.matmul(tile_cols(bank[4:8], j), h1t[:, k, j * P:(j + 1) * P], w2[:, k, :],
                                                start=(k == 0), stop=(k == 2 * KD - 1))
                last.then_inc(m_h2, 1)
                pe.wait_ge(ln[2]["done"], s + 1)
                for b in range(4):
                    k, half = b // 2, b % 2
                    for j in range(4 * half, min(4 * half + 4, SUP)):
                        last = nc.tensor.transpose(bank[b][:, (j % 4) * P:(j % 4 + 1) * P],
                                                   nrm[:, j, k * P:(k + 1) * P], ident[:])
                    last.then_inc(m_tr2, 1)
                pe.wait_ge(m_x2t, s * 4 + 4)
                for j in range(SUP):
                    for k in range(KD):
                        last = nc.tensor.matmul(bank[4][:, j * EXPERTS:(j + 1) * EXPERTS], x2t[:, k, j * P:(j + 1) * P],
                                                wr[:, k, :], start=(k == 0), stop=(k == KD - 1))
                last.then_inc(m_lg, 1)

                def hidden(e):
                    for i in range(8):
                        m, n = i // 2, i % 2
                        if 8 * e + i >= 4:
                            pe.wait_ge(m_hidt, s * (8 * EXPERTS) + (8 * e + i - 3))
                        for k in range(KD):
                            last = nc.tensor.matmul(bank[i % 4][:, 0:NW], we1[:, e, k, m * P:(m + 1) * P],
                                                    x2t[:, k, n * NW:(n + 1) * NW], start=(k == 0), stop=(k == KD - 1))
                        last.then_inc(m_hid, 1)

                def down(e):
                    pe.wait_ge(m_hidt, s * (8 * EXPERTS) + (8 * e + 8))
                    for j in range(SUP):
                        if e and j % 2 == 0:
                            pe.wait_ge(m_yacc, s * (SUP * EXPERTS) + SUP * (e - 1) + min(j | 1, SUP - 1) + 1)
                        for k in range(HB):
                            last = nc.tensor.matmul(tile_cols(bank[4:8], j), hot[e % 2][:, k, j * P:(j + 1) * P],
                                                    we2[:, e, k, :], start=(k == 0), stop=(k == HB - 1))
                        if j % 2 or j == SUP - 1:
                            last.then_inc(m_y, 1)
                hidden(0)
                pe.wait_ge(m_wfull, s + 1)
                for b in range(2):
                    for j in range(4 * b, min(4 * b + 4, SUP)):
                        last = nc.tensor.transpose(bank[5 + b][0:EXPERTS, (j % 4) * P:(j % 4 + 1) * P],
                                                   wfull[:, j, :], ident[:])
                    last.then_inc(m_wtp, 1)
                pe.wait_ge(m_wt, s * 2 + 2)
                for j in range(SUP):
                    last = nc.tensor.matmul(tile_cols(bank[4:8], j), wt[:, j * P:(j + 1) * P], be2[:],
                                            start=True, stop=True)
                last.then_inc(m_yb, 1)
                hidden(1)
                pe.wait_ge(m_y0, s * SUP + SUP)
                for e in range(EXPERTS):
                    down(e)
                    if e + 2 < EXPERTS:
                        hidden(e + 2)

        @block.vector
        def _(dve):
            dve.wait_ge(m_colst, 1)
            dve.wait_ge(m_const, 4)
            for k in range(KD):
                last = nc.vector.tensor_scalar(betab[:, k, :], ones[:], cols[:, BETA + k:BETA + k + 1], None, ALU.mult)
            last.then_inc(m_bd, 1)
            for k in range(KD):
                for b in range(P // HD):
                    q = slice(b * HD, (b + 1) * HD)
                    nc.vector.tensor_copy(bdkv[q, k, q], kvacc[q, k, q])
                    last = nc.vector.tensor_scalar(bdks[q, k, q], ones[q, q], kvacc[q, k, P:P + 1], None, ALU.mult)
            last.then_inc(m_bd, 1)
            dve.wait_ge(m_w, 16 * (3 + EXPERTS + 6 + EXPERTS))
            dve.wait_ge(m_fold, 1)
            nc.vector.tensor_copy(c1[:], bank[1][:, 0:2 * D // P])
            nc.vector.tensor_tensor(ce[:], bank[2][:, 0:EXPERTS * HB], cols[:, 0:EXPERTS * HB], ALU.add)
            nc.vector.tensor_tensor(lb[:], bank[3][:, 0:EXPERTS], br[:], ALU.add)
            for k in range(KD):
                nc.vector.tensor_scalar(w1[:, KD + k, :], w1[:, KD + k, :], cols[:, G1 + k:G1 + k + 1], None, ALU.mult)
                nc.vector.tensor_scalar(wr[:, k, :], wr[:, k, :], cols[:, GAMMA + k:GAMMA + k + 1], None, ALU.mult)
                last = nc.vector.tensor_scalar(we1[:, :, k, :], we1[:, :, k, :], cols[:, GAMMA + k:GAMMA + k + 1],
                                               None, ALU.mult)
            last.then_inc(m_setup, 1)
            dve.sem_inc(m_accfree, 1)

            def moments(l, src, s, per):
                for j in range(SUP):
                    last = nc.vector.bn_stats(stats[:, j, :], src(j))
                last.then_inc(ln[l]["stats"], 1)
                dve.wait_ge(ln[l]["stats"], s + 1)
                dve.sem_inc(keep["turn"], 1)
                for j in range(SUP):
                    last = nc.vector.bn_aggr(mv[:, j, :], stats[:, j, :])
                last.then_inc(ln[l]["var"], 1)
                dve.wait_ge(ln[l]["std"], s * per + 1)
                nc.vector.reciprocal(rstd[:], std[:]).then_inc(ln[l]["rstd"], 1)
                dve.wait_ge(ln[l]["rstd"], s * per + 1)

            def normalise(l, src, s, by):
                for j in range(SUP):
                    last = nc.vector.tensor_scalar(nrm[:, j, :], src(j), mv[:, j, 0:1], by[:, j:j + 1],
                                                   ALU.subtract, ALU.mult)
                last.then_inc(ln[l]["done"], 1)

            with dve.Fori(0, SUPERS) as s:
                for i in range(4):
                    m, n = i // 2, i % 2
                    dve.wait_ge(m_q, s * 4 + (i + 1))
                    nc.vector.tensor_scalar(qmin[:, i % 2, :], bank[i][:, 0:NW], 0.0, None, ALU.min).then_inc(m_qmin, 1)
                    dve.wait_ge(m_qexp, s * 4 + (i + 1))
                    nc.vector.scalar_tensor_tensor(qt[:, m, n * NW:(n + 1) * NW], bank[i][:, 0:NW], 0.0,
                                                   qexp[:, i % 2, :], ALU.max, ALU.add).then_inc(m_qt, 1)
                for i in range(4):
                    m, n = i // 2, i % 2
                    dve.wait_ge(m_att, s * 4 + (i + 1))
                    nc.vector.tensor_scalar(den[:, i % 2, :], bank[5 + 2 * (i % 2)][:, 0:NW], ATT_EPS, None, ALU.add)\
                      .then_inc(m_den, 1)
                    dve.wait_ge(m_den, s * 8 + (2 * i + 1))
                    nc.vector.reciprocal(rden[:, i % 2, :], den[:, i % 2, :]).then_inc(m_den, 1)
                    dve.wait_ge(m_den, s * 8 + (2 * i + 2))
                    nc.vector.tensor_tensor(msgt[:, m, n * NW:(n + 1) * NW], bank[4 + 2 * (i % 2)][:, 0:NW],
                                            rden[:, i % 2, :], ALU.mult).then_inc(m_msg, 1)
                dve.wait_ge(m_m1, s + 1)
                first = lambda j: tile_cols(bank[0:4], j)
                moments(0, first, s, 1)
                normalise(0, first, s, rstd)
                dve.wait_ge(m_h2, s + 1)
                second = lambda j: tile_cols(bank[4:8], j)
                moments(1, second, s, 1)
                normalise(1, second, s, rstd)
                dve.wait_ge(ln[1]["done"], s + 1)
                nc.vector.tensor_tensor(nrm[:], nrm[:], g2[:].unsqueeze(1).to_broadcast([P, SUP, D]), ALU.mult)\
                  .then_inc(m_x2, 1)
                dve.wait_ge(m_x2, s * 2 + 1)
                dve.wait_ge(m_accb, s + 1)
                nc.vector.tensor_tensor(x2[:], nrm[:], acc[:], ALU.add).then_inc(m_x2, 1)
                dve.wait_ge(m_x2, s * 2 + 2)
                dve.sem_inc(m_accfree, 1)
                rows_of = lambda j: x2[:, j, :]
                moments(2, rows_of, s, 2)
                nc.vector.tensor_tensor(var2[:], rstd[:], rstd[:], ALU.mult).then_inc(ln[2]["step"], 1)
                dve.wait_ge(ln[2]["step"], s * 2 + 1)
                nc.vector.tensor_tensor(var2[:], var2[:], mv[:, :, 1], ALU.mult).then_inc(ln[2]["var"], 1)
                dve.wait_ge(ln[2]["std"], s * 2 + 2)
                nc.vector.reciprocal(rstd2[:], std[:]).then_inc(ln[2]["rstd"], 1)
                dve.wait_ge(ln[2]["rstd"], s * 2 + 2)
                nc.vector.tensor_tensor(rstd2[:], rstd2[:], rstd[:], ALU.mult).then_inc(ln[2]["step"], 1)
                dve.wait_ge(ln[2]["step"], s * 2 + 2)
                normalise(2, rows_of, s, rstd2)
                dve.wait_ge(m_lg, s + 1)
                nc.vector.tensor_tensor(lg[:], bank[4][:, 0:SUP * EXPERTS].rearrange("p (j e) -> p j e", j=SUP),
                                        lb[:].unsqueeze(1).to_broadcast([P, SUP, EXPERTS]), ALU.add).then_inc(m_route, 1)
                dve.wait_ge(m_route, s * 9 + 1)
                dve.sem_inc(keep["turn"], 1)
                for j in range(SUP):
                    last = nc.vector.max(top[:, j, :], lg[:, j, :])
                last.then_inc(m_route, 1)
                dve.wait_ge(m_route, s * 9 + 2)
                nc.vector.tensor_tensor(gap[:], top[:, :, 1], top[:, :, 0], ALU.subtract).then_inc(m_gap, 1)
                for j in range(SUP):
                    last = nc.vector.max_index(idx[:, j, :], top[:, j, :], lg[:, j, :])
                last.then_inc(m_route, 1)
                dve.wait_ge(m_route, s * 9 + 3)
                nc.vector.tensor_copy(idxf[:], idx[:]).then_inc(m_route, 1)
                dve.wait_ge(m_exp, s + 1)
                nc.vector.tensor_scalar(wgt[:, :, 1], gap[:], 1.0, None, ALU.add).then_inc(m_route, 1)
                dve.wait_ge(m_route, s * 9 + 5)
                nc.vector.reciprocal(wgt[:, :, 0], wgt[:, :, 1]).then_inc(m_route, 1)
                dve.wait_ge(m_route, s * 9 + 6)
                nc.vector.tensor_tensor(wgt[:, :, 1], gap[:], wgt[:, :, 0], ALU.mult).then_inc(m_route, 1)
                for i in range(2):
                    last = nc.vector.tensor_tensor(pick[:, i], iota8[:],
                                                   idxf[:, :, i:i + 1].to_broadcast([P, SUP, EXPERTS]), ALU.is_equal)
                last.then_inc(m_route, 1)
                dve.wait_ge(m_route, s * 9 + 8)
                for i in range(2):
                    last = nc.vector.tensor_tensor(pick[:, i], pick[:, i],
                                                   wgt[:, :, i:i + 1].to_broadcast([P, SUP, EXPERTS]), ALU.mult)
                last.then_inc(m_route, 1)
                dve.wait_ge(m_route, s * 9 + 9)
                nc.vector.tensor_tensor(wfull[:], pick[:, 0], pick[:, 1], ALU.add).then_inc(m_wfull, 1)
                dve.wait_ge(m_yb, s + 1)
                dve.wait_ge(m_yfree, s + 1)
                for j in range(SUP):
                    nc.vector.tensor_tensor(yacc[:, j, :], second(j), x2[:, j, :], ALU.add).then_inc(m_y0, 1)
                dve.wait_ge(m_y0, s * SUP + SUP)
                dve.wait_ge(m_wfull, s + 1)
                for e in range(EXPERTS):
                    for j in range(SUP):
                        dve.wait_ge(m_y, s * (4 * EXPERTS) + (4 * e + j // 2 + 1))
                        if e:
                            dve.wait_ge(m_yacc, s * (SUP * EXPERTS) + (SUP * (e - 1) + j + 1))
                        nc.vector.scalar_tensor_tensor(yacc[:, j, :], second(j), wfull[:, j, e:e + 1], yacc[:, j, :],
                                                       ALU.mult, ALU.add).then_inc(m_yacc, 1)
                dve.wait_ge(m_yacc, s * (SUP * EXPERTS) + SUP * EXPERTS)


INPUTS = ["x", "src", "dst",
          "gnn_W1_l", "gnn_b1", "gnn_W1_r", "gnn_W2_l", "gnn_b2", "gnn_W2_r",
          "mix_Wq", "mix_Wk", "mix_Wv", "mix_Wm", "mix_W1", "mix_W2", "mix_g1", "mix_b1", "mix_g2", "mix_b2",
          "ffn_gamma", "ffn_beta", "ffn_Wr", "ffn_br", "ffn_W1", "ffn_b1", "ffn_W2", "ffn_b2"]


def kernel(**inputs):
    import numpy as np
    import concourse.bacc as bacc
    from concourse.bass_utils import run_bass_kernel_spmd

    nc = bacc.Bacc("TRN2", target_bir_lowering=False, num_devices=1)
    arrays, t_in = {}, {}
    for name in INPUTS:
        a = np.ascontiguousarray(inputs[name if name in inputs else "L0_" + name])
        if name == "x":
            padded = np.zeros((NPAD, D), a.dtype)
            padded[:N_NODES] = a
            a = padded
        arrays[f"in_{name}"] = a
        t_in[name] = nc.dram_tensor(f"in_{name}", a.shape, mybir.dt.from_np(a.dtype), kind="ExternalInput").ap()
    out = nc.dram_tensor("out", (NPAD, D), F32, kind="ExternalOutput").ap()
    program(nc, t_in, out)
    r = run_bass_kernel_spmd(nc, [arrays], core_ids=[0])
    return r.results[0]["out"][:N_NODES]
```

```python
from contextlib import ExitStack

import concourse.bass as bass
from concourse import mybir

F32 = mybir.dt.float32
F16 = mybir.dt.float16
F8 = mybir.dt.float8e4
I32 = mybir.dt.int32
U32 = mybir.dt.uint32
ALU = mybir.AluOpType
ACT = mybir.ActivationFunctionType

P = 128
N_NODES, N_EDGES, D = 6250, 200000, 256
KD = D // P
TILES = -(-N_NODES // P)
NPAD = TILES * P
SUP = 7
SUPERS = TILES // SUP
R = SUP * P
NB = 2
NW = R // NB
LN_EPS = 1e-5
ATT_EPS = 1e-6
HEADS, HD = 8, 32
EXPERTS, HID = 8, 512
HB = HID // P

GN = 8
GROUPS = P // GN
CHUNKS = 3
GE = CHUNKS * P
EROW = 32
WROWS = GE // EROW
GC = GN * TILES
ROW = 400
ROWS = N_EDGES // ROW
STILES = -(-(TILES * GROUPS + 1) // P)
CAP = 16
CSCALE = CAP / 2.0
VEC = [i * KD for i in range(4)]
CHOICES = 2 * SUP
REGION = NPAD + P
LISTS = -(-(EXPERTS * REGION + P) // (P * P)) * P * P
LTILES = (2 * NPAD + EXPERTS * (P - 1)) // P
AHEAD = 3
LOOPED = (LTILES - AHEAD) // 2 * 2
PLACE_STEPS = 3 + 2 * 4 + 5
ENTRY_STEPS = 5
EP = 125
ELEN = N_EDGES // EP
LO_SCALE = 2048.0
FAR = -1.0e6

ONEHOTS = 4
BANKS = 4
SPLIT = (0, TILES // 2, TILES)


def program(nc, t_in, out):
    with ExitStack() as ctx:
        def kept_sem(name):
            return ctx.enter_context(nc.semaphore(name))

        def dram(name, shape, dt):
            return nc.dram_tensor(name, shape, dt).ap()

        d = dict(
            edges=dram("edges", [(N_EDGES + GE) // EROW, 2 * EROW], F32),
            adj=dram("adj", [TILES, P, TILES * P // 4], I32),
            xnt=dram("xnt", [TILES, P, KD, P], F32),
            acc=dram("acc", [NPAD, D], F32),
            table=dram("table", [NPAD, D], F32),
            lists=dram("lists", [LISTS, 4], F32),
            feat1=dram("feat1", [NPAD, D], F32),
            feat2=dram("feat2", [NPAD, D], F32),
        )

        def sb(stack, name, shape, dt):
            return stack.enter_context(nc.sbuf_tensor(name, shape, dt))

        keep = dict(
            ident=sb(ctx, "ident", [P, P], F32),
            eps=sb(ctx, "eps", [P, 1], F32),
            kvacc=sb(ctx, "kvacc", [P, KD, P + 1], F32),
            uncovered=sb(ctx, "uncovered", [P, 1], F32),
            flag=sb(ctx, "flag", [1, 1], I32),
            turn=kept_sem("turn"),
        )

        def run(phase, *args):
            used = []
            with ExitStack() as mem:
                def sem(name, pool_dma=False):
                    if pool_dma:
                        return kept_sem(name)
                    used.append(mem.enter_context(nc.semaphore(name)))
                    return used[-1]
                phase(nc, sem, mem, d, *args)
                with nc.Block() as block:
                    @block.gpsimd
                    def _(pool):
                        for s in used:
                            pool.sem_clear(s)

        with ExitStack() as graph:
            keep["window"] = sb(graph, "window", [P, STILES, WROWS], I32)
            run(edge_phase, t_in, keep)
            keep["gathered"] = sb(graph, "gathered", [P, STILES, GE, 2], F32)
            keep["yh"] = sb(graph, "yh", [P, TILES, D + 2], F16)
            keep["yl"] = sb(graph, "yl", [P, TILES, D], F16)
            keep["w2lr"] = sb(graph, "w2lr", [P, KD, 2 * D], F32)
            keep["w1r"] = sb(graph, "w1r", [P, KD, D], F32)
            keep["b1"] = sb(graph, "b1", [P, D], F32)
            keep["b2"] = sb(graph, "b2", [P, D], F32)
            keep["rdeg"] = sb(graph, "rdeg", [P, TILES], F32)
            keep["unscale"] = sb(graph, "unscale", [P, 2], F32)
            run(norm_phase, t_in, keep)
            run(count_phase, keep)
            with ExitStack() as layers:
                keep["y2h"] = sb(layers, "y2h", [P, TILES, D], F16)
                keep["y2l"] = sb(layers, "y2l", [P, TILES, D], F16)
                for n, (h0, h1) in enumerate(zip(SPLIT, SPLIT[1:])):
                    keep[f"part{n}"] = sb(layers, f"part{n}", [P, h1 - h0, P], F8)
                run(layer1_phase, keep)
                run(layer2_phase, keep)
        run(general_phase, t_in, keep)
        for name, n in (("we1", EXPERTS * KD * HID), ("we2", EXPERTS * HB * D), ("be1", EXPERTS * HID),
                        ("be2", EXPERTS * D), ("cols", 4 * KD), ("betab", KD * P), ("ends", EXPERTS)):
            keep[name] = sb(ctx, name, [P, n], F32)
        keep["we1"] = keep["we1"][:].rearrange("p (e k h) -> p e k h", e=EXPERTS, k=KD)
        keep["we2"] = keep["we2"][:].rearrange("p (e k f) -> p e k f", e=EXPERTS, k=HB)
        keep["betab"] = keep["betab"][:].rearrange("p (k c) -> p k c", k=KD)
        run(mix_phase, t_in, keep, out)
        run(expert_phase, keep, out)


def edge_phase(nc, sem, mem, d, t_in, keep):
    def sb(name, shape, dt):
        return mem.enter_context(nc.sbuf_tensor(name, shape, dt))

    src, dst = t_in["src"], t_in["dst"]
    src_i = sb("src_i", [EP, ELEN], I32)
    dst_i = sb("dst_i", [EP, ELEN], I32)
    lo_i = sb("lo_i", [EP, ELEN], I32)
    pair = sb("pair", [EP, ELEN, 2], F32)
    pad = sb("pad", [P, CHUNKS, 2], F32)
    first_i = sb("first_i", [1, ROWS], I32)
    first_f = sb("first_f", [1, ROWS], F32)
    ones_row = sb("ones_row", [1, P], F32)
    firsts = sb("firsts", [P, ROWS], F32)
    bound = sb("bound", [P, STILES], F32)
    below = sb("below", [P, STILES], F32)
    row_i = sb("row_i", [P, STILES], I32)
    rows_i = sb("rows_i", [P, STILES, ROW], I32)
    rows_f = sb("rows_f", [P, STILES, ROW], F32)
    scratch = sb("scratch", [P, STILES, max(ROWS, ROW)], F32)
    within = sb("within", [P, STILES], F32)
    start_f = sb("start_f", [P, STILES], F32)
    start_i = sb("start_i", [P, STILES], I32)
    row0 = sb("row0", [P, STILES], F32)
    steps = sb("steps", [P, STILES, WROWS], F32)
    spread = mem.enter_context(nc.psum_tensor("spread", [P, 512], F32))

    dst_f = sb("dst_f", [EP, ELEN + 1], F32)
    next_i = sb("next_i", [EP, 1], I32)
    falls = sb("falls", [EP, ELEN], F32)
    e_next, e_order = sem("e_next"), sem("e_order")
    e_dst, e_src, e_first = sem("e_dst"), sem("e_src"), sem("e_first")
    e_const = sem("e_const")
    e_split = sem("e_split")
    e_firstf, e_spread = sem("e_firstf"), sem("e_spread")
    e_search = sem("e_search")
    e_rowi, e_rows = sem("e_rowi"), sem("e_rows", pool_dma=True)
    e_stored = sem("e_stored")
    dst_rows = dst.rearrange("(r n) -> r n", n=ROW)

    with nc.Block() as block:
        @block.sync
        def _(sp):
            with nc.allow_non_contiguous_dma(reason="one element of each row"):
                sp.dma_start(first_i[:], dst.rearrange("(r n) -> n r", n=ROW)[0:1, :]).then_inc(e_first, 16)
            sp.dma_start(dst_i[:], dst.rearrange("(p n) -> p n", p=EP)).then_inc(e_dst, 16)
            sp.dma_start(src_i[:], src.rearrange("(p n) -> p n", p=EP)).then_inc(e_src, 16)
            sp.wait_ge(e_order, 1)
            with nc.allow_non_contiguous_dma(reason="one element of each row"):
                sp.dma_start(next_i[0:EP - 1, :], dst.rearrange("(p n) -> p n", p=EP)[1:EP, 0:1]).then_inc(e_next, 16)
            sp.wait_ge(e_const, 1)
            flat = d["edges"].rearrange("r (n c) -> (r n) c", c=2)
            sp.dma_start(flat[N_EDGES:N_EDGES + GE, :].rearrange("(p n) c -> p n c", p=P), pad[:]).then_inc(e_stored, 16)
            sp.wait_ge(e_split, 5)
            sp.dma_start(flat[0:N_EDGES, :].rearrange("(p n) c -> p n c", p=EP), pair[:])\
              .then_inc(e_stored, 16)
            sp.wait_ge(e_stored, 32)

        @block.gpsimd
        def _(pool):
            nc.gpsimd.memset(pad[:, :, 0:1], 0.0)
            nc.gpsimd.memset(pad[:, :, 1:2], FAR).then_inc(e_const, 1)
            nc.gpsimd.memset(ones_row[:], 1.0).then_inc(e_const, 1)
            nc.gpsimd.iota(bound[:], [[GN * P, STILES]], base=0, channel_multiplier=GN,
                           allow_small_or_imprecise_dtypes=True).then_inc(e_const, 1)
            nc.gpsimd.memset(keep["eps"][:], LN_EPS).then_inc(e_const, 1)
            nc.gpsimd.memset(keep["kvacc"][:], 0.0).then_inc(e_const, 1)
            nc.gpsimd.memset(keep["ident"][:], 0.0).then_inc(e_const, 1)
            nc.gpsimd.iota(steps[:], [[0, STILES], [1, WROWS]], base=0, channel_multiplier=0,
                           allow_small_or_imprecise_dtypes=True).then_inc(e_const, 1)
            pool.wait_ge(e_const, 6)
            nc.gpsimd.affine_select(out=keep["ident"][:], in_=keep["ident"][:], compare_op=ALU.not_equal,
                                    fill=1.0, base=0, pattern=[[-1, P]], channel_multiplier=1).then_inc(e_const, 1)
            pool.wait_ge(e_rowi, 1)
            for r in range(STILES):
                pool.indirect_dma_start(rows_i[:, r, :], None, dst_rows,
                                        bass.IndirectOffsetOnAxis(ap=row_i[:, r:r + 1], axis=0)).then_inc(e_rows, 16)
            pool.wait_ge(e_const, 8)
            pool.wait_ge(e_rows, 16 * STILES)

        @block.tensor
        def _(pe):
            pe.wait_ge(e_const, 2)
            pe.wait_ge(e_firstf, 1)
            nc.tensor.matmul(spread[:, 0:ROWS], ones_row[:], first_f[:], start=True, stop=True).then_inc(e_spread, 1)

        @block.vector
        def _(dve):
            nc.vector.memset(next_i[:], N_NODES).then_inc(e_order, 1)
            nc.vector.memset(keep["uncovered"][:], 0.0).then_inc(e_order, 1)
            dve.wait_ge(e_first, 16)
            nc.vector.tensor_copy(first_f[:], first_i[:]).then_inc(e_firstf, 1)
            dve.wait_ge(e_const, 3)
            dve.wait_ge(e_spread, 1)
            nc.vector.tensor_copy(firsts[:], spread[:, 0:ROWS]).then_inc(e_search, 1)
            dve.wait_ge(e_search, 1)
            for r in range(STILES):
                last = nc.vector.tensor_scalar(scratch[:, r, 0:ROWS], firsts[:], bound[:, r:r + 1], 0.0,
                                               ALU.is_lt, ALU.add, accum_out=below[:, r:r + 1])
            last.then_inc(e_search, 1)
            dve.wait_ge(e_search, 2)
            nc.vector.tensor_scalar(below[:], below[:], -1.0, 0.0, ALU.add, ALU.max).then_inc(e_search, 1)
            dve.wait_ge(e_search, 3)
            nc.vector.tensor_copy(row_i[:], below[:]).then_inc(e_rowi, 1)
            dve.wait_ge(e_src, 16)
            dve.wait_ge(e_dst, 16)
            dve.wait_ge(e_next, 16)
            nc.vector.tensor_copy(dst_f[:, 0:ELEN], dst_i[:]).then_inc(e_order, 1)
            nc.vector.tensor_copy(dst_f[:, ELEN:], next_i[:]).then_inc(e_order, 1)
            dve.wait_ge(e_order, 4)
            nc.vector.tensor_tensor(falls[:], dst_f[:, 0:ELEN], dst_f[:, 1:], ALU.subtract).then_inc(e_order, 1)
            dve.wait_ge(e_order, 5)
            nc.vector.tensor_scalar(falls[:], falls[:], 0.0, 0.0, ALU.is_gt, ALU.add,
                                    accum_out=keep["uncovered"][0:EP, :]).then_inc(e_order, 1)
            dve.wait_ge(e_order, 6)
            nc.vector.tensor_scalar(lo_i[:], src_i[:], P - 1, None, ALU.bitwise_and).then_inc(e_split, 1)
            dve.wait_ge(e_split, 1)
            nc.vector.tensor_scalar(src_i[:], src_i[:], 7, None, ALU.logical_shift_right).then_inc(e_split, 1)
            nc.vector.tensor_scalar(dst_i[:], dst_i[:], TILES, None, ALU.mult).then_inc(e_split, 1)
            nc.vector.tensor_copy(pair[:, :, 0], lo_i[:]).then_inc(e_split, 1)
            dve.wait_ge(e_split, 4)
            nc.vector.tensor_tensor(pair[:, :, 1], src_i[:], dst_i[:], ALU.add).then_inc(e_split, 1)
            dve.wait_ge(e_rows, 16 * STILES)
            nc.vector.tensor_copy(rows_f[:], rows_i[:]).then_inc(e_search, 1)
            dve.wait_ge(e_search, 4)
            for r in range(STILES):
                last = nc.vector.tensor_scalar(scratch[:, r, 0:ROW], rows_f[:, r, :], bound[:, r:r + 1], 0.0,
                                               ALU.is_lt, ALU.add, accum_out=within[:, r:r + 1])
            last.then_inc(e_search, 1)
            dve.wait_ge(e_search, 5)
            nc.vector.scalar_tensor_tensor(start_f[:], below[:], float(ROW), within[:], ALU.mult, ALU.add)\
              .then_inc(e_search, 1)
            dve.wait_ge(e_search, 6)
            nc.vector.tensor_copy(start_i[:], start_f[:]).then_inc(e_search, 1)
            dve.wait_ge(e_search, 7)
            nc.vector.tensor_scalar(start_i[:], start_i[:], 5, None, ALU.logical_shift_right).then_inc(e_search, 1)
            dve.wait_ge(e_search, 8)
            nc.vector.tensor_copy(row0[:], start_i[:]).then_inc(e_search, 1)
            dve.wait_ge(e_search, 9)
            dve.wait_ge(e_const, 7)
            nc.vector.tensor_tensor(keep["window"][:], steps[:], row0[:].unsqueeze(2).to_broadcast([P, STILES, WROWS]),
                                    ALU.add).then_inc(e_search, 1)
            dve.wait_ge(e_search, 10)


def norm_phase(nc, sem, mem, d, t_in, keep):
    def sb(name, shape, dt):
        return mem.enter_context(nc.sbuf_tensor(name, shape, dt))

    def ps(name):
        return mem.enter_context(nc.psum_tensor(name, [P, 512], F32))

    ident, eps, kvacc, yh, yl = (keep[k] for k in ("ident", "eps", "kvacc", "yh", "yl"))
    w2lr, w1r, b1, b2, unscale = (keep[k] for k in ("w2lr", "w1r", "b1", "b2", "unscale"))
    xb = sb("xb", [P, SUP, D], F32)
    xn = sb("xn", [P, SUP, D], F32)
    xr = sb("xr", [P, SUP, D], F32)
    xnt = sb("xnt_sb", [P, KD, R], F32)
    wyk = sb("wyk", [P, KD, 2 * D], F32)
    wv = sb("wv", [P, KD, D], F32)
    stats = sb("stats", [P, SUP, 6], F32)
    meanvar = sb("meanvar", [P, SUP, 2], F32)
    std = sb("std", [P, SUP], F32)
    rstd = sb("rstd", [P, SUP], F32)
    kmin = sb("kmin", [P, 2, D], F32)
    kexp = sb("kexp", [P, 2, D], F32)
    kbuf = sb("kbuf", [P, SUP, D], F32)
    vbuf = sb("vbuf", [P, SUP, KD, P + 1], F32)
    valid = sb("valid", [P, TILES], F32)
    ones = sb("ones", [P, P], F32)
    squares = sb("squares", [P, 4, KD * D], F32)
    sumsq = sb("sumsq", [P, 4], F32)
    norms = sb("norms", [P, 4], F32)
    bnd = sb("bnd", [P, 2], F32)
    tmp = sb("tmp", [P, 2], F32)
    scale = sb("scale", [P, 2], F32)
    rscale = sb("rscale", [P, 2], F32)
    pt = [ps(f"pt{i}") for i in range(2)]
    pyk = [ps(f"pyk{i}") for i in range(2)]
    pv = [ps(f"pv{i}") for i in range(2)]
    pkv = ps("pkv")

    n_w, n_b = sem("n_w"), sem("n_b")
    n_gather = sem("n_gather", pool_dma=True)
    n_const = sem("n_const")
    n_sq, n_norm, n_sc = sem("n_sq"), sem("n_norm"), sem("n_sc")
    n_sums = sem("n_sums")
    n_x, n_xfree = sem("n_x"), sem("n_xfree")
    n_stats, n_var, n_std, n_rstd, n_xn = (sem(f"n_{k}") for k in ("stats", "var", "std", "rstd", "xn"))
    n_xr, n_xrfree, n_xrst = sem("n_xr"), sem("n_xrfree"), sem("n_xrst")
    n_tr, n_xnt, n_xntst, n_xntfree = sem("n_tr"), sem("n_xnt"), sem("n_xntst"), sem("n_xntfree")
    n_yk, n_ykfree = sem("n_yk"), sem("n_ykfree")
    n_yh, n_v, n_kmin, n_kexp, n_k = (sem(f"n_{k}") for k in ("yh", "v", "kmin", "kexp", "k"))
    n_yl, n_ones = sem("n_yl"), sem("n_ones")
    n_kv, n_kvacc = sem("n_kv"), sem("n_kvacc")

    kb = lambda w: w.rearrange("(k p) n -> p k n", p=P)
    x_s = t_in["x"].rearrange("(s j p) f -> s p j f", p=P, j=SUP)
    acc_s = d["acc"].rearrange("(s j p) f -> s p j f", p=P, j=SUP)
    xnt_s = d["xnt"].rearrange("(s j) p k c -> s p k j c", j=SUP)

    with nc.Block() as block:
        @block.sync
        def _(sp):
            sp.dma_start(wyk[:, :, 0:D], kb(t_in["gnn_W1_l"])).then_inc(n_w, 16)
            sp.dma_start(wyk[:, :, D:2 * D], kb(t_in["mix_Wk"])).then_inc(n_w, 16)
            sp.dma_start(wv[:], kb(t_in["mix_Wv"])).then_inc(n_w, 16)
            sp.dma_start(w1r[:], kb(t_in["gnn_W1_r"])).then_inc(n_w, 16)
            sp.dma_start(w2lr[:, :, 0:D], kb(t_in["gnn_W2_l"])).then_inc(n_w, 16)
            sp.dma_start(w2lr[:, :, D:2 * D], kb(t_in["gnn_W2_r"])).then_inc(n_w, 16)
            sp.dma_start(b1[:], t_in["gnn_b1"].unsqueeze(0).to_broadcast([P, D])).then_inc(n_b, 16)
            sp.dma_start(b2[:], t_in["gnn_b2"].unsqueeze(0).to_broadcast([P, D])).then_inc(n_b, 16)
            sp.sem_inc(n_xrfree, 1)
            sp.sem_inc(n_xntfree, 1)
            with sp.Fori(0, SUPERS) as s:
                sp.wait_ge(n_xfree, s + 1)
                sp.dma_start(xb[:], x_s[bass.ds(s, 1)].rearrange("o p j f -> (o p) j f")).then_inc(n_x, 16)
                sp.wait_ge(n_xr, s + 1)
                sp.dma_start(acc_s[bass.ds(s, 1)].rearrange("o p j f -> (o p) j f"), xr[:]).then_inc(n_xrst, 16)
                sp.wait_ge(n_xnt, 4 * s + 4)
                for k in range(KD):
                    sp.dma_start(xnt_s[bass.ds(s, 1), :, k].rearrange("o p j c -> (o p) j c"),
                                 xnt[:, k, :].rearrange("p (j c) -> p j c", j=SUP)).then_inc(n_xntst, 16)
                sp.wait_ge(n_xrst, 16 * s + 16)
                sp.sem_inc(n_xrfree, 1)
                sp.wait_ge(n_xntst, 32 * s + 32)
                sp.sem_inc(n_xntfree, 1)

        @block.gpsimd
        def _(pool):
            nc.gpsimd.memset(ones[:], 1.0).then_inc(n_const, 1)
            nc.gpsimd.memset(valid[:], 1.0).then_inc(n_const, 1)
            nc.gpsimd.memset(yh[:, :, D:D + 2], 1.0).then_inc(n_const, 1)
            pool.wait_ge(n_const, 3)
            nc.gpsimd.affine_select(out=valid[:], in_=valid[:], compare_op=ALU.is_ge, fill=0.0,
                                    base=N_NODES - 1, pattern=[[-P, TILES]], channel_multiplier=-1).then_inc(n_const, 1)
            pool.wait_ge(n_const, 4)
            pool.sem_inc(n_xfree, 1)
            for r in range(STILES):
                for k in range(WROWS):
                    pool.indirect_dma_start(keep["gathered"][:, r, k * EROW:(k + 1) * EROW, :].rearrange("p n c -> p (n c)"),
                                            None, d["edges"],
                                            bass.IndirectOffsetOnAxis(ap=keep["window"][:, r, k:k + 1], axis=0))\
                        .then_inc(n_gather, 16)
            with pool.Fori(0, SUPERS) as s:
                pool.wait_ge(n_xn, s + 1)
                pool.wait_ge(n_xrfree, s + 1)
                nc.gpsimd.tensor_tensor(xr[:], xb[:], xn[:], ALU.add).then_inc(n_xr, 1)
                pool.wait_ge(n_xr, s + 1)
                pool.sem_inc(n_xfree, 1)
            pool.wait_ge(n_gather, 16 * STILES * WROWS)

        @block.scalar
        def _(act):
            act.wait_ge(n_w, 96)
            act.wait_ge(n_b, 32)
            for i, w in enumerate((wyk[:, :, 0:D], w1r[:], w2lr[:, :, 0:D])):
                nc.scalar.activation(squares[:, i, :].rearrange("p (k n) -> p k n", k=KD), w, ACT.Square,
                                     accum_out=sumsq[:, i:i + 1]).then_inc(n_sq, 1)
            nc.scalar.activation(squares[:, 3, 0:D], b1[:], ACT.Square, accum_out=sumsq[:, 3:4]).then_inc(n_sq, 1)
            act.wait_ge(n_sums, 1)
            act.wait_ge(n_sq, 4)
            nc.scalar.activation(norms[:, 0:3], pt[0][:, 0:3], ACT.Sqrt).then_inc(n_norm, 1)
            nc.scalar.activation(norms[:, 3:4], sumsq[:, 3:4], ACT.Sqrt).then_inc(n_norm, 1)
            with act.Fori(0, SUPERS) as s:
                act.wait_ge(n_var, s + 1)
                nc.scalar.activation(std[:], meanvar[:, :, 1], ACT.Sqrt, bias=eps[:]).then_inc(n_std, 1)
                act.wait_ge(n_xntfree, s + 1)
                for b in range(4):
                    k, half = b // 2, b % 2
                    act.wait_ge(n_tr, 4 * s + b + 1)
                    w = (4, 3)[half] * P
                    nc.scalar.activation(xnt[:, k, half * 4 * P:half * 4 * P + w], pt[half][:, 0:w], ACT.Copy)\
                      .then_inc(n_xnt, 1)
                for j in range(SUP):
                    act.wait_ge(n_yk, s * SUP + (j + 1))
                    nc.scalar.activation(yh[:, bass.ds(s * SUP + j, 1), 0:D].rearrange("p o f -> p (o f)"),
                                         pyk[j % 2][:, 0:D], ACT.Copy, scale=1.0 / LO_SCALE).then_inc(n_yh, 1)
                    nc.scalar.activation(vbuf[:, j, :, 0:P],
                                         pv[j % 2][:, 0:D].rearrange("p (k f) -> p k f", k=KD),
                                         ACT.Copy).then_inc(n_v, 1)
                    act.wait_ge(n_kmin, s * SUP + (j + 1))
                    nc.scalar.activation(kexp[:, j % 2, :], kmin[:, j % 2, :], ACT.Exp).then_inc(n_kexp, 1)

        @block.vector
        def _(dve):
            dve.wait_ge(n_norm, 2)
            top = float(D) ** 0.5
            nc.vector.tensor_tensor(tmp[:, 0:1], norms[:, 0:1], norms[:, 1:2], ALU.add).then_inc(n_sc, 1)
            nc.vector.tensor_scalar(bnd[:, 0:1], norms[:, 0:1], top, None, ALU.mult).then_inc(n_sc, 1)
            dve.wait_ge(n_sc, 2)
            nc.vector.scalar_tensor_tensor(tmp[:, 1:2], tmp[:, 0:1], top, norms[:, 3:4], ALU.mult, ALU.add)\
              .then_inc(n_sc, 1)
            dve.wait_ge(n_sc, 3)
            nc.vector.tensor_tensor(bnd[:, 1:2], tmp[:, 1:2], norms[:, 2:3], ALU.mult).then_inc(n_sc, 1)
            dve.wait_ge(n_sc, 4)
            nc.vector.tensor_scalar(bnd[:], bnd[:], 1e-20, None, ALU.max).then_inc(n_sc, 1)
            dve.wait_ge(n_sc, 5)
            nc.vector.reciprocal(scale[:], bnd[:]).then_inc(n_sc, 1)
            dve.wait_ge(n_sc, 6)
            nc.vector.tensor_scalar(scale[:], scale[:], 2.0 ** 15 * LO_SCALE, None, ALU.mult).then_inc(n_sc, 1)
            dve.wait_ge(n_sc, 7)
            nc.vector.tensor_scalar(scale[:].bitcast(I32), scale[:].bitcast(I32), 0x7F800000, None,
                                    ALU.bitwise_and).then_inc(n_sc, 1)
            dve.wait_ge(n_sc, 8)
            nc.vector.reciprocal(rscale[:], scale[:]).then_inc(n_sc, 1)
            nc.vector.tensor_scalar(wyk[:, :, 0:D], wyk[:, :, 0:D], scale[:, 0:1], None, ALU.mult).then_inc(n_sc, 1)
            nc.vector.tensor_scalar(w2lr[:, :, 0:D], w2lr[:, :, 0:D], scale[:, 1:2], None, ALU.mult).then_inc(n_sc, 1)
            dve.wait_ge(n_sc, 11)
            nc.vector.tensor_scalar(unscale[:], rscale[:], LO_SCALE, None, ALU.mult).then_inc(n_sc, 1)
            dve.wait_ge(n_const, 4)
            dve.sem_inc(n_ykfree, 2)
            with dve.Fori(0, SUPERS) as s:
                dve.wait_ge(n_x, 16 * s + 16)
                for j in range(SUP):
                    last = nc.vector.bn_stats(stats[:, j, :], xb[:, j, :])
                last.then_inc(n_stats, 1)
                dve.wait_ge(n_stats, s + 1)
                dve.sem_inc(keep["turn"], 1)
                for j in range(SUP):
                    last = nc.vector.bn_aggr(meanvar[:, j, :], stats[:, j, :])
                last.then_inc(n_var, 1)
                dve.wait_ge(n_std, s + 1)
                nc.vector.reciprocal(rstd[:], std[:]).then_inc(n_rstd, 1)
                dve.wait_ge(n_rstd, s + 1)
                for j in range(SUP):
                    last = nc.vector.tensor_scalar(xn[:, j, :], xb[:, j, :], meanvar[:, j, 0:1], rstd[:, j:j + 1],
                                                   ALU.subtract, ALU.mult)
                last.then_inc(n_xn, 1)
                nc.vector.tensor_copy(vbuf[:, :, :, P:P + 1].rearrange("p j k o -> p j (k o)"),
                                      valid[:, bass.ds(s * SUP, SUP)].unsqueeze(2).to_broadcast([P, SUP, KD]))\
                  .then_inc(n_ones, 1)
                for j in range(SUP):
                    dve.wait_ge(n_yk, s * SUP + (j + 1))
                    dve.wait_ge(n_yh, s * SUP + (j + 1))
                    nc.vector.tensor_scalar(kmin[:, j % 2, :], pyk[j % 2][:, D:2 * D], 0.0, None, ALU.min)\
                      .then_inc(n_kmin, 1)
                    nc.vector.scalar_tensor_tensor(yl[:, bass.ds(s * SUP + j, 1), :].rearrange("p o f -> p (o f)"),
                                                   yh[:, bass.ds(s * SUP + j, 1), 0:D].rearrange("p o f -> p (o f)"),
                                                   -LO_SCALE, pyk[j % 2][:, 0:D], ALU.mult, ALU.add).then_inc(n_yl, 1)
                    dve.wait_ge(n_kexp, s * SUP + (j + 1))
                    nc.vector.scalar_tensor_tensor(kbuf[:, j, :], pyk[j % 2][:, D:2 * D], 0.0, kexp[:, j % 2, :],
                                                   ALU.max, ALU.add).then_inc(n_ykfree, 1)
                dve.wait_ge(n_kv, s + 1)
                nc.vector.tensor_tensor(kvacc[:], pkv[:, 0:KD * (P + 1)].rearrange("p (k n) -> p k n", k=KD),
                                        kvacc[:], ALU.add).then_inc(n_kvacc, 1)
                dve.wait_ge(n_kvacc, s + 1)

        @block.tensor
        def _(pe):
            pe.wait_ge(n_const, 1)
            pe.wait_ge(n_sq, 4)
            nc.tensor.matmul(pt[0][:, 0:3], ones[:], sumsq[:, 0:3], start=True, stop=True).then_inc(n_sums, 1)
            pe.wait_ge(n_sc, 11)
            with pe.Fori(0, SUPERS) as s:
                pe.wait_ge(n_xn, s + 1)
                for b in range(4):
                    k, half = b // 2, b % 2
                    if b >= 2:
                        pe.wait_ge(n_xnt, s * 4 + (b - 1))
                    for j in range(4 * half, min(4 * half + 4, SUP)):
                        last = nc.tensor.transpose(pt[half][:, (j % 4) * P:(j % 4 + 1) * P],
                                                   xn[:, j, k * P:(k + 1) * P], ident[:])
                    last.then_inc(n_tr, 1)
                pe.wait_ge(n_xnt, 4 * s + 4)
                for j in range(SUP):
                    pe.wait_ge(n_ykfree, s * SUP + (j + 1))
                    for k in range(KD):
                        nc.tensor.matmul(pyk[j % 2][:], xnt[:, k, j * P:(j + 1) * P], wyk[:, k, :],
                                         start=(k == 0), stop=(k == KD - 1))
                    for k in range(KD):
                        last = nc.tensor.matmul(pv[j % 2][:, 0:D], xnt[:, k, j * P:(j + 1) * P],
                                                wv[:, k, :], start=(k == 0), stop=(k == KD - 1))
                    last.then_inc(n_yk, 1)
                pe.wait_ge(n_ykfree, s * SUP + (SUP + 2))
                pe.wait_ge(n_v, s * SUP + SUP)
                pe.wait_ge(n_ones, s + 1)
                for k in range(KD):
                    for j in range(SUP):
                        last = nc.tensor.matmul(pkv[:, k * (P + 1):(k + 1) * (P + 1)], kbuf[:, j, k * P:(k + 1) * P],
                                                vbuf[:, j, k, :], start=(j == 0), stop=(j == SUP - 1))
                last.then_inc(n_kv, 1)


def count_phase(nc, sem, mem, d, keep):
    def sb(name, shape, dt):
        return mem.enter_context(nc.sbuf_tensor(name, shape, dt))

    ident, gathered = keep["ident"], keep["gathered"]
    lo_all = sb("lo_all", [P, STILES * P, CHUNKS], F16)
    key_all = sb("key_all", [P, STILES * P, CHUNKS], F32)
    iota_key = sb("iota_key", [P, GC], F16)
    iota_lo = sb("iota_lo", [P, P, GROUPS * CHUNKS], F16)
    keybase = sb("keybase", [P, STILES * P, CHUNKS], F32)
    lo = sb("lo", [P, GROUPS * CHUNKS], F16)
    key = sb("key", [P, GROUPS, CHUNKS], F32)
    hot_key = sb("hot_key", [P, ONEHOTS, CHUNKS, GC], F16)
    hot_lo = [sb(f"hot_lo{i}", [P, P, GROUPS * CHUNKS], F16) for i in range(2)]
    counts = [sb(f"counts{i}", [P, TILES, P], F8) for i in range(2)]
    pc = [mem.enter_context(nc.psum_tensor(f"pc{i}", [P, 512], F32)) for i in range(BANKS)]

    c_const = sem("c_const")
    c_turned, c_taken = sem("c_turned"), sem("c_taken")
    c_keys = sem("c_keys")
    c_hot = sem("c_hot")
    c_group = sem("c_group")
    c_evac = sem("c_evac")
    c_countsfree = [sem(f"c_countsfree{i}") for i in range(2)]
    c_stored = [sem(f"c_stored{i}", pool_dma=True) for i in range(2)]
    late = sb("late", [P, STILES * P], F32)
    missed = sb("missed", [P, 1], F32)
    c_late = sem("c_late")

    with nc.Block() as block:
        @block.sync
        def _(sp):
            pass

        @block.gpsimd
        def _(pool):
            iota = lambda *a, **k: nc.gpsimd.iota(*a, allow_small_or_imprecise_dtypes=True, **k)
            iota(iota_key[:], [[1, GC]], base=0, channel_multiplier=0).then_inc(c_const, 1)
            iota(iota_lo[:], [[1, P], [0, GROUPS * CHUNKS]], base=0, channel_multiplier=0).then_inc(c_const, 1)
            iota(keybase[:], [[GC, STILES * P], [0, CHUNKS]], base=0, channel_multiplier=0).then_inc(c_const, 1)
            for b in range(2):
                pool.sem_inc(c_countsfree[b], 1)

            def store(t, b, turn):
                pool.wait_ge(c_evac, t * GROUPS + (BANKS + GROUPS))
                pool.dma_start(d["adj"][bass.ds(t, 1)].rearrange("o p c -> (o p) c"),
                               counts[b][:].rearrange("p a b -> p (a b)").bitcast(I32)).then_inc(c_stored[b], 16)
                pool.wait_ge(c_stored[b], turn * 16)
                pool.sem_inc(c_countsfree[b], 1)
            with pool.Fori(0, TILES // 2) as i:
                store(i * 2, 0, i + 1)
                store(i * 2 + 1, 1, i + 1)
            store(TILES - 1, 0, TILES // 2 + 1)

        @block.vector
        def _(dve):
            dve.wait_ge(c_const, 3)
            for r in range(STILES):
                dve.wait_ge(c_turned, r + 1)
                here = slice(r * P, (r + 1) * P)
                nc.vector.tensor_copy(lo_all[:, here, :], pc[2 * (r % 2)][:, 0:GE].rearrange("p (c g) -> p g c", g=P))
                nc.vector.tensor_tensor(key_all[:, here, :], pc[2 * (r % 2) + 1][:, 0:GE].rearrange("p (c g) -> p g c", g=P),
                                        keybase[:, here, :], ALU.subtract).then_inc(c_taken, 1)
            dve.wait_ge(c_taken, STILES)
            nc.vector.tensor_scalar(late[:], key_all[:, :, CHUNKS - 1], -(GC - 1) / 2.0, None, ALU.add)\
              .then_inc(c_late, 1)
            dve.wait_ge(c_late, 1)
            nc.vector.tensor_tensor(late[:], late[:], late[:], ALU.mult).then_inc(c_late, 1)
            dve.wait_ge(c_late, 2)
            nc.vector.tensor_scalar(late[:], late[:], (GC / 2.0) ** 2, 0.0, ALU.is_lt, ALU.add,
                                    accum_out=missed[:]).then_inc(c_late, 1)
            dve.wait_ge(c_late, 3)
            nc.vector.scalar_tensor_tensor(keep["uncovered"][:], missed[:], ident[:, P - 1:P], keep["uncovered"][:],
                                           ALU.mult, ALU.add).then_inc(c_late, 1)
            dve.wait_ge(c_late, 4)

            def onehots(t, b):
                nc.vector.tensor_copy(lo[:], lo_all[:, bass.ds(t * GROUPS, GROUPS), :].rearrange("p g c -> p (g c)"))\
                  .then_inc(c_keys, 1)
                nc.vector.tensor_copy(key[:], key_all[:, bass.ds(t * GROUPS, GROUPS), :]).then_inc(c_keys, 1)
                dve.wait_ge(c_keys, t * 2 + 2)
                nc.vector.tensor_tensor(hot_lo[b][:], iota_lo[:],
                                        lo[:].unsqueeze(1).to_broadcast([P, P, GROUPS * CHUNKS]), ALU.is_equal)
                for g in range(GROUPS):
                    dve.wait_ge(c_group, t * GROUPS + (g + 1))
                    for c in range(CHUNKS):
                        last = nc.vector.tensor_scalar(hot_key[:, g % ONEHOTS, c, :], iota_key[:], key[:, g, c:c + 1],
                                                       None, ALU.is_equal)
                    last.then_inc(c_hot, 1)
                dve.wait_ge(c_hot, t * GROUPS + GROUPS)
            with dve.Fori(0, TILES // 2) as i:
                onehots(i * 2, 0)
                onehots(i * 2 + 1, 1)
            onehots(TILES - 1, 0)

        @block.tensor
        def _(pe):
            for r in range(STILES):
                if r >= 2:
                    pe.wait_ge(c_taken, r - 1)
                for c in range(CHUNKS):
                    for i in range(2):
                        last = nc.tensor.transpose(pc[2 * (r % 2) + i][:, c * P:(c + 1) * P],
                                                   gathered[:, r, c * P:(c + 1) * P, i], ident[:])
                last.then_inc(c_turned, 1)
            pe.wait_ge(c_taken, STILES)
            pe.sem_inc(c_group, ONEHOTS)

            def multiply(t, b):
                for g in range(GROUPS):
                    pe.wait_ge(c_hot, t * GROUPS + (g + 1))
                    pe.wait_ge(c_evac, t * GROUPS + (g + 1))
                    for c in range(CHUNKS):
                        last = nc.tensor.matmul(pc[g % BANKS][:, 0:GC], hot_lo[b][:, :, g * CHUNKS + c],
                                                hot_key[:, g % ONEHOTS, c, :], start=(c == 0), stop=(c == CHUNKS - 1))
                    last.then_inc(c_group, 1)
            with pe.Fori(0, TILES // 2) as i:
                multiply(i * 2, 0)
                multiply(i * 2 + 1, 1)
            multiply(TILES - 1, 0)

        @block.scalar
        def _(act):
            act.sem_inc(c_evac, BANKS)

            def evacuate(t, b, turn):
                act.wait_ge(c_countsfree[b], turn)
                for g in range(GROUPS):
                    act.wait_ge(c_group, t * GROUPS + (ONEHOTS + g + 1))
                    act.sem_inc(keep["turn"], 1)
                    nc.scalar.activation(counts[b][:, :, g * GN:(g + 1) * GN].rearrange("p h n -> p n h"),
                                         pc[g % BANKS][:, 0:GC].rearrange("p (n h) -> p n h", n=GN),
                                         ACT.Copy, scale=1.0 / CSCALE, saturate=False).then_inc(c_evac, 1)
            with act.Fori(0, TILES // 2) as i:
                evacuate(i * 2, 0, i + 1)
                evacuate(i * 2 + 1, 1, i + 1)
            evacuate(TILES - 1, 0, TILES // 2 + 1)


def aggregate(pe, nc, keep, s, part, q, ph, pl, yh, yl, cols, t):
    pe.wait_ge(s["part"][q], t * 16 + 16)
    pe.wait_ge(s["bankfree"][q], t + 1)
    pe.sem_inc(keep["turn"], 1)
    h0, h1 = SPLIT[q], SPLIT[q + 1]
    for h in range(h0, h1):
        nc.tensor.matmul(ph[q][:, 0:cols], part[q][:, h - h0, :], yh[:, h, 0:cols], start=(h == h0), stop=(h == h1 - 1))
        last = nc.tensor.matmul(pl[q][:, 0:D], part[q][:, h - h0, :], yl[:, h, :], start=(h == h0), stop=(h == h1 - 1))
    last.then_inc(s["summed"][q], 1)


def load_parts(sp, s, d, part, t, seen=None):
    for q in range(2):
        sp.wait_ge(s["summed"][q], t + 1)
        if seen:
            sp.wait_ge(seen[q], t + 1)
        sp.dma_start(part[q][:].rearrange("p h n -> p (h n)").bitcast(I32),
                     d["adj"][bass.ds(t, 1), :, SPLIT[q] * P // 4:SPLIT[q + 1] * P // 4].rearrange("o p c -> (o p) c"))\
          .then_inc(s["part"][q], 16)


def aggregation_semaphores(sem, p):
    pair = lambda n: [sem(f"{p}_{n}{q}") for q in range(2)]
    return dict(part=pair("part"), summed=pair("summed"), bankfree=pair("bankfree"),
                comb=sem(f"{p}_comb"))


def combine(dve, nc, s, ph, pl, first, total, cols, t):
    dve.wait_ge(s["summed"][0], t + 2)
    nc.vector.tensor_copy(first[:, 0:cols], ph[0][:, 0:cols]).then_inc(s["comb"], 1)
    dve.wait_ge(s["comb"], t * 4 + 1)
    nc.vector.scalar_tensor_tensor(first[:, 0:D], pl[0][:, 0:D], 1.0 / LO_SCALE, first[:, 0:D], ALU.mult, ALU.add)\
      .then_inc(s["comb"], 1)
    dve.wait_ge(s["comb"], t * 4 + 2)
    dve.sem_inc(s["bankfree"][0], 1)
    dve.wait_ge(s["summed"][1], t + 2)
    nc.vector.tensor_tensor(total[:, 0:cols], ph[1][:, 0:cols], first[:, 0:cols], ALU.add).then_inc(s["comb"], 1)
    dve.wait_ge(s["comb"], t * 4 + 3)
    nc.vector.scalar_tensor_tensor(total[:, 0:D], pl[1][:, 0:D], 1.0 / LO_SCALE, total[:, 0:D], ALU.mult, ALU.add)\
      .then_inc(s["comb"], 1)
    dve.wait_ge(s["comb"], t * 4 + 4)
    dve.sem_inc(s["bankfree"][1], 1)


def layer1_phase(nc, sem, mem, d, keep):
    def sb(name, shape, dt):
        return mem.enter_context(nc.sbuf_tensor(name, shape, dt))

    ident, yh, yl, y2h, y2l, w1r, w2lr, b1, b2, rdeg, unscale = (keep[k] for k in (
        "ident", "yh", "yl", "y2h", "y2l", "w1r", "w2lr", "b1", "b2", "rdeg", "unscale"))
    part = [keep["part0"], keep["part1"]]
    first, total = sb("first", [P, D + 1], F32), sb("total", [P, D + 1], F32)
    acc_in, acc_out = sb("acc_in", [P, D], F32), sb("acc_out", [P, D], F32)
    xt = sb("xt", [P, KD, P], F32)
    rsum = sb("rsum", [P, 2], F32)
    h0 = sb("h0", [P, D], F32)
    h = sb("h", [P, D], F32)
    ht = sb("ht", [P, KD, P], F32)
    ps = lambda n: mem.enter_context(nc.psum_tensor(n, [P, 512], F32))
    ph, pl = [ps("ph0"), ps("ph1")], [ps("pl0"), ps("pl1")]
    pr, ptr, py2 = ps("pr"), ps("ptr"), ps("py2")

    seen = sb("seen", [P, TILES * P // 4], I32)
    large = sb("large", [P, TILES * P // 4], F32)
    faults = sb("faults", [P, 2], F32)
    ones = sb("g_ones", [P, 1], F32)
    g_seen = [sem("g_seen0"), sem("g_seen1")]
    g_fault, g_sum = sem("g_fault"), sem("g_sum")
    s = aggregation_semaphores(sem, "g")
    g_xt, g_root, g_acc, g_accfree = sem("g_xt"), sem("g_root"), sem("g_acc"), sem("g_accfree")
    g_h, g_tr, g_ht, g_y2, g_y2h = sem("g_h"), sem("g_tr"), sem("g_ht"), sem("g_y2"), sem("g_y2h")
    g_step = sem("g_step")
    g_y2free, g_out, g_outfree, g_stored = sem("g_y2free"), sem("g_out"), sem("g_outfree"), sem("g_stored", pool_dma=True)
    g_pre, g_tail = sem("g_pre"), sem("g_tail")

    with nc.Block() as block:
        @block.sync
        def _(sp):
            def load_tile(t):
                load_parts(sp, s, d, part, t, g_seen)
                sp.wait_ge(g_root, t + 1)
                sp.dma_start(xt[:], d["xnt"][bass.ds(t, 1)].rearrange("o p k c -> (o p) k c")).then_inc(g_xt, 16)

            def load_acc(t):
                sp.wait_ge(g_accfree, t + 1)
                sp.dma_start(acc_in[:], d["acc"][bass.ds(t * P, P), :]).then_inc(g_acc, 16)
            load_tile(0)
            with sp.Fori(1, TILES) as t:
                load_tile(t)
                load_acc(t - 1)
            load_acc(TILES - 1)

        @block.gpsimd
        def _(pool):
            pool.sem_inc(g_outfree, 1)
            with pool.Fori(0, TILES) as t:
                pool.wait_ge(g_out, t + 1)
                pool.dma_start(d["acc"][bass.ds(t * P, P), :], acc_out[:]).then_inc(g_stored, 16)
                pool.wait_ge(g_stored, t * 16 + 16)
                pool.sem_inc(g_outfree, 1)

        @block.tensor
        def _(pe):
            for q in range(2):
                pe.sem_inc(s["summed"][q], 1)
            pe.sem_inc(g_root, 1)

            def tail_transpose(t):
                pe.wait_ge(g_h, t + 1)
                for k in range(KD):
                    last = nc.tensor.transpose(ptr[:, k * P:(k + 1) * P], h[:, k * P:(k + 1) * P], ident[:])
                last.then_inc(g_tr, 1)

            def tail_project(t):
                pe.wait_ge(g_ht, t + 1)
                pe.wait_ge(g_y2free, t + 1)
                for k in range(KD):
                    last = nc.tensor.matmul(py2[:], ht[:, k, :], w2lr[:, k, :], start=(k == 0), stop=(k == KD - 1))
                last.then_inc(g_y2, 1)

            def root(t):
                pe.wait_ge(g_xt, t * 16 + 16)
                for k in range(KD):
                    last = nc.tensor.matmul(pr[:, 0:D], xt[:, k, :], w1r[:, k, :], start=(k == 0), stop=(k == KD - 1))
                last.then_inc(g_root, 1)

            def sums(t, q):
                aggregate(pe, nc, keep, s, part, q, ph, pl, yh, yl, D + 2, t)
            sums(0, 0)
            root(0)
            sums(0, 1)
            with pe.Fori(1, TILES) as t:
                sums(t, 0)
                tail_transpose(t - 1)
                root(t)
                sums(t, 1)
                tail_project(t - 1)
            tail_transpose(TILES - 1)
            tail_project(TILES - 1)
            pe.wait_ge(g_fault, 5)
            nc.tensor.matmul(pr[0:1, 0:1], faults[:, 1:2], ones[:], start=True, stop=True).then_inc(g_sum, 1)

        @block.scalar
        def _(act):
            with act.Fori(0, TILES) as t:
                act.wait_ge(g_tr, t + 1)
                nc.scalar.activation(ht[:].rearrange("p k c -> p (k c)"), ptr[:, 0:D], ACT.Copy).then_inc(g_ht, 1)
                act.wait_ge(g_y2, t + 1)
                nc.scalar.activation(y2h[:, bass.ds(t, 1), :].rearrange("p o f -> p (o f)"), py2[:, 0:D],
                                     ACT.Copy, scale=1.0 / LO_SCALE).then_inc(g_y2h, 1)

        @block.vector
        def _(dve):
            for q in range(2):
                dve.sem_inc(s["bankfree"][q], 1)
            dve.sem_inc(g_accfree, 1)
            dve.sem_inc(g_y2free, 1)
            nc.vector.memset(ones[:], 1.0).then_inc(g_fault, 1)
            nc.vector.memset(seen[:], 0).then_inc(g_seen[0], 1)
            dve.sem_inc(g_seen[1], 1)

            def look(t, q):
                dve.wait_ge(s["part"][q], t * 16 + 16)
                dve.wait_ge(g_seen[q], t + 1)
                here = seen[:, SPLIT[q] * P // 4:SPLIT[q + 1] * P // 4]
                nc.vector.tensor_tensor(here, here, part[q][:].rearrange("p h n -> p (h n)").bitcast(I32),
                                        ALU.bitwise_or).then_inc(g_seen[q], 1)

            def head(t):
                look(t, 0)
                look(t, 1)
                combine(dve, nc, s, ph, pl, first, total, D + 1, t)
                nc.vector.tensor_scalar(rsum[:, 0:1], total[:, D:D + 1], CSCALE, 1.0, ALU.mult, ALU.max).then_inc(g_step, 1)
                dve.wait_ge(g_step, t * 5 + 1)
                nc.vector.reciprocal(rsum[:, 1:2], rsum[:, 0:1]).then_inc(g_step, 1)
                dve.wait_ge(g_step, t * 5 + 2)
                nc.vector.tensor_scalar(rsum[:, 0:1], rsum[:, 1:2], unscale[:, 0:1], CSCALE, ALU.mult, ALU.mult).then_inc(g_step, 1)
                nc.vector.tensor_scalar(rdeg[:, bass.ds(t, 1)], rsum[:, 1:2], unscale[:, 1:2], CSCALE, ALU.mult, ALU.mult)\
                  .then_inc(g_step, 1)
                dve.wait_ge(g_step, t * 5 + 4)
                dve.wait_ge(g_root, t + 2)
                nc.vector.scalar_tensor_tensor(h0[:], total[:, 0:D], rsum[:, 0:1], b1[:], ALU.mult, ALU.add)\
                  .then_inc(g_step, 1)
                dve.wait_ge(g_step, t * 5 + 5)
                nc.vector.tensor_tensor(h0[:], pr[:, 0:D], h0[:], ALU.add).then_inc(g_pre, 1)
                dve.wait_ge(g_pre, t + 1)
                nc.vector.tensor_scalar(h[:], h0[:], 0.0, None, ALU.max).then_inc(g_h, 1)

            def tail(t):
                dve.wait_ge(g_y2h, t + 1)
                nc.vector.scalar_tensor_tensor(y2l[:, bass.ds(t, 1), :].rearrange("p o f -> p (o f)"),
                                               y2h[:, bass.ds(t, 1), :].rearrange("p o f -> p (o f)"),
                                               -LO_SCALE, py2[:, 0:D], ALU.mult, ALU.add).then_inc(g_tail, 1)
                dve.wait_ge(g_acc, t * 16 + 16)
                dve.wait_ge(g_outfree, t + 1)
                nc.vector.tensor_tensor(acc_out[:], py2[:, D:2 * D], acc_in[:], ALU.add).then_inc(g_tail, 1)
                dve.wait_ge(g_tail, t * 2 + 2)
                dve.sem_inc(g_accfree, 1)
                dve.sem_inc(g_y2free, 1)
                nc.vector.tensor_tensor(acc_out[:], acc_out[:], b2[:], ALU.add).then_inc(g_out, 1)
                dve.wait_ge(g_out, t + 1)
            head(0)
            with dve.Fori(1, TILES) as t:
                head(t)
                tail(t - 1)
            tail(TILES - 1)
            dve.wait_ge(g_seen[0], TILES + 1)
            dve.wait_ge(g_seen[1], TILES + 1)
            nc.vector.tensor_scalar(seen[:], seen[:], 0x40404040, None, ALU.bitwise_and).then_inc(g_fault, 1)
            dve.wait_ge(g_fault, 2)
            nc.vector.tensor_copy(large[:], seen[:]).then_inc(g_fault, 1)
            dve.wait_ge(g_fault, 3)
            nc.vector.tensor_scalar(large[:], large[:], 0.0, 0.0, ALU.is_gt, ALU.add,
                                    accum_out=faults[:, 0:1]).then_inc(g_fault, 1)
            dve.wait_ge(g_fault, 4)
            nc.vector.tensor_tensor(faults[:, 1:2], faults[:, 0:1], keep["uncovered"][:], ALU.add).then_inc(g_fault, 1)
            dve.wait_ge(g_sum, 1)
            nc.vector.tensor_scalar(faults[0:1, 0:1], pr[0:1, 0:1], 1.0, None, ALU.min).then_inc(g_fault, 1)
            dve.wait_ge(g_fault, 6)
            nc.vector.tensor_copy(keep["flag"][:], faults[0:1, 0:1]).then_inc(g_fault, 1)
            dve.wait_ge(g_fault, 7)


def layer2_phase(nc, sem, mem, d, keep):
    y2h, y2l, rdeg = keep["y2h"], keep["y2l"], keep["rdeg"]
    part = [keep["part0"], keep["part1"]]
    first, total, acc_in, acc_out = (mem.enter_context(nc.sbuf_tensor(f"h_{n}", [P, D], F32)) for n in (
        "first", "total", "acc_in", "acc_out"))
    ph, pl = ([mem.enter_context(nc.psum_tensor(f"h_{n}{q}", [P, 512], F32)) for q in range(2)] for n in ("ph", "pl"))
    s = aggregation_semaphores(sem, "h")
    h_acc, h_accfree, h_out, h_outfree = (sem(f"h_{k}") for k in ("acc", "accfree", "out", "outfree"))
    h_stored = sem("h_stored", pool_dma=True)

    with nc.Block() as block:
        @block.sync
        def _(sp):
            with sp.Fori(0, TILES) as t:
                load_parts(sp, s, d, part, t)
                sp.wait_ge(h_accfree, t + 1)
                sp.dma_start(acc_in[:], d["acc"][bass.ds(t * P, P), :]).then_inc(h_acc, 16)

        @block.gpsimd
        def _(pool):
            pool.sem_inc(h_outfree, 1)
            with pool.Fori(0, TILES) as t:
                pool.wait_ge(h_out, t + 1)
                pool.dma_start(d["acc"][bass.ds(t * P, P), :], acc_out[:]).then_inc(h_stored, 16)
                pool.wait_ge(h_stored, t * 16 + 16)
                pool.sem_inc(h_outfree, 1)

        @block.tensor
        def _(pe):
            for q in range(2):
                pe.sem_inc(s["summed"][q], 1)
            with pe.Fori(0, TILES) as t:
                for q in range(2):
                    aggregate(pe, nc, keep, s, part, q, ph, pl, y2h, y2l, D, t)

        @block.vector
        def _(dve):
            for q in range(2):
                dve.sem_inc(s["bankfree"][q], 1)
            dve.sem_inc(h_accfree, 1)
            with dve.Fori(0, TILES) as t:
                combine(dve, nc, s, ph, pl, first, total, D, t)
                dve.wait_ge(h_acc, t * 16 + 16)
                dve.wait_ge(h_outfree, t + 1)
                nc.vector.scalar_tensor_tensor(acc_out[:], total[:, 0:D], rdeg[:, bass.ds(t, 1)], acc_in[:],
                                               ALU.mult, ALU.add).then_inc(h_out, 1)
                dve.wait_ge(h_out, t + 1)
                dve.sem_inc(h_accfree, 1)

        @block.scalar
        def _(act):
            pass


def general_phase(nc, sem, mem, d, t_in, keep):
    def sb(name, shape, dt=F32):
        return mem.enter_context(nc.sbuf_tensor(name, shape, dt))

    ident = keep["ident"]
    src_i = sb("x_src", [EP, ELEN], I32)
    dst_i = sb("x_dst", [EP, ELEN], I32)
    dst_f = sb("x_dstf", [EP, ELEN])
    tbase = sb("x_tbase", [EP, TILES])
    iota_t = sb("x_iota", [EP, P])
    rel = sb("x_rel", [EP, TILES])
    col = sb("x_col", [EP, 1], I32)
    feat = sb("x_feat", [EP, D + 1])
    hot = sb("x_hot", [EP, SUP, P])
    agg = sb("x_agg", [P, TILES, D + 1])
    wl, wr = sb("x_wl", [P, 2, KD, D]), sb("x_wr", [P, 2, KD, D])
    bias = sb("x_bias", [P, 2, D])
    deg = sb("x_deg", [P, TILES])
    mean, own, turned = sb("x_mean", [P, D]), sb("x_own", [P, D]), sb("x_turned", [P, 2 * KD, P])
    xin, base = sb("x_in", [P, D]), sb("x_base", [P, D])
    res = sb("x_res", [P, D])
    bank = [mem.enter_context(nc.psum_tensor(f"x_bank{i}", [P, 512], F32)) for i in range(SUP)]

    x_const, x_load = sem("x_const"), sem("x_load")
    x_in, x_back, x_rows, x_rowst = sem("x_in"), sem("x_back"), sem("x_rows"), sem("x_rowst")
    x_col, x_hot, x_prod, x_sum = ([sem(f"x_{n}{i}") for i in range(2)] for n in ("col", "hot", "prod", "sum"))
    x_gather = [sem(f"x_gather{i}", pool_dma=True) for i in range(2)]
    x_mean, x_tile, x_turn, x_turned, x_out, x_res, x_stored = ([sem(f"x_{n}{i}") for i in range(2)] for n in (
        "mean", "tile", "turn", "turned", "out", "res", "stored"))
    kb = lambda w: w.rearrange("(k p) n -> p k n", p=P)
    rows_of = lambda table, t: table[bass.ds(t * P, P), :]
    tables = [d["feat1"], d["feat2"]]
    results = [d["feat2"], d["acc"]]

    with nc.Block() as block:
        @block.sync
        def _(sp):
            with sp.If(sp.value_load(keep["flag"][0:1, 0:1], min_val=0, max_val=1) > 0):
                sp.dma_start(src_i[:], t_in["src"].rearrange("(p n) -> p n", p=EP)).then_inc(x_load, 16)
                sp.dma_start(dst_i[:], t_in["dst"].rearrange("(p n) -> p n", p=EP)).then_inc(x_load, 16)
                for i, n in enumerate(("1", "2")):
                    sp.dma_start(wl[:, i], kb(t_in[f"gnn_W{n}_l"])).then_inc(x_load, 16)
                    sp.dma_start(wr[:, i], kb(t_in[f"gnn_W{n}_r"])).then_inc(x_load, 16)
                    sp.dma_start(bias[:, i], t_in[f"gnn_b{n}"].unsqueeze(0).to_broadcast([P, D])).then_inc(x_load, 16)
                with sp.Fori(0, TILES) as t:
                    sp.dma_start(turned[:, 0:KD, :], d["xnt"][bass.ds(t, 1)].rearrange("o p k c -> (o p) k c"))\
                      .then_inc(x_in, 16)
                    sp.wait_ge(x_rows, t + 1)
                    sp.sem_inc(keep["turn"], 1)
                    sp.dma_start(rows_of(d["feat1"], t), own[:]).then_inc(x_rowst, 16)
                    sp.wait_ge(x_rowst, t * 16 + 16)
                    sp.sem_inc(keep["turn"], 1)
                for i in range(2):
                    with sp.Fori(0, TILES) as t:
                        sp.wait_ge(x_mean[i], t + 1)
                        sp.sem_inc(keep["turn"], 1)
                        sp.dma_start(own[:], rows_of(tables[i], t)).then_inc(x_tile[i], 16)
                        sp.dma_start(base[:], rows_of(d["feat1"], t)).then_inc(x_tile[i], 16)
                        sp.dma_start(xin[:], rows_of(t_in["x"], t)).then_inc(x_tile[i], 16)
                        sp.wait_ge(x_res[i], t * 3 + 3)
                        sp.sem_inc(keep["turn"], 1)
                        sp.dma_start(rows_of(results[i], t), res[:]).then_inc(x_stored[i], 16)
                        sp.wait_ge(x_stored[i], t * 16 + 16)
                        sp.sem_inc(keep["turn"], 1)

        @block.gpsimd
        def _(pool):
            with pool.If(pool.value_load(keep["flag"][0:1, 0:1], min_val=0, max_val=1) > 0):
                nc.gpsimd.iota(tbase[:], [[-P, TILES]], base=0, channel_multiplier=0,
                               allow_small_or_imprecise_dtypes=True).then_inc(x_const, 1)
                nc.gpsimd.iota(iota_t[:], [[1, P]], base=0, channel_multiplier=0,
                               allow_small_or_imprecise_dtypes=True).then_inc(x_const, 1)
                nc.gpsimd.memset(feat[:, D:D + 1], 1.0).then_inc(x_const, 1)
                pool.wait_ge(x_const, 3)
                pool.wait_ge(x_rowst, 16 * TILES)
                for i in range(2):
                    if i:
                        pool.wait_ge(x_stored[0], 16 * TILES)
                    with pool.Fori(0, ELEN) as c:
                        pool.wait_ge(x_col[i], c + 1)
                        pool.sem_inc(keep["turn"], 1)
                        pool.indirect_dma_start(feat[:, 0:D], None, tables[i],
                                                bass.IndirectOffsetOnAxis(ap=col[:, 0:1], axis=0)).then_inc(x_gather[i], 16)

        @block.tensor
        def _(pe):
            with pe.If(pe.value_load(keep["flag"][0:1, 0:1], min_val=0, max_val=1) > 0):
                with pe.Fori(0, TILES) as t:
                    pe.wait_ge(x_in, t * 16 + 16)
                    for k in range(KD):
                        last = nc.tensor.transpose(bank[0][:, k * P:(k + 1) * P], turned[:, k, :], ident[:])
                    last.then_inc(x_back, 1)
                for i in range(2):
                    with pe.Fori(0, ELEN) as c:
                        pe.wait_ge(x_gather[i], c * 16 + 16)
                        for b in range(SUPERS):
                            pe.wait_ge(x_hot[i], c * SUPERS + (b + 1))
                            for j in range(SUP):
                                last = nc.tensor.matmul(bank[j][:, 0:D + 1], hot[:, j, :], feat[:], start=True, stop=True)
                            last.then_inc(x_prod[i], 1)
                    with pe.Fori(0, TILES) as t:
                        pe.wait_ge(x_mean[i], t + 1)
                        pe.wait_ge(x_tile[i], t * 48 + 48)
                        for k in range(KD):
                            nc.tensor.transpose(bank[0][:, k * P:(k + 1) * P], mean[:, k * P:(k + 1) * P], ident[:])
                            last = nc.tensor.transpose(bank[0][:, (KD + k) * P:(KD + k + 1) * P],
                                                       own[:, k * P:(k + 1) * P], ident[:])
                        last.then_inc(x_turn[i], 1)
                        pe.wait_ge(x_turned[i], t + 1)
                        for k in range(2 * KD):
                            w = wl if k < KD else wr
                            last = nc.tensor.matmul(bank[1][:, 0:D], turned[:, k, :], w[:, i, k % KD, :],
                                                    start=(k == 0), stop=(k == 2 * KD - 1))
                        last.then_inc(x_out[i], 1)

        @block.scalar
        def _(act):
            pass

        @block.vector
        def _(dve):
            with dve.If(dve.value_load(keep["flag"][0:1, 0:1], min_val=0, max_val=1) > 0):
                with dve.Fori(0, TILES) as t:
                    dve.wait_ge(x_back, t + 1)
                    nc.vector.tensor_copy(own[:], bank[0][:, 0:D]).then_inc(x_rows, 1)
                dve.wait_ge(x_rowst, 16 * TILES)
                dve.wait_ge(x_const, 3)
                dve.wait_ge(x_load, 16 * 8)
                nc.vector.tensor_copy(dst_f[:], dst_i[:]).then_inc(x_const, 1)
                for i in range(2):
                    nc.vector.memset(agg[:], 0.0).then_inc(x_const, 1)
                    dve.wait_ge(x_const, 5 + 3 * i)
                    with dve.Fori(0, ELEN) as c:
                        nc.vector.tensor_copy(col[:], src_i[:, bass.ds(c, 1)]).then_inc(x_col[i], 1)
                        nc.vector.tensor_scalar(rel[:], tbase[:], dst_f[:, bass.ds(c, 1)], None, ALU.add)\
                          .then_inc(x_sum[i], 1)
                        dve.wait_ge(x_sum[i], c * (SUPERS + 1) + 1)
                        for b in range(SUPERS):
                            for j in range(SUP):
                                last = nc.vector.tensor_scalar(hot[:, j, :], iota_t[:], rel[:, b * SUP + j:b * SUP + j + 1],
                                                               None, ALU.is_equal)
                            last.then_inc(x_hot[i], 1)
                            dve.wait_ge(x_prod[i], c * SUPERS + (b + 1))
                            for j in range(SUP):
                                last = nc.vector.tensor_tensor(agg[:, b * SUP + j, :], bank[j][:, 0:D + 1],
                                                               agg[:, b * SUP + j, :], ALU.add)
                            last.then_inc(x_sum[i], 1)
                            dve.wait_ge(x_sum[i], c * (SUPERS + 1) + (b + 2))
                        dve.wait_ge(x_col[i], c + 1)
                    nc.vector.tensor_scalar(deg[:], agg[:, :, D], 1.0, None, ALU.max).then_inc(x_const, 1)
                    dve.wait_ge(x_const, 6 + 3 * i)
                    nc.vector.reciprocal(deg[:], deg[:]).then_inc(x_const, 1)
                    dve.wait_ge(x_const, 7 + 3 * i)
                    with dve.Fori(0, TILES) as t:
                        nc.vector.tensor_scalar(mean[:], agg[:, bass.ds(t, 1), 0:D].rearrange("p o f -> p (o f)"),
                                                deg[:, bass.ds(t, 1)], None, ALU.mult).then_inc(x_mean[i], 1)
                        dve.wait_ge(x_turn[i], t + 1)
                        nc.vector.tensor_copy(turned[:].rearrange("p k c -> p (k c)"), bank[0][:]).then_inc(x_turned[i], 1)
                        dve.wait_ge(x_out[i], t + 1)
                        nc.vector.tensor_tensor(res[:], bank[1][:, 0:D], bias[:, i, :], ALU.add).then_inc(x_res[i], 1)
                        dve.wait_ge(x_res[i], t * 3 + 1)
                        if i == 0:
                            nc.vector.tensor_scalar(res[:], res[:], 0.0, None, ALU.max).then_inc(x_res[i], 2)
                        else:
                            nc.vector.tensor_tensor(res[:], res[:], xin[:], ALU.add).then_inc(x_res[i], 1)
                            dve.wait_ge(x_res[i], t * 3 + 2)
                            nc.vector.tensor_tensor(res[:], res[:], base[:], ALU.add).then_inc(x_res[i], 1)
                        dve.wait_ge(x_stored[i], t * 16 + 16)


def mix_phase(nc, sem, mem, d, t_in, keep, out):
    def sb(name, shape, dt=F32):
        return mem.enter_context(nc.sbuf_tensor(name, shape, dt))

    ident, eps, kvacc = keep["ident"], keep["eps"], keep["kvacc"]
    NV = 4 * KD
    wq, wm = sb("wq", [P, KD, D]), sb("wm", [P, KD, D])
    w1, w2 = sb("w1", [P, 2 * KD, 2 * D]), sb("w2", [P, 2 * KD, D])
    we1, we2, be1, be2 = (keep[k] for k in ("we1", "we2", "be1", "be2"))
    wr = sb("wr", [P, KD, EXPERTS])
    g2, b2 = sb("mix_g2", [P, D]), sb("mix_b2", [P, D])
    br = sb("br", [P, EXPERTS])
    rows = sb("vec_rows", [NV, P])
    cols, betab = keep["cols"], keep["betab"]
    G1, B1, GAMMA, BETA = VEC
    ones = sb("ones2", [P, P])
    bdkv, bdks = sb("bdkv", [P, KD, P]), sb("bdks", [P, KD, P])
    c1 = sb("c1", [P, 2 * D // P])
    lb = sb("lb", [P, EXPERTS])
    iota8 = sb("iota8", [P, SUP, EXPERTS])
    xq, xh = sb("xq", [P, KD, R]), sb("xh", [P, KD, R])
    qt, msgt, m1t = (sb(n, [P, KD, R]) for n in ("qt", "msgt", "m1t"))
    x2t = qt
    qmin, qexp = sb("qmin", [P, 2, NW]), sb("qexp", [P, 2, NW])
    den, rden = qmin, qexp
    nrm1 = sb("nrm1", [P, SUP, D])
    nrm = sb("nrm", [P, SUP, D])
    h1t = sb("h1t", [P, 2 * D // P, R])
    filler = h1t[:].rearrange("p m r -> p (m r)")[:, 0:LISTS // P * 4].rearrange("p (n c) -> p n c", c=4)
    acc, x2 = (sb(n, [P, SUP, D]) for n in ("m_acc", "x2"))
    stats, mv = sb("m_stats", [P, SUP, 6]), sb("m_mv", [P, SUP, 2])
    std, rstd, rstd2, var2 = (sb(n, [P, SUP]) for n in ("m_std", "m_rstd", "m_rstd2", "m_var2"))
    lg, top = sb("lg", [P, SUP, EXPERTS]), sb("top", [P, SUP, 8])
    idx, idxf = sb("idx", [P, SUP, 8], U32), sb("idxf", [P, SUP, 8])
    gap, wgt = sb("gap", [P, SUP]), sb("wgt", [P, SUP, 2])
    pick = sb("pick", [P, 2 * SUP * EXPERTS])
    picked = pick[:].rearrange("p (i j e) -> p i j e", i=2, j=SUP)
    before, everyone = sb("before", [P, P]), sb("everyone", [P, P])
    chosen = sb("chosen", [P, CHOICES, EXPERTS])
    upto = [sb(f"upto{i}", [P, CHOICES, EXPERTS]) for i in range(2)]
    place = sb("place", [P, CHOICES, EXPERTS])
    place_f, place_i = sb("place_f", [P, CHOICES]), sb("place_i", [P, CHOICES], I32)
    entry = sb("entry", [P, CHOICES, 4])
    node = sb("node", [P, CHOICES])
    zeros = sb("zeros", [P, D])
    ends = keep["ends"]
    bank = [mem.enter_context(nc.psum_tensor(f"bank{i}", [P, 512], F32)) for i in range(8)]

    m_w, m_row = sem("m_w"), sem("m_row")
    m_const, m_cols, m_colst, m_fold, m_scaled, m_bd, m_setup = (sem(f"m_{k}") for k in (
        "const", "cols", "colst", "fold", "scaled", "bd", "setup"))
    m_xq, m_xh = sem("m_xq"), sem("m_xh")
    m_accin, m_accb, m_accfree = sem("m_accin"), sem("m_accb"), sem("m_accfree")
    m_q, m_qmin, m_qexp, m_qt = sem("m_q"), sem("m_qmin"), sem("m_qexp"), sem("m_qt")
    m_att, m_den, m_msg = sem("m_att"), sem("m_den"), sem("m_msg")
    m_m1, m_tr1, m_m1t = sem("m_m1"), sem("m_tr1"), sem("m_m1t")
    m_h1, m_h1t, m_h2, m_x2 = sem("m_h1"), sem("m_h1t"), sem("m_h2"), sem("m_x2")
    m_tr2, m_x2t = sem("m_tr2"), sem("m_x2t")
    m_lg, m_route, m_gap, m_exp = (sem(f"m_{k}") for k in ("lg", "route", "gap", "exp"))
    m_pick, m_count, m_place, m_entry = sem("m_pick"), sem("m_count"), sem("m_place"), sem("m_entry")
    m_listfree = sem("m_listfree")
    m_counted = sem("m_counted")
    m_listed = sem("m_listed", pool_dma=True)
    m_ew, m_fill, m_filled, m_x2st, m_nrmst = (sem(f"m_{k}") for k in ("ew", "fill", "filled", "x2st", "nrmst"))
    ln = [{k: sem(f"m_ln{i}_{k}") for k in ("stats", "var", "std", "rstd", "done") + ("step",) * (i == 2)} for i in range(3)]

    kb = lambda w: w.rearrange("(k p) n -> p k n", p=P)
    acc_s = d["acc"].rearrange("(s j p) f -> s p j f", p=P, j=SUP)
    out_s = out[0:NPAD, :].rearrange("(s j p) f -> s p j f", p=P, j=SUP)
    table_s = d["table"].rearrange("(s j p) f -> s p j f", p=P, j=SUP)
    xnt_s = d["xnt"].rearrange("(s j) p k c -> s p k j c", j=SUP)
    tile_cols = lambda b, j: b[j // 2][:, (j % 2) * D:(j % 2 + 1) * D]
    row_vec = lambda v, n: v.rearrange("(k p) -> k p", p=P)

    def wait(eng, signal, value):
        if not isinstance(value, int) or value > 0:
            eng.wait_ge(signal, value)

    with nc.Block() as block:
        @block.sync
        def _(sp):
            r = 0
            for v, n in ((row_vec(t_in["mix_g1"], KD), KD), (row_vec(t_in["mix_b1"], KD), KD),
                         (row_vec(t_in["ffn_gamma"], KD), KD), (row_vec(t_in["ffn_beta"], KD), KD)):
                sp.dma_start(rows[r:r + n, :], v).then_inc(m_row, 16)
                r += n
            sp.dma_start(w1[:], kb(t_in["mix_W1"])).then_inc(m_w, 16)
            sp.dma_start(wr[:], kb(t_in["ffn_Wr"])).then_inc(m_w, 16)
            sp.dma_start(br[:], t_in["ffn_br"].unsqueeze(0).to_broadcast([P, EXPERTS])).then_inc(m_w, 16)
            sp.dma_start(wq[:], kb(t_in["mix_Wq"])).then_inc(m_w, 16)
            sp.dma_start(wm[:], kb(t_in["mix_Wm"])).then_inc(m_w, 16)
            sp.dma_start(w2[:], kb(t_in["mix_W2"])).then_inc(m_w, 16)
            sp.dma_start(g2[:], t_in["mix_g2"].unsqueeze(0).to_broadcast([P, D])).then_inc(m_w, 16)
            sp.dma_start(b2[:], t_in["mix_b2"].unsqueeze(0).to_broadcast([P, D])).then_inc(m_w, 16)

            def fetch(buf, signal, s):
                for k in range(KD):
                    sp.dma_start(buf[:, k, :].rearrange("p (j c) -> p j c", j=SUP),
                                 xnt_s[bass.ds(s, 1), :, k].rearrange("o p j c -> (o p) j c")).then_inc(signal, 16)

            def fetch_acc(s):
                wait(sp, m_accfree, s)
                sp.dma_start(acc[:], acc_s[bass.ds(s, 1)].rearrange("o p j f -> (o p) j f")).then_inc(m_accin, 16)
            fetch(xq, m_xq, 0)
            fetch(xh, m_xh, 0)
            fetch_acc(0)
            sp.wait_ge(m_fill, 2)
            sp.dma_start(d["lists"].rearrange("(p n) c -> p n c", p=P), filler).then_inc(m_filled, 16)
            sp.dma_start(out[NPAD:NPAD + P, :], zeros[:]).then_inc(m_filled, 16)
            for e in range(EXPERTS):
                sp.dma_start(we1[:, e], kb(t_in["ffn_W1"][e])).then_inc(m_ew, 16)
                sp.dma_start(we2[:, e], kb(t_in["ffn_W2"][e])).then_inc(m_ew, 16)
            sp.dma_start(be1[:], t_in["ffn_b1"].rearrange("e h -> (e h)").unsqueeze(0).to_broadcast([P, EXPERTS * HID]))\
              .then_inc(m_ew, 16)
            sp.dma_start(be2[:], t_in["ffn_b2"].rearrange("e h -> (e h)").unsqueeze(0).to_broadcast([P, EXPERTS * D]))\
              .then_inc(m_ew, 16)
            sp.wait_ge(m_filled, 32)

            sp.wait_ge(m_q, 4)
            fetch(xq, m_xq, 1)

            def step(s, first=False, more=2):
                if more > 1:
                    sp.wait_ge(m_q, (s + 1) * 4 + 4)
                    fetch(xq, m_xq, s + 2)
                if not first:
                    sp.wait_ge(m_x2, (s - 1) * 2 + 2)
                    sp.dma_start(out_s[bass.ds(s - 1, 1)].rearrange("o p j f -> (o p) j f"), x2[:]).then_inc(m_x2st, 16)
                    fetch_acc(s)
                    sp.wait_ge(ln[2]["done"], s)
                    sp.dma_start(table_s[bass.ds(s - 1, 1)].rearrange("o p j f -> (o p) j f"), nrm[:])\
                      .then_inc(m_nrmst, 16)
                if more:
                    sp.wait_ge(m_h1, s * 8 + 8)
                    fetch(xh, m_xh, s + 1)
            step(0, first=True)
            with sp.Fori(1, SUPERS - 2) as s:
                step(s)
            step(SUPERS - 2, more=1)
            step(SUPERS - 1, more=0)
            sp.wait_ge(m_x2, SUPERS * 2)
            sp.dma_start(out_s[SUPERS - 1], x2[:]).then_inc(m_x2st, 16)
            sp.wait_ge(ln[2]["done"], SUPERS)
            sp.dma_start(table_s[SUPERS - 1], nrm[:]).then_inc(m_nrmst, 16)
            sp.wait_ge(m_x2st, 16 * SUPERS)
            sp.wait_ge(m_nrmst, 16 * SUPERS)
            sp.wait_ge(m_ew, 16 * (2 * EXPERTS + 2))

        @block.gpsimd
        def _(pool):
            nc.gpsimd.memset(bdkv[:], 0.0).then_inc(m_const, 1)
            nc.gpsimd.memset(bdks[:], 0.0).then_inc(m_const, 1)
            nc.gpsimd.memset(ones[:], 1.0).then_inc(m_const, 1)
            nc.gpsimd.memset(filler, 0.0).then_inc(m_const, 1)
            nc.gpsimd.memset(zeros[:], 0.0).then_inc(m_fill, 1)
            nc.gpsimd.memset(before[:], 1.0).then_inc(m_const, 1)
            nc.gpsimd.memset(everyone[:], 1.0).then_inc(m_const, 1)
            nc.gpsimd.memset(entry[:], 0.0).then_inc(m_const, 1)
            nc.gpsimd.iota(node[:], [[0, 2], [P, SUP]], base=0, channel_multiplier=1,
                           allow_small_or_imprecise_dtypes=True).then_inc(m_const, 1)
            nc.gpsimd.iota(ends[:], [[REGION, EXPERTS]], base=0, channel_multiplier=0,
                           allow_small_or_imprecise_dtypes=True).then_inc(m_const, 1)
            nc.gpsimd.iota(iota8[:], [[0, SUP], [1, EXPERTS]], base=0, channel_multiplier=0,
                           allow_small_or_imprecise_dtypes=True).then_inc(m_const, 1)
            pool.wait_ge(m_const, 10)
            nc.gpsimd.iota(filler[:, :, 2], [[0, LISTS // P // P], [1, P]], base=NPAD, channel_multiplier=0,
                           allow_small_or_imprecise_dtypes=True).then_inc(m_fill, 1)
            nc.gpsimd.affine_select(out=before[:], in_=before[:], compare_op=ALU.is_ge, fill=0.0,
                                    base=-1, pattern=[[1, P]], channel_multiplier=-1).then_inc(m_const, 1)
            pool.wait_ge(m_w, 16 * 8)

            def add_bias(s):
                pool.wait_ge(m_accin, s * 16 + 16)
                nc.gpsimd.tensor_tensor(acc[:], acc[:], b2[:].unsqueeze(1).to_broadcast([P, SUP, D]), ALU.add)\
                  .then_inc(m_accb, 1)

            def enter(s):
                pool.wait_ge(m_entry, s * ENTRY_STEPS + ENTRY_STEPS)
                pool.wait_ge(m_filled, 32)
                pool.sem_inc(keep["turn"], 1)
                for b in range(CHOICES):
                    pool.indirect_dma_start(d["lists"], bass.IndirectOffsetOnAxis(ap=place_i[:, b:b + 1], axis=0),
                                            entry[:, b, :], None).then_inc(m_listed, 16)
                pool.wait_ge(m_listed, s * (16 * CHOICES) + 16 * CHOICES)
                pool.sem_inc(m_listfree, 1)
            add_bias(0)
            with pool.Fori(0, SUPERS - 1) as s:
                add_bias(s + 1)
                enter(s)
            enter(SUPERS - 1)
            pool.wait_ge(m_listed, 16 * CHOICES * SUPERS)

        @block.scalar
        def _(act):
            act.wait_ge(m_cols, 1)
            nc.scalar.activation(cols[:], bank[0][:, 0:NV], ACT.Copy).then_inc(m_colst, 1)

            def stdev(l, src, s, per, k):
                act.wait_ge(ln[l]["var"], s * per + (k + 1))
                nc.scalar.activation(std[:], src, ACT.Sqrt, bias=eps[:]).then_inc(ln[l]["std"], 1)
            act.wait_ge(m_filled, 32)

            def exps(s):
                for i in range(4):
                    act.wait_ge(m_qmin, s * 4 + (i + 1))
                    nc.scalar.activation(qexp[:, i % 2, :], qmin[:, i % 2, :], ACT.Exp).then_inc(m_qexp, 1)

            def copies(to, turned, done, s):
                for b in range(4):
                    k, half, w = b // 2, b % 2, (4, 3)[b % 2] * P
                    act.wait_ge(turned, s * 4 + (b + 1))
                    nc.scalar.activation(to[:, k, half * 4 * P:half * 4 * P + w], bank[4 + b][:, 0:w], ACT.Copy)\
                      .then_inc(done, 1)

            def relus(s, blocks):
                for i in blocks:
                    m, n = i // 2, i % 2
                    act.wait_ge(m_h1, s * 8 + (i + 1))
                    nc.scalar.activation(h1t[:, m, n * NW:(n + 1) * NW], bank[4 + i % 4][:, 0:NW], ACT.Relu,
                                         bias=c1[:, m:m + 1]).then_inc(m_h1t, 1)

            def stdevs_x2(s):
                stdev(2, mv[:, :, 1], s, 2, 0)
                stdev(2, var2[:], s, 2, 1)

            def route(s):
                copies(x2t, m_tr2, m_x2t, s)
                act.wait_ge(m_gap, s + 1)
                nc.scalar.activation(gap[:], gap[:], ACT.Exp).then_inc(m_exp, 1)

            def step(s, first=False, last=False):
                if not first:
                    stdev(1, mv[:, :, 1], s - 1, 1, 0)
                copies(m1t, m_tr1, m_m1t, s)
                if not last:
                    exps(s + 1)
                relus(s, (0, 1))
                if not first:
                    stdevs_x2(s - 1)
                relus(s, (2, 3, 4))
                if not last:
                    stdev(0, mv[:, :, 1], s + 1, 1, 0)
                relus(s, (5, 6, 7))
                if not first:
                    route(s - 1)
            exps(0)
            stdev(0, mv[:, :, 1], 0, 1, 0)
            step(0, first=True)
            with act.Fori(1, SUPERS - 1) as s:
                step(s)
            step(SUPERS - 1, last=True)
            stdev(1, mv[:, :, 1], SUPERS - 1, 1, 0)
            stdevs_x2(SUPERS - 1)
            route(SUPERS - 1)

        @block.tensor
        def _(pe):
            pe.wait_ge(m_row, 64)
            nc.tensor.transpose(bank[0][:, 0:NV], rows[:], ident[0:NV, 0:NV]).then_inc(m_cols, 1)
            pe.wait_ge(m_colst, 1)
            pe.wait_ge(m_bd, 1)
            pe.wait_ge(m_w, 16 * 8)
            for m in range(2 * D // P):
                for k in range(KD):
                    nc.tensor.matmul(bank[1][:, m:m + 1], w1[:, KD + k, m * P:(m + 1) * P], cols[:, B1 + k:B1 + k + 1],
                                     start=(k == 0), stop=(k == KD - 1))
            for k in range(KD):
                last = nc.tensor.matmul(bank[3][:, 0:EXPERTS], betab[:, k, :], wr[:, k, :],
                                        start=(k == 0), stop=(k == KD - 1))
            last.then_inc(m_fold, 1)
            pe.wait_ge(m_setup, 1)
            pe.wait_ge(m_const, 11)

            def queries(s, first=False):
                pe.wait_ge(m_xq, s * 32 + 32)
                for i in range(4):
                    m, n = i // 2, i % 2
                    if not first:
                        pe.wait_ge(m_m1t, (s - 1) * 4 + (i + 1))
                    for k in range(KD):
                        last = nc.tensor.matmul(bank[4 + i][:, 0:NW], wq[:, k, m * P:(m + 1) * P],
                                                xq[:, k, n * NW:(n + 1) * NW], start=(k == 0), stop=(k == KD - 1))
                    last.then_inc(m_q, 1)

            def attend(s, first=False):
                if not first:
                    wait(pe, ln[1]["done"], s - 1)
                for i in range(4):
                    m, n = i // 2, i % 2
                    pe.wait_ge(m_qt, s * 4 + (i + 1))
                    if i >= 2:
                        pe.wait_ge(m_msg, s * 4 + (i - 1))
                    nc.tensor.matmul(bank[2 * (i % 2)][:, 0:NW], bdkv[:, m, :], qt[:, m, n * NW:(n + 1) * NW],
                                     start=True, stop=True)
                    nc.tensor.matmul(bank[1 + 2 * (i % 2)][:, 0:NW], bdks[:, m, :], qt[:, m, n * NW:(n + 1) * NW],
                                     start=True, stop=True).then_inc(m_att, 1)

            def project(s):
                pe.wait_ge(m_msg, s * 4 + 4)
                for j in range(SUP):
                    for k in range(KD):
                        last = nc.tensor.matmul(tile_cols(bank[0:4], j), msgt[:, k, j * P:(j + 1) * P], wm[:, k, :],
                                                start=(k == 0), stop=(k == KD - 1))
                last.then_inc(m_m1, 1)

            def turn(src, done, s, free, value):
                for b in range(4):
                    k, half = b // 2, b % 2
                    if free:
                        pe.wait_ge(free, value + b)
                    for j in range(4 * half, min(4 * half + 4, SUP)):
                        last = nc.tensor.transpose(bank[4 + b][:, (j % 4) * P:(j % 4 + 1) * P],
                                                   src[:, j, k * P:(k + 1) * P], ident[:])
                    last.then_inc(done, 1)

            def hidden(s, blocks, last_step=False):
                for i in blocks:
                    m, n = i // 2, i % 2
                    if i == 0:
                        pe.wait_ge(m_xh, s * 32 + 32)
                        pe.wait_ge(m_m1t, s * 4 + 4)
                    if i >= 4:
                        pe.wait_ge(m_h1t, s * 8 + (i - 3))
                    elif not last_step:
                        pe.wait_ge(m_qt, (s + 1) * 4 + (i + 1))
                    for k in range(2 * KD):
                        src = xh if k < KD else m1t
                        last = nc.tensor.matmul(bank[4 + i % 4][:, 0:NW], w1[:, k, m * P:(m + 1) * P],
                                                src[:, k % KD, n * NW:(n + 1) * NW],
                                                start=(k == 0), stop=(k == 2 * KD - 1))
                    last.then_inc(m_h1, 1)

            def feed(s, last_step=False):
                pe.wait_ge(m_h1t, s * 8 + 8)
                if last_step:
                    pe.wait_ge(ln[1]["done"], s)
                else:
                    pe.wait_ge(ln[0]["done"], s + 2)
                for j in range(SUP):
                    for k in range(2 * KD):
                        last = nc.tensor.matmul(tile_cols(bank[0:4], j), h1t[:, k, j * P:(j + 1) * P], w2[:, k, :],
                                                start=(k == 0), stop=(k == 2 * KD - 1))
                last.then_inc(m_h2, 1)

            def logits(s, free):
                pe.wait_ge(ln[2]["done"], s + 1)
                turn(nrm, m_tr2, s, *free)
                pe.wait_ge(m_x2t, s * 4 + 4)
                for j in range(SUP):
                    for k in range(KD):
                        last = nc.tensor.matmul(bank[4][:, j * EXPERTS:(j + 1) * EXPERTS], x2t[:, k, j * P:(j + 1) * P],
                                                wr[:, k, :], start=(k == 0), stop=(k == KD - 1))
                last.then_inc(m_lg, 1)

            def counts(s):
                pe.wait_ge(m_pick, s + 1)
                nc.tensor.matmul(bank[5][:, 0:CHOICES * EXPERTS], before[:], pick[:], start=True, stop=True)
                nc.tensor.matmul(bank[6][:, 0:CHOICES * EXPERTS], everyone[:], pick[:], start=True, stop=True)\
                  .then_inc(m_count, 1)

            def step(s, first=False, last=False):
                pe.wait_ge(ln[0]["done"], s + 1)
                if not first:
                    wait(pe, m_counted, s - 1)
                turn(nrm1, m_tr1, s, None, 0)
                if not last:
                    queries(s + 1)
                hidden(s, (0, 1, 2), last)
                if not last:
                    attend(s + 1, first)
                hidden(s, (3, 4), last)
                if not last:
                    project(s + 1)
                hidden(s, (5, 6, 7), last)
                if not first:
                    logits(s - 1, (m_h1t, s * 8 + 5))
                feed(s, last)
                if not first:
                    counts(s - 1)
            queries(0, True)
            attend(0, True)
            project(0)
            step(0, first=True)
            with pe.Fori(1, SUPERS - 1) as s:
                step(s)
            step(SUPERS - 1, last=True)
            pe.wait_ge(m_counted, SUPERS - 1)
            logits(SUPERS - 1, (None, 0))
            counts(SUPERS - 1)

        @block.vector
        def _(dve):
            dve.wait_ge(m_colst, 1)
            dve.wait_ge(m_const, 11)
            for k in range(KD):
                last = nc.vector.tensor_scalar(betab[:, k, :], ones[:], cols[:, BETA + k:BETA + k + 1], None, ALU.mult)
            last.then_inc(m_bd, 1)
            for k in range(KD):
                for b in range(P // HD):
                    q = slice(b * HD, (b + 1) * HD)
                    nc.vector.tensor_copy(bdkv[q, k, q], kvacc[q, k, q])
                    last = nc.vector.tensor_scalar(bdks[q, k, q], ones[q, q], kvacc[q, k, P:P + 1], None, ALU.mult)
            last.then_inc(m_bd, 1)
            dve.wait_ge(m_w, 16 * 8)
            dve.wait_ge(m_fold, 1)
            nc.vector.tensor_copy(c1[:], bank[1][:, 0:2 * D // P])
            nc.vector.tensor_tensor(lb[:], bank[3][:, 0:EXPERTS], br[:], ALU.add)
            for k in range(KD):
                nc.vector.tensor_scalar(w1[:, KD + k, :], w1[:, KD + k, :], cols[:, G1 + k:G1 + k + 1], None, ALU.mult)
                last = nc.vector.tensor_scalar(wr[:, k, :], wr[:, k, :], cols[:, GAMMA + k:GAMMA + k + 1],
                                               None, ALU.mult)
            last.then_inc(m_setup, 1)
            dve.sem_inc(m_listfree, 1)

            def moments(l, src, s, per):
                for j in range(SUP):
                    last = nc.vector.bn_stats(stats[:, j, :], src(j))
                last.then_inc(ln[l]["stats"], 1)
                dve.wait_ge(ln[l]["stats"], s + 1)
                dve.sem_inc(keep["turn"], 1)
                for j in range(SUP):
                    last = nc.vector.bn_aggr(mv[:, j, :], stats[:, j, :])
                last.then_inc(ln[l]["var"], 1)
                dve.wait_ge(ln[l]["std"], s * per + 1)
                nc.vector.reciprocal(rstd[:], std[:]).then_inc(ln[l]["rstd"], 1)
                dve.wait_ge(ln[l]["rstd"], s * per + 1)

            def normalise(l, src, s, by):
                to = nrm if l else nrm1
                for j in range(SUP):
                    last = nc.vector.tensor_scalar(to[:, j, :], src(j), mv[:, j, 0:1], by[:, j:j + 1],
                                                   ALU.subtract, ALU.mult)
                last.then_inc(ln[l]["done"], 1)
            low = lambda j: tile_cols(bank[0:4], j)
            rows_of = lambda j: x2[:, j, :]

            def elus(s):
                for i in range(4):
                    m, n = i // 2, i % 2
                    dve.wait_ge(m_q, s * 4 + (i + 1))
                    nc.vector.tensor_scalar(qmin[:, i % 2, :], bank[4 + i][:, 0:NW], 0.0, None, ALU.min).then_inc(m_qmin, 1)
                    dve.wait_ge(m_qexp, s * 4 + (i + 1))
                    nc.vector.scalar_tensor_tensor(qt[:, m, n * NW:(n + 1) * NW], bank[4 + i][:, 0:NW], 0.0,
                                                   qexp[:, i % 2, :], ALU.max, ALU.add).then_inc(m_qt, 1)

            def messages(s):
                for i in range(4):
                    m, n = i // 2, i % 2
                    dve.wait_ge(m_att, s * 4 + (i + 1))
                    nc.vector.tensor_scalar(den[:, i % 2, :], bank[1 + 2 * (i % 2)][:, 0:NW], ATT_EPS, None, ALU.add)\
                      .then_inc(m_den, 1)
                    dve.wait_ge(m_den, s * 8 + (2 * i + 1))
                    nc.vector.reciprocal(rden[:, i % 2, :], den[:, i % 2, :]).then_inc(m_den, 1)
                    dve.wait_ge(m_den, s * 8 + (2 * i + 2))
                    nc.vector.tensor_tensor(msgt[:, m, n * NW:(n + 1) * NW], bank[2 * (i % 2)][:, 0:NW],
                                            rden[:, i % 2, :], ALU.mult).then_inc(m_msg, 1)

            def norm_messages(s):
                dve.wait_ge(m_m1, s + 1)
                moments(0, low, s, 1)
                normalise(0, low, s, rstd)

            def norm_feed(s):
                dve.wait_ge(m_h2, s + 1)
                moments(1, low, s, 1)
                wait(dve, m_nrmst, s * 16)
                normalise(1, low, s, rstd)

            def residual(s):
                dve.wait_ge(ln[1]["done"], s + 1)
                nc.vector.tensor_tensor(nrm[:], nrm[:], g2[:].unsqueeze(1).to_broadcast([P, SUP, D]), ALU.mult)\
                  .then_inc(m_x2, 1)
                dve.wait_ge(m_x2, s * 2 + 1)
                dve.wait_ge(m_accb, s + 1)
                wait(dve, m_x2st, s * 16)
                nc.vector.tensor_tensor(x2[:], nrm[:], acc[:], ALU.add).then_inc(m_x2, 1)
                dve.wait_ge(m_x2, s * 2 + 2)
                dve.sem_inc(m_accfree, 1)
                moments(2, rows_of, s, 2)
                nc.vector.tensor_tensor(var2[:], rstd[:], rstd[:], ALU.mult).then_inc(ln[2]["step"], 1)
                dve.wait_ge(ln[2]["step"], s * 2 + 1)
                nc.vector.tensor_tensor(var2[:], var2[:], mv[:, :, 1], ALU.mult).then_inc(ln[2]["var"], 1)
                dve.wait_ge(ln[2]["std"], s * 2 + 2)
                nc.vector.reciprocal(rstd2[:], std[:]).then_inc(ln[2]["rstd"], 1)
                dve.wait_ge(ln[2]["rstd"], s * 2 + 2)
                nc.vector.tensor_tensor(rstd2[:], rstd2[:], rstd[:], ALU.mult).then_inc(ln[2]["step"], 1)
                dve.wait_ge(ln[2]["step"], s * 2 + 2)
                normalise(2, rows_of, s, rstd2)

            def route(s):
                dve.wait_ge(m_lg, s + 1)
                nc.vector.tensor_tensor(lg[:], bank[4][:, 0:SUP * EXPERTS].rearrange("p (j e) -> p j e", j=SUP),
                                        lb[:].unsqueeze(1).to_broadcast([P, SUP, EXPERTS]), ALU.add).then_inc(m_route, 1)
                dve.wait_ge(m_route, s * 7 + 1)
                dve.sem_inc(keep["turn"], 1)
                for j in range(SUP):
                    last = nc.vector.max(top[:, j, :], lg[:, j, :])
                last.then_inc(m_route, 1)
                dve.wait_ge(m_route, s * 7 + 2)
                nc.vector.tensor_tensor(gap[:], top[:, :, 1], top[:, :, 0], ALU.subtract).then_inc(m_gap, 1)
                for j in range(SUP):
                    last = nc.vector.max_index(idx[:, j, :], top[:, j, :], lg[:, j, :])
                last.then_inc(m_route, 1)
                dve.wait_ge(m_route, s * 7 + 3)
                nc.vector.tensor_copy(idxf[:], idx[:]).then_inc(m_route, 1)
                dve.wait_ge(m_exp, s + 1)
                nc.vector.tensor_scalar(wgt[:, :, 1], gap[:], 1.0, None, ALU.add).then_inc(m_route, 1)
                dve.wait_ge(m_route, s * 7 + 5)
                nc.vector.reciprocal(wgt[:, :, 0], wgt[:, :, 1]).then_inc(m_route, 1)
                dve.wait_ge(m_route, s * 7 + 6)
                nc.vector.tensor_tensor(wgt[:, :, 1], gap[:], wgt[:, :, 0], ALU.mult).then_inc(m_route, 1)
                for i in range(2):
                    last = nc.vector.tensor_tensor(picked[:, i], iota8[:],
                                                   idxf[:, :, i:i + 1].to_broadcast([P, SUP, EXPERTS]), ALU.is_equal)
                last.then_inc(m_pick, 1)
                dve.wait_ge(m_count, s + 1)
                count = bank[6][:, 0:CHOICES * EXPERTS].rearrange("p (b e) -> p b e", b=CHOICES)
                ahead = bank[5][:, 0:CHOICES * EXPERTS].rearrange("p (b e) -> p b e", b=CHOICES)
                nc.vector.tensor_copy(chosen[:], count).then_inc(m_place, 1)
                nc.vector.tensor_copy(upto[0][:, 1:, :], count[:, 1:, :]).then_inc(m_place, 1)
                nc.vector.tensor_tensor(upto[0][:, 0, :], count[:, 0, :], ends[:], ALU.add).then_inc(m_place, 1)
                dve.wait_ge(m_place, s * PLACE_STEPS + 3)
                n, w, done = 0, 1, 3
                while w < CHOICES:
                    nc.vector.tensor_copy(upto[1 - n][:, 0:w, :], upto[n][:, 0:w, :]).then_inc(m_place, 1)
                    nc.vector.tensor_tensor(upto[1 - n][:, w:, :], upto[n][:, w:, :], upto[n][:, :CHOICES - w, :], ALU.add)\
                      .then_inc(m_place, 1)
                    n, w, done = 1 - n, 2 * w, done + 2
                    dve.wait_ge(m_place, s * PLACE_STEPS + done)
                nc.vector.tensor_copy(ends[:], upto[n][:, CHOICES - 1, :]).then_inc(m_place, 1)
                nc.vector.tensor_tensor(place[:], ahead, upto[n][:], ALU.add).then_inc(m_place, 1)
                dve.wait_ge(m_place, s * PLACE_STEPS + done + 2)
                dve.sem_inc(m_counted, 1)
                nc.vector.tensor_tensor(place[:], place[:], chosen[:], ALU.subtract).then_inc(m_place, 1)
                dve.wait_ge(m_place, s * PLACE_STEPS + done + 3)
                nc.vector.tensor_tensor(place[:], place[:], pick[:].rearrange("p (b e) -> p b e", b=CHOICES), ALU.mult)\
                  .then_inc(m_place, 1)
                dve.wait_ge(m_place, s * PLACE_STEPS + done + 4)
                nc.vector.tensor_reduce(place_f[:], place[:], mybir.AxisListType.X, ALU.add).then_inc(m_place, 1)
                dve.wait_ge(m_place, s * PLACE_STEPS + done + 5)
                assert done + 5 == PLACE_STEPS
                dve.wait_ge(m_listfree, s + 1)
                nc.vector.tensor_copy(place_i[:], place_f[:]).then_inc(m_entry, 1)
                for i in (0, 2):
                    nc.vector.tensor_copy(entry[:, :, i], node[:]).then_inc(m_entry, 1)
                nc.vector.tensor_copy(entry[:, :, 1].rearrange("p (i j) -> p i j", i=2), wgt[:].rearrange("p j i -> p i j"))\
                  .then_inc(m_entry, 1)
                dve.wait_ge(m_entry, s * ENTRY_STEPS + 4)
                nc.vector.tensor_scalar(node[:], node[:], float(R), None, ALU.add).then_inc(m_entry, 1)
                dve.wait_ge(m_entry, s * ENTRY_STEPS + ENTRY_STEPS)

            def step(s, first=False, last=False):
                if not first:
                    norm_feed(s - 1)
                if not last:
                    elus(s + 1)
                if not first:
                    residual(s - 1)
                if not last:
                    messages(s + 1)
                    norm_messages(s + 1)
                if not first:
                    route(s - 1)
            elus(0)
            messages(0)
            norm_messages(0)
            step(0, first=True)
            with dve.Fori(1, SUPERS - 1) as s:
                step(s)
            step(SUPERS - 1, last=True)
            norm_feed(SUPERS - 1)
            residual(SUPERS - 1)
            route(SUPERS - 1)


def expert_phase(nc, sem, mem, d, keep, out):
    def sb(name, shape, dt=F32):
        return mem.enter_context(nc.sbuf_tensor(f"moe_{name}", shape, dt))

    ident, we1, we2, be1, be2, cols, betab, ends = (keep[k] for k in (
        "ident", "we1", "we2", "be1", "be2", "cols", "betab", "ends"))
    GAMMA = VEC[2]
    region = sb("region", [1, EXPERTS])
    cum = [sb(f"cum{i}", [1, EXPERTS]) for i in range(2)]
    need, need_i = sb("need", [1, EXPERTS]), sb("need_i", [1, EXPERTS], I32)
    tile_no = sb("tile_no", [1, LTILES, EXPERTS])
    past, behind = sb("past", [1, LTILES, EXPERTS]), sb("behind", [1, LTILES, EXPERTS])
    expert_f, gone, row_f = sb("expert_f", [1, LTILES]), sb("gone", [1, LTILES]), sb("row_f", [1, LTILES])
    expert_i, row_i = sb("expert_i", [1, LTILES], I32), sb("row_i", [1, LTILES], I32)
    ents = sb("ents", [P, LTILES, 4])
    source = [sb(f"source{i}", [P, 1], I32) for i in range(2)]
    target = [sb(f"target{i}", [P, 1], I32) for i in range(2)]
    weight = [sb(f"weight{i}", [P, 1]) for i in range(2)]
    rows = [sb(f"rows{i}", [P, D]) for i in range(2)]
    rows_t = sb("rows_t", [P, KD * P])
    hid, hid_act, hid_t = sb("hid", [P, HID]), sb("hid_act", [P, HID]), sb("hid_t", [P, HB * P])
    yb, yw = sb("yb", [P, D]), [sb(f"yw{i}", [P, D]) for i in range(2)]
    ps = lambda n: mem.enter_context(nc.psum_tensor(n, [P, 512], F32))
    p_rows, p_hid, p_hidt, p_y = ps("p_rows"), ps("p_hid"), ps("p_hidt"), ps("p_y")
    p_beta = [ps("p_beta0"), ps("p_beta1")]

    y_const, y_plan, y_beta, y_bias, y_scaled = (sem(f"y_{k}") for k in ("const", "plan", "beta", "bias", "scaled"))
    y_ents = [sem(f"y_ents{i}") for i in range(2)]
    y_rows = [sem(f"y_rows{i}", pool_dma=True) for i in range(2)]
    y_added = sem("y_added", pool_dma=True)
    y_addfree = sem("y_addfree")
    y_source = sem("y_source")
    y_tr = sem("y_tr")
    y_rowst, y_hid, y_biased, y_gelu, y_htr, y_hidt, y_out, y_yb, y_yw = (sem(f"y_{k}") for k in (
        "rowst", "hid", "biased", "gelu", "htr", "hidt", "out", "yb", "yw"))
    PLAN = 19

    with nc.Block() as block:
        @block.sync
        def _(sp):
            sp.wait_ge(y_plan, PLAN)

            def load(half, b):
                i = half * 2 + b
                row = sp.value_load(row_i[0:1, bass.ds(i, 1)], min_val=0, max_val=EXPERTS * REGION)
                sp.dma_start(ents[:, bass.ds(i, 1), :].rearrange("p o c -> p (o c)"), d["lists"][bass.ds(row, P), :])\
                  .then_inc(y_ents[b], 16)
            load(0, 0)
            load(0, 1)
            with sp.Fori(1, LTILES // 2) as half:
                for b in range(2):
                    sp.wait_ge(y_ents[b], half * 16)
                    sp.sem_inc(keep["turn"], 1)
                    load(half, b)
            sp.wait_ge(y_ents[0], LTILES // 2 * 16)
            load(LTILES // 2, 0)

        @block.gpsimd
        def _(pool):
            nc.gpsimd.iota(region[:], [[REGION, EXPERTS]], base=0, channel_multiplier=0,
                           allow_small_or_imprecise_dtypes=True).then_inc(y_const, 1)
            nc.gpsimd.iota(tile_no[:], [[1, LTILES], [0, EXPERTS]], base=0, channel_multiplier=0,
                           allow_small_or_imprecise_dtypes=True).then_inc(y_const, 1)
            pool.sem_inc(y_addfree, 2)

            def gather(half, b):
                pool.wait_ge(y_source, half * 2 + (b + 1))
                pool.sem_inc(keep["turn"], 1)
                pool.indirect_dma_start(rows[b][:], None, d["table"],
                                        bass.IndirectOffsetOnAxis(ap=source[b][:, 0:1], axis=0)).then_inc(y_rows[b], 16)

            def add(half, b):
                pool.wait_ge(y_yw, half * 2 + (b + 2))
                pool.sem_inc(keep["turn"], 1)
                pool.indirect_dma_start(out, bass.IndirectOffsetOnAxis(ap=target[b][:, 0:1], axis=0),
                                        yw[b][:], None, compute_op=ALU.add).then_inc(y_added, 16)
                pool.wait_ge(y_added, half * 32 + (b + 1) * 16)
                pool.sem_inc(y_addfree, 1)

            def step(half, b, last=None):
                if last is None or last + AHEAD < LTILES:
                    gather(half + (b + AHEAD) // 2, (b + AHEAD) % 2)
                add(half, b)
            for i in range(AHEAD):
                gather(i // 2, i % 2)
            with pool.Fori(0, LOOPED // 2) as half:
                step(half, 0)
                step(half, 1)
            for i in range(LOOPED, LTILES):
                step(i // 2, i % 2, i)

        @block.tensor
        def _(pe):
            for e in range(EXPERTS):
                if e >= 2:
                    pe.wait_ge(y_bias, e - 1)
                for k in range(KD):
                    last = nc.tensor.matmul(p_beta[e % 2][:], betab[:, k, :], we1[:, e, k, :],
                                            start=(k == 0), stop=(k == KD - 1))
                last.then_inc(y_beta, 1)
            pe.sem_inc(y_tr, 2)
            for s in (y_hid, y_htr, y_out):
                pe.sem_inc(s, 1)

            def turn_rows(half, b):
                i = half * 2 + b
                pe.wait_ge(y_rows[b], half * 16 + 16)
                pe.wait_ge(y_rowst, i + 1)
                for k in range(KD):
                    last = nc.tensor.transpose(p_rows[:, k * P:(k + 1) * P], rows[b][:, k * P:(k + 1) * P], ident[:])
                last.then_inc(y_tr, 1)

            def up(half, b):
                i = half * 2 + b
                e = pe.value_load(expert_i[0:1, bass.ds(i, 1)], min_val=0, max_val=EXPERTS - 1)
                pe.wait_ge(y_rowst, i + 2)
                pe.wait_ge(y_biased, i + 1)
                for k in range(KD):
                    last = nc.tensor.matmul(p_hid[:], rows_t[:, k * P:(k + 1) * P],
                                            we1[:, bass.ds(e, 1), k, :].rearrange("p o h -> p (o h)"),
                                            start=(k == 0), stop=(k == KD - 1))
                last.then_inc(y_hid, 1)

            def turn_hidden(half, b):
                i = half * 2 + b
                pe.wait_ge(y_gelu, i + 2)
                pe.wait_ge(y_hidt, i + 1)
                for k in range(HB):
                    last = nc.tensor.transpose(p_hidt[:, k * P:(k + 1) * P], hid_act[:, k * P:(k + 1) * P], ident[:])
                last.then_inc(y_htr, 1)

            def down(half, b):
                i = half * 2 + b
                e = pe.value_load(expert_i[0:1, bass.ds(i, 1)], min_val=0, max_val=EXPERTS - 1)
                pe.wait_ge(y_hidt, i + 2)
                pe.wait_ge(y_yb, i + 1)
                for k in range(HB):
                    last = nc.tensor.matmul(p_y[:, 0:D], hid_t[:, k * P:(k + 1) * P],
                                            we2[:, bass.ds(e, 1), k, :].rearrange("p o f -> p (o f)"),
                                            start=(k == 0), stop=(k == HB - 1))
                last.then_inc(y_out, 1)

            def step(half, b, last=None):
                turn_hidden(half, b)
                if last is None or last + 1 < LTILES:
                    up(half + (b + 1) // 2, (b + 1) % 2)
                if last is None or last + 2 < LTILES:
                    turn_rows(half + 1, b)
                down(half, b)
            pe.wait_ge(y_plan, PLAN)
            turn_rows(0, 0)
            pe.wait_ge(y_scaled, EXPERTS)
            up(0, 0)
            turn_rows(0, 1)
            with pe.Fori(0, LOOPED // 2) as half:
                step(half, 0)
                step(half, 1)
            for i in range(LOOPED, LTILES):
                step(i // 2, i % 2, i)

        @block.scalar
        def _(act):
            for s in (y_rowst, y_gelu, y_hidt, y_yw):
                act.sem_inc(s, 1)
            for e in range(EXPERTS):
                act.wait_ge(y_beta, e + 1)
                for k in range(KD):
                    last = nc.scalar.activation(we1[:, e, k, :], we1[:, e, k, :], ACT.Copy,
                                                scale=cols[:, GAMMA + k:GAMMA + k + 1])
                last.then_inc(y_scaled, 1)

            def copy_rows(i):
                act.wait_ge(y_tr, i + 3)
                act.wait_ge(y_hid, i + 1)
                nc.scalar.activation(rows_t[:], p_rows[:, 0:KD * P], ACT.Copy).then_inc(y_rowst, 1)

            def gelu(i):
                act.wait_ge(y_biased, i + 2)
                act.wait_ge(y_htr, i + 1)
                nc.scalar.activation(hid_act[:], hid[:], ACT.Gelu).then_inc(y_gelu, 1)

            def copy_hidden(i):
                act.wait_ge(y_htr, i + 2)
                act.wait_ge(y_out, i + 1)
                nc.scalar.activation(hid_t[:], p_hidt[:], ACT.Copy).then_inc(y_hidt, 1)

            def weigh(i, b):
                act.wait_ge(y_yb, i + 2)
                act.wait_ge(y_addfree, i + 1)
                nc.scalar.activation(yw[b][:], yb[:], ACT.Copy, scale=weight[b][:]).then_inc(y_yw, 1)

            def step(half, b, last=None):
                i = half * 2 + b
                copy_hidden(i)
                if last is None or last + 2 < LTILES:
                    copy_rows(i + 2)
                if last is None or last + 1 < LTILES:
                    gelu(i + 1)
                weigh(i, b)
            copy_rows(0)
            copy_rows(1)
            gelu(0)
            with act.Fori(0, LOOPED // 2) as half:
                step(half, 0)
                step(half, 1)
            for i in range(LOOPED, LTILES):
                step(i // 2, i % 2, i)

        @block.vector
        def _(dve):
            for s in (y_biased, y_yb):
                dve.sem_inc(s, 1)
            steps = [0]

            def plan(instruction):
                instruction.then_inc(y_plan, 1)
                steps[0] += 1
                dve.wait_ge(y_plan, steps[0])
            dve.wait_ge(y_const, 2)
            plan(nc.vector.tensor_tensor(need[:], ends[0:1, :], region[:], ALU.subtract))
            plan(nc.vector.tensor_scalar(need[:], need[:], float(P - 1), None, ALU.add))
            plan(nc.vector.tensor_copy(need_i[:], need[:]))
            plan(nc.vector.tensor_scalar(need_i[:], need_i[:], 7, None, ALU.logical_shift_right))
            plan(nc.vector.tensor_copy(need[:], need_i[:]))
            plan(nc.vector.tensor_copy(cum[0][:], need[:]))
            n, w = 0, 1
            while w < EXPERTS:
                nc.vector.tensor_copy(cum[1 - n][:, 0:w], cum[n][:, 0:w])
                plan(nc.vector.tensor_tensor(cum[1 - n][:, w:], cum[n][:, w:], cum[n][:, :EXPERTS - w], ALU.add))
                n, w = 1 - n, 2 * w
            plan(nc.vector.tensor_tensor(past[:], tile_no[:], cum[n][:].unsqueeze(1).to_broadcast([1, LTILES, EXPERTS]),
                                         ALU.is_ge))
            plan(nc.vector.tensor_reduce(expert_f[:], past[:], mybir.AxisListType.X, ALU.add))
            plan(nc.vector.tensor_tensor(behind[:], past[:], need[:].unsqueeze(1).to_broadcast([1, LTILES, EXPERTS]),
                                         ALU.mult))
            plan(nc.vector.tensor_reduce(gone[:], behind[:], mybir.AxisListType.X, ALU.add))
            plan(nc.vector.tensor_tensor(gone[:], tile_no[:, :, 0], gone[:], ALU.subtract))
            plan(nc.vector.tensor_scalar(gone[:], gone[:], float(P), None, ALU.mult))
            plan(nc.vector.scalar_tensor_tensor(row_f[:], expert_f[:], float(REGION), gone[:], ALU.mult, ALU.add))
            plan(nc.vector.tensor_scalar(row_f[:], row_f[:], float(EXPERTS * REGION), None, ALU.min))
            nc.vector.tensor_scalar(expert_f[:], expert_f[:], float(EXPERTS - 1), None, ALU.min)
            plan(nc.vector.tensor_copy(row_i[:], row_f[:]))
            plan(nc.vector.tensor_copy(expert_i[:], expert_f[:]))
            assert steps[0] == PLAN, steps
            for e in range(EXPERTS):
                dve.wait_ge(y_beta, e + 1)
                nc.vector.tensor_tensor(be1[:, e * HID:(e + 1) * HID], p_beta[e % 2][:], be1[:, e * HID:(e + 1) * HID],
                                        ALU.add).then_inc(y_bias, 1)
            dve.wait_ge(y_bias, EXPERTS)

            def sources(half, b):
                i = half * 2 + b
                dve.wait_ge(y_ents[b], half * 16 + 16)
                dve.wait_ge(y_tr, i + 1)
                nc.vector.tensor_copy(source[b][:], ents[:, bass.ds(i, 1), 0]).then_inc(y_source, 1)

            def bias(i):
                e = dve.value_load(expert_i[0:1, bass.ds(i, 1)], min_val=0, max_val=EXPERTS - 1)
                dve.wait_ge(y_hid, i + 2)
                dve.wait_ge(y_gelu, i + 1)
                nc.vector.tensor_tensor(hid[:], p_hid[:], be1[:, bass.ds(e * HID, HID)], ALU.add).then_inc(y_biased, 1)
                return e

            def finish(i, b):
                e = dve.value_load(expert_i[0:1, bass.ds(i, 1)], min_val=0, max_val=EXPERTS - 1)
                dve.wait_ge(y_addfree, i + 1)
                dve.wait_ge(y_yw, i + 1)
                dve.sem_inc(keep["turn"], 1)
                nc.vector.tensor_copy(target[b][:], ents[:, bass.ds(i, 1), 2])
                nc.vector.tensor_copy(weight[b][:], ents[:, bass.ds(i, 1), 1])
                dve.wait_ge(y_out, i + 2)
                nc.vector.tensor_tensor(yb[:], p_y[:, 0:D], be2[:, bass.ds(e * D, D)], ALU.add).then_inc(y_yb, 1)

            def step(half, b, last=None):
                i = half * 2 + b
                if last is None or last + AHEAD < LTILES:
                    sources(half + (b + AHEAD) // 2, (b + AHEAD) % 2)
                if last is None or last + 1 < LTILES:
                    bias(i + 1)
                finish(i, b)
            for i in range(AHEAD):
                sources(i // 2, i % 2)
            bias(0)
            with dve.Fori(0, LOOPED // 2) as half:
                step(half, 0)
                step(half, 1)
            for i in range(LOOPED, LTILES):
                step(i // 2, i % 2, i)


INPUTS = ["x", "src", "dst",
          "gnn_W1_l", "gnn_b1", "gnn_W1_r", "gnn_W2_l", "gnn_b2", "gnn_W2_r",
          "mix_Wq", "mix_Wk", "mix_Wv", "mix_Wm", "mix_W1", "mix_W2", "mix_g1", "mix_b1", "mix_g2", "mix_b2",
          "ffn_gamma", "ffn_beta", "ffn_Wr", "ffn_br", "ffn_W1", "ffn_b1", "ffn_W2", "ffn_b2"]


def kernel(**inputs):
    import numpy as np
    import concourse.bacc as bacc
    from concourse.bass_utils import run_bass_kernel_spmd

    nc = bacc.Bacc("TRN2", target_bir_lowering=False, num_devices=1)
    arrays, t_in = {}, {}
    for name in INPUTS:
        a = np.ascontiguousarray(inputs[name if name in inputs else "L0_" + name])
        if name == "x":
            padded = np.zeros((NPAD, D), a.dtype)
            padded[:N_NODES] = a
            a = padded
        arrays[f"in_{name}"] = a
        t_in[name] = nc.dram_tensor(f"in_{name}", a.shape, mybir.dt.from_np(a.dtype), kind="ExternalInput").ap()
    out = nc.dram_tensor("out", (NPAD + P, D), F32, kind="ExternalOutput").ap()
    program(nc, t_in, out)
    r = run_bass_kernel_spmd(nc, [arrays], core_ids=[0])
    return r.results[0]["out"][:N_NODES]
```

```python
from contextlib import ExitStack

import concourse.bass as bass
from concourse import mybir

F32 = mybir.dt.float32
F16 = mybir.dt.float16
F8 = mybir.dt.float8e4
I32 = mybir.dt.int32
U32 = mybir.dt.uint32
ALU = mybir.AluOpType
ACT = mybir.ActivationFunctionType

P = 128
N_NODES, N_EDGES, D = 6250, 200000, 256
KD = D // P
TILES = -(-N_NODES // P)
NPAD = TILES * P
SUP = 7
SUPERS = TILES // SUP
R = SUP * P
NB = 2
NW = R // NB
LN_EPS = 1e-5
ATT_EPS = 1e-6
HEADS, HD = 8, 32
EXPERTS, HID = 8, 512
HB = HID // P

GN = 8
GROUPS = P // GN
CHUNKS = 3
GE = CHUNKS * P
EROW = 32
WROWS = GE // EROW
GC = GN * TILES
ROW = 400
ROWS = N_EDGES // ROW
STILES = -(-(TILES * GROUPS + 1) // P)
CAP = 16
CSCALE = CAP / 2.0
VEC = [i * KD for i in range(4)]
CHOICES = 2 * SUP
REGION = NPAD + P
LISTS = -(-(EXPERTS * REGION + P) // (P * P)) * P * P
LTILES = (2 * NPAD + EXPERTS * (P - 1)) // P
AHEAD = 3
LOOPED = (LTILES - AHEAD) // 2 * 2
PLACE_STEPS = 3 + 2 * 4 + 5
ENTRY_STEPS = 5
EP = 125
ELEN = N_EDGES // EP
LO_SCALE = 2048.0
FAR = -1.0e6

ONEHOTS = 4
BANKS = 2
SPLIT = (0, TILES // 2, TILES)


def program(nc, t_in, out):
    with ExitStack() as ctx:
        def kept_sem(name):
            return ctx.enter_context(nc.semaphore(name))

        def dram(name, shape, dt):
            return nc.dram_tensor(name, shape, dt).ap()

        d = dict(
            edges=dram("edges", [(N_EDGES + GE) // EROW, 2 * EROW], F32),
            adj=dram("adj", [TILES, P, TILES * P // 4], I32),
            xnt=dram("xnt", [TILES, P, KD, P], F32),
            acc=dram("acc", [NPAD, D], F32),
            table=dram("table", [NPAD, D], F32),
            lists=dram("lists", [LISTS, 4], F32),
            feat1=dram("feat1", [NPAD, D], F32),
            feat2=dram("feat2", [NPAD, D], F32),
        )

        def sb(stack, name, shape, dt):
            return stack.enter_context(nc.sbuf_tensor(name, shape, dt))

        keep = dict(
            ident=sb(ctx, "ident", [P, P], F32),
            eps=sb(ctx, "eps", [P, 1], F32),
            kvacc=sb(ctx, "kvacc", [P, KD, P + 1], F32),
            uncovered=sb(ctx, "uncovered", [P, 1], F32),
            flag=sb(ctx, "flag", [1, 1], I32),
            turn=kept_sem("turn"),
        )

        def run(phase, *args, last=False):
            used = []
            with ExitStack() as mem:
                def sem(name, pool_dma=False):
                    if pool_dma:
                        return kept_sem(name)
                    used.append(mem.enter_context(nc.semaphore(name)))
                    return used[-1]
                phase(nc, sem, mem, d, *args)
                if last:
                    return
                with nc.Block() as block:
                    @block.gpsimd
                    def _(pool):
                        for s in used:
                            pool.sem_clear(s)

        with ExitStack() as graph:
            keep["window"] = sb(graph, "window", [P, STILES, WROWS], I32)
            run(edge_phase, t_in, keep)
            keep["lo_all"] = sb(graph, "lo_all", [P, STILES * P, CHUNKS], F16)
            keep["key_all"] = sb(graph, "key_all", [P, STILES * P, CHUNKS], F32)
            keep["iota_key"] = sb(graph, "iota_key", [P, GC], F16)
            keep["iota_lo"] = sb(graph, "iota_lo", [P, P, GROUPS * CHUNKS], F16)
            keep["yh"] = sb(graph, "yh", [P, TILES, D + 2], F16)
            keep["yl"] = sb(graph, "yl", [P, TILES, D], F16)
            keep["w2lr"] = sb(graph, "w2lr", [P, KD, 2 * D], F32)
            keep["w1r"] = sb(graph, "w1r", [P, KD, D], F32)
            keep["b1"] = sb(graph, "b1", [P, D], F32)
            keep["b2"] = sb(graph, "b2", [P, D], F32)
            keep["rdeg"] = sb(graph, "rdeg", [P, TILES], F32)
            keep["unscale"] = sb(graph, "unscale", [P, 2], F32)
            with ExitStack() as windows:
                keep["keybase"] = sb(windows, "keybase", [P, STILES * P, CHUNKS], F32)
                keep["gathered"] = sb(windows, "gathered", [P, STILES, GE, 2], F32)
                run(norm_phase, t_in, keep)
                run(turn_phase, keep)
            keep["y2h"] = sb(graph, "y2h", [P, TILES, D], F16)
            keep["y2l"] = sb(graph, "y2l", [P, TILES, D], F16)
            run(layer1_phase, keep)
            run(layer2_phase, keep)
        run(general_phase, t_in, keep)
        for name, n in (("we1", EXPERTS * KD * HID), ("we2", EXPERTS * HB * D), ("be1", EXPERTS * HID),
                        ("be2", EXPERTS * D), ("cols", 4 * KD), ("betab", KD * P), ("ends", EXPERTS)):
            keep[name] = sb(ctx, name, [P, n], F32)
        keep["we1"] = keep["we1"][:].rearrange("p (e k h) -> p e k h", e=EXPERTS, k=KD)
        keep["we2"] = keep["we2"][:].rearrange("p (e k f) -> p e k f", e=EXPERTS, k=HB)
        keep["betab"] = keep["betab"][:].rearrange("p (k c) -> p k c", k=KD)
        run(mix_phase, t_in, keep, out)
        run(expert_phase, keep, out, last=True)


def edge_phase(nc, sem, mem, d, t_in, keep):
    def sb(name, shape, dt):
        return mem.enter_context(nc.sbuf_tensor(name, shape, dt))

    src, dst = t_in["src"], t_in["dst"]
    src_i = sb("src_i", [EP, ELEN], I32)
    dst_i = sb("dst_i", [EP, ELEN], I32)
    lo_i = sb("lo_i", [EP, ELEN], I32)
    pair = sb("pair", [EP, ELEN, 2], F32)
    pad = sb("pad", [P, CHUNKS, 2], F32)
    first_i = sb("first_i", [1, ROWS], I32)
    first_f = sb("first_f", [1, ROWS], F32)
    ones_row = sb("ones_row", [1, P], F32)
    firsts = sb("firsts", [P, ROWS], F32)
    bound = sb("bound", [P, STILES], F32)
    below = sb("below", [P, STILES], F32)
    row_i = sb("row_i", [P, STILES], I32)
    rows_i = sb("rows_i", [P, STILES, ROW], I32)
    rows_f = sb("rows_f", [P, STILES, ROW], F32)
    scratch = sb("scratch", [P, STILES, max(ROWS, ROW)], F32)
    within = sb("within", [P, STILES], F32)
    start_f = sb("start_f", [P, STILES], F32)
    start_i = sb("start_i", [P, STILES], I32)
    row0 = sb("row0", [P, STILES], F32)
    steps = sb("steps", [P, STILES, WROWS], F32)
    spread = mem.enter_context(nc.psum_tensor("spread", [P, 512], F32))

    dst_f = sb("dst_f", [EP, ELEN + 1], F32)
    next_i = sb("next_i", [EP, 1], I32)
    falls = sb("falls", [EP, ELEN], F32)
    e_next, e_order = sem("e_next"), sem("e_order")
    e_dst, e_src, e_first = sem("e_dst"), sem("e_src"), sem("e_first")
    e_const = sem("e_const")
    e_split = sem("e_split")
    e_firstf, e_spread = sem("e_firstf"), sem("e_spread")
    e_search = sem("e_search")
    e_rowi, e_rows = sem("e_rowi"), sem("e_rows", pool_dma=True)
    e_stored = sem("e_stored")
    dst_rows = dst.rearrange("(r n) -> r n", n=ROW)

    with nc.Block() as block:
        @block.sync
        def _(sp):
            with nc.allow_non_contiguous_dma(reason="one element of each row"):
                sp.dma_start(first_i[:], dst.rearrange("(r n) -> n r", n=ROW)[0:1, :]).then_inc(e_first, 16)
            sp.dma_start(dst_i[:], dst.rearrange("(p n) -> p n", p=EP)).then_inc(e_dst, 16)
            sp.dma_start(src_i[:], src.rearrange("(p n) -> p n", p=EP)).then_inc(e_src, 16)
            sp.wait_ge(e_order, 1)
            with nc.allow_non_contiguous_dma(reason="one element of each row"):
                sp.dma_start(next_i[0:EP - 1, :], dst.rearrange("(p n) -> p n", p=EP)[1:EP, 0:1]).then_inc(e_next, 16)
            sp.wait_ge(e_const, 1)
            flat = d["edges"].rearrange("r (n c) -> (r n) c", c=2)
            sp.dma_start(flat[N_EDGES:N_EDGES + GE, :].rearrange("(p n) c -> p n c", p=P), pad[:]).then_inc(e_stored, 16)
            sp.wait_ge(e_split, 5)
            sp.dma_start(flat[0:N_EDGES, :].rearrange("(p n) c -> p n c", p=EP), pair[:])\
              .then_inc(e_stored, 16)
            sp.wait_ge(e_stored, 32)

        @block.gpsimd
        def _(pool):
            nc.gpsimd.memset(pad[:, :, 0:1], 0.0)
            nc.gpsimd.memset(pad[:, :, 1:2], FAR).then_inc(e_const, 1)
            nc.gpsimd.memset(ones_row[:], 1.0).then_inc(e_const, 1)
            nc.gpsimd.iota(bound[:], [[GN * P, STILES]], base=0, channel_multiplier=GN,
                           allow_small_or_imprecise_dtypes=True).then_inc(e_const, 1)
            nc.gpsimd.memset(keep["eps"][:], LN_EPS).then_inc(e_const, 1)
            nc.gpsimd.memset(keep["kvacc"][:], 0.0).then_inc(e_const, 1)
            nc.gpsimd.memset(keep["ident"][:], 0.0).then_inc(e_const, 1)
            nc.gpsimd.iota(steps[:], [[0, STILES], [1, WROWS]], base=0, channel_multiplier=0,
                           allow_small_or_imprecise_dtypes=True).then_inc(e_const, 1)
            pool.wait_ge(e_const, 6)
            nc.gpsimd.affine_select(out=keep["ident"][:], in_=keep["ident"][:], compare_op=ALU.not_equal,
                                    fill=1.0, base=0, pattern=[[-1, P]], channel_multiplier=1).then_inc(e_const, 1)
            pool.wait_ge(e_rowi, 1)
            for r in range(STILES):
                pool.indirect_dma_start(rows_i[:, r, :], None, dst_rows,
                                        bass.IndirectOffsetOnAxis(ap=row_i[:, r:r + 1], axis=0)).then_inc(e_rows, 16)
            pool.wait_ge(e_const, 8)
            pool.wait_ge(e_rows, 16 * STILES)

        @block.tensor
        def _(pe):
            pe.wait_ge(e_const, 2)
            pe.wait_ge(e_firstf, 1)
            nc.tensor.matmul(spread[:, 0:ROWS], ones_row[:], first_f[:], start=True, stop=True).then_inc(e_spread, 1)

        @block.vector
        def _(dve):
            nc.vector.memset(next_i[:], N_NODES).then_inc(e_order, 1)
            nc.vector.memset(keep["uncovered"][:], 0.0).then_inc(e_order, 1)
            dve.wait_ge(e_first, 16)
            nc.vector.tensor_copy(first_f[:], first_i[:]).then_inc(e_firstf, 1)
            dve.wait_ge(e_const, 3)
            dve.wait_ge(e_spread, 1)
            nc.vector.tensor_copy(firsts[:], spread[:, 0:ROWS]).then_inc(e_search, 1)
            dve.wait_ge(e_search, 1)
            for r in range(STILES):
                last = nc.vector.tensor_scalar(scratch[:, r, 0:ROWS], firsts[:], bound[:, r:r + 1], 0.0,
                                               ALU.is_lt, ALU.add, accum_out=below[:, r:r + 1])
            last.then_inc(e_search, 1)
            dve.wait_ge(e_search, 2)
            nc.vector.tensor_scalar(below[:], below[:], -1.0, 0.0, ALU.add, ALU.max).then_inc(e_search, 1)
            dve.wait_ge(e_search, 3)
            nc.vector.tensor_copy(row_i[:], below[:]).then_inc(e_rowi, 1)
            dve.wait_ge(e_src, 16)
            dve.wait_ge(e_dst, 16)
            dve.wait_ge(e_next, 16)
            nc.vector.tensor_copy(dst_f[:, 0:ELEN], dst_i[:]).then_inc(e_order, 1)
            nc.vector.tensor_copy(dst_f[:, ELEN:], next_i[:]).then_inc(e_order, 1)
            dve.wait_ge(e_order, 4)
            nc.vector.tensor_tensor(falls[:], dst_f[:, 0:ELEN], dst_f[:, 1:], ALU.subtract).then_inc(e_order, 1)
            dve.wait_ge(e_order, 5)
            nc.vector.tensor_scalar(falls[:], falls[:], 0.0, 0.0, ALU.is_gt, ALU.add,
                                    accum_out=keep["uncovered"][0:EP, :]).then_inc(e_order, 1)
            dve.wait_ge(e_order, 6)
            nc.vector.tensor_scalar(lo_i[:], src_i[:], P - 1, None, ALU.bitwise_and).then_inc(e_split, 1)
            dve.wait_ge(e_split, 1)
            nc.vector.tensor_scalar(src_i[:], src_i[:], 7, None, ALU.logical_shift_right).then_inc(e_split, 1)
            nc.vector.tensor_scalar(dst_i[:], dst_i[:], TILES, None, ALU.mult).then_inc(e_split, 1)
            nc.vector.tensor_copy(pair[:, :, 0], lo_i[:]).then_inc(e_split, 1)
            dve.wait_ge(e_split, 4)
            nc.vector.tensor_tensor(pair[:, :, 1], src_i[:], dst_i[:], ALU.add).then_inc(e_split, 1)
            dve.wait_ge(e_rows, 16 * STILES)
            nc.vector.tensor_copy(rows_f[:], rows_i[:]).then_inc(e_search, 1)
            dve.wait_ge(e_search, 4)
            for r in range(STILES):
                last = nc.vector.tensor_scalar(scratch[:, r, 0:ROW], rows_f[:, r, :], bound[:, r:r + 1], 0.0,
                                               ALU.is_lt, ALU.add, accum_out=within[:, r:r + 1])
            last.then_inc(e_search, 1)
            dve.wait_ge(e_search, 5)
            nc.vector.scalar_tensor_tensor(start_f[:], below[:], float(ROW), within[:], ALU.mult, ALU.add)\
              .then_inc(e_search, 1)
            dve.wait_ge(e_search, 6)
            nc.vector.tensor_copy(start_i[:], start_f[:]).then_inc(e_search, 1)
            dve.wait_ge(e_search, 7)
            nc.vector.tensor_scalar(start_i[:], start_i[:], 5, None, ALU.logical_shift_right).then_inc(e_search, 1)
            dve.wait_ge(e_search, 8)
            nc.vector.tensor_copy(row0[:], start_i[:]).then_inc(e_search, 1)
            dve.wait_ge(e_search, 9)
            dve.wait_ge(e_const, 7)
            nc.vector.tensor_tensor(keep["window"][:], steps[:], row0[:].unsqueeze(2).to_broadcast([P, STILES, WROWS]),
                                    ALU.add).then_inc(e_search, 1)
            dve.wait_ge(e_search, 10)


def norm_phase(nc, sem, mem, d, t_in, keep):
    def sb(name, shape, dt):
        return mem.enter_context(nc.sbuf_tensor(name, shape, dt))

    def ps(name):
        return mem.enter_context(nc.psum_tensor(name, [P, 512], F32))

    ident, eps, kvacc, yh, yl = (keep[k] for k in ("ident", "eps", "kvacc", "yh", "yl"))
    w2lr, w1r, b1, b2, unscale = (keep[k] for k in ("w2lr", "w1r", "b1", "b2", "unscale"))
    xb = sb("xb", [P, SUP, D], F32)
    xn = sb("xn", [P, SUP, D], F32)
    xr = sb("xr", [P, SUP, D], F32)
    xnt = sb("xnt_sb", [P, KD, R], F32)
    wyk = sb("wyk", [P, KD, 2 * D], F32)
    wv = sb("wv", [P, KD, D], F32)
    stats = sb("stats", [P, SUP, 6], F32)
    meanvar = sb("meanvar", [P, SUP, 2], F32)
    std = sb("std", [P, SUP], F32)
    rstd = sb("rstd", [P, SUP], F32)
    kmin = sb("kmin", [P, 2, D], F32)
    kexp = sb("kexp", [P, 2, D], F32)
    kbuf = sb("kbuf", [P, SUP, D], F32)
    vbuf = sb("vbuf", [P, SUP, KD, P + 1], F32)
    valid = sb("valid", [P, TILES], F32)
    ones = sb("ones", [P, P], F32)
    squares = sb("squares", [P, 4, KD * D], F32)
    sumsq = sb("sumsq", [P, 4], F32)
    norms = sb("norms", [P, 4], F32)
    bnd = sb("bnd", [P, 2], F32)
    tmp = sb("tmp", [P, 2], F32)
    scale = sb("scale", [P, 2], F32)
    rscale = sb("rscale", [P, 2], F32)
    pt = [ps(f"pt{i}") for i in range(2)]
    pyk = [ps(f"pyk{i}") for i in range(2)]
    pv = [ps(f"pv{i}") for i in range(2)]
    pkv = ps("pkv")

    n_w, n_b = sem("n_w"), sem("n_b")
    n_gather = sem("n_gather", pool_dma=True)
    n_const = sem("n_const")
    n_sq, n_norm, n_sc = sem("n_sq"), sem("n_norm"), sem("n_sc")
    n_sums = sem("n_sums")
    n_x, n_xfree = sem("n_x"), sem("n_xfree")
    n_stats, n_var, n_std, n_rstd, n_xn = (sem(f"n_{k}") for k in ("stats", "var", "std", "rstd", "xn"))
    n_xr, n_xrfree, n_xrst = sem("n_xr"), sem("n_xrfree"), sem("n_xrst")
    n_tr, n_xnt, n_xntst, n_xntfree = sem("n_tr"), sem("n_xnt"), sem("n_xntst"), sem("n_xntfree")
    n_yk, n_ykfree = sem("n_yk"), sem("n_ykfree")
    n_yh, n_v, n_kmin, n_kexp, n_k = (sem(f"n_{k}") for k in ("yh", "v", "kmin", "kexp", "k"))
    n_yl, n_ones = sem("n_yl"), sem("n_ones")
    n_kv, n_kvacc = sem("n_kv"), sem("n_kvacc")

    NEXT = 2
    kb = lambda w: w.rearrange("(k p) n -> p k n", p=P)
    x_s = t_in["x"].rearrange("(s j p) f -> s p j f", p=P, j=SUP)
    acc_s = d["acc"].rearrange("(s j p) f -> s p j f", p=P, j=SUP)
    xnt_s = d["xnt"].rearrange("(s j) p k c -> s p k j c", j=SUP)

    with nc.Block() as block:
        @block.sync
        def _(sp):
            sp.dma_start(xb[:], x_s[0]).then_inc(n_x, 16)
            sp.dma_start(wyk[:, :, 0:D], kb(t_in["gnn_W1_l"])).then_inc(n_w, 16)
            sp.dma_start(wyk[:, :, D:2 * D], kb(t_in["mix_Wk"])).then_inc(n_w, 16)
            sp.dma_start(wv[:], kb(t_in["mix_Wv"])).then_inc(n_w, 16)
            sp.dma_start(w1r[:], kb(t_in["gnn_W1_r"])).then_inc(n_w, 16)
            sp.dma_start(w2lr[:, :, 0:D], kb(t_in["gnn_W2_l"])).then_inc(n_w, 16)
            sp.dma_start(w2lr[:, :, D:2 * D], kb(t_in["gnn_W2_r"])).then_inc(n_w, 16)
            sp.dma_start(b1[:], t_in["gnn_b1"].unsqueeze(0).to_broadcast([P, D])).then_inc(n_b, 16)
            sp.dma_start(b2[:], t_in["gnn_b2"].unsqueeze(0).to_broadcast([P, D])).then_inc(n_b, 16)
            sp.sem_inc(n_xrfree, 1)
            sp.sem_inc(n_xntfree, 1)

            def step(s, last=False):
                if not last:
                    sp.wait_ge(n_xfree, s + 1)
                    sp.dma_start(xb[:], x_s[bass.ds(s + 1, 1)].rearrange("o p j f -> (o p) j f")).then_inc(n_x, 16)
                sp.wait_ge(n_xr, s + 1)
                sp.dma_start(acc_s[bass.ds(s, 1)].rearrange("o p j f -> (o p) j f"), xr[:]).then_inc(n_xrst, 16)
                sp.wait_ge(n_xnt, 4 * s + 4)
                for k in range(KD):
                    sp.dma_start(xnt_s[bass.ds(s, 1), :, k].rearrange("o p j c -> (o p) j c"),
                                 xnt[:, k, :].rearrange("p (j c) -> p j c", j=SUP)).then_inc(n_xntst, 16)
                sp.wait_ge(n_xrst, 16 * s + 16)
                sp.sem_inc(n_xrfree, 1)
                sp.wait_ge(n_xntst, 32 * s + 32)
                sp.sem_inc(n_xntfree, 1)
            with sp.Fori(0, SUPERS - 1) as s:
                step(s)
            step(SUPERS - 1, last=True)

        @block.gpsimd
        def _(pool):
            nc.gpsimd.memset(ones[:], 1.0).then_inc(n_const, 1)
            nc.gpsimd.memset(valid[:], 1.0).then_inc(n_const, 1)
            nc.gpsimd.memset(yh[:, :, D:D + 2], 1.0).then_inc(n_const, 1)
            pool.wait_ge(n_const, 3)
            nc.gpsimd.affine_select(out=valid[:], in_=valid[:], compare_op=ALU.is_ge, fill=0.0,
                                    base=N_NODES - 1, pattern=[[-P, TILES]], channel_multiplier=-1).then_inc(n_const, 1)
            pool.wait_ge(n_const, 4)
            iota = lambda *a, **k: nc.gpsimd.iota(*a, allow_small_or_imprecise_dtypes=True, **k)
            for s in range(SUPERS):
                pool.wait_ge(n_xn, s + 1)
                pool.wait_ge(n_xrfree, s + 1)
                nc.gpsimd.tensor_tensor(xr[:], xb[:], xn[:], ALU.add).then_inc(n_xr, 1)
                pool.wait_ge(n_xr, s + 1)
                pool.sem_inc(n_xfree, 1)
                for r in range(s, STILES, SUPERS):
                    for k in range(WROWS):
                        pool.indirect_dma_start(keep["gathered"][:, r, k * EROW:(k + 1) * EROW, :].rearrange("p n c -> p (n c)"),
                                                None, d["edges"],
                                                bass.IndirectOffsetOnAxis(ap=keep["window"][:, r, k:k + 1], axis=0))\
                            .then_inc(n_gather, 16)
            iota(keep["keybase"][:], [[GC, STILES * P], [0, CHUNKS]], base=0, channel_multiplier=0).then_inc(n_const, 1)
            iota(keep["iota_key"][:], [[1, GC]], base=0, channel_multiplier=0).then_inc(n_const, 1)
            iota(keep["iota_lo"][:], [[1, P], [0, GROUPS * CHUNKS]], base=0, channel_multiplier=0).then_inc(n_const, 1)
            pool.wait_ge(n_const, 7)
            pool.wait_ge(n_gather, 16 * STILES * WROWS)

        @block.scalar
        def _(act):
            def stdev(s):
                act.wait_ge(n_var, s + 1)
                nc.scalar.activation(std[:], meanvar[:, :, 1], ACT.Sqrt, bias=eps[:]).then_inc(n_std, 1)
            stdev(0)
            act.wait_ge(n_w, 96)
            act.wait_ge(n_b, 32)
            for i, w in enumerate((wyk[:, :, 0:D], w1r[:], w2lr[:, :, 0:D])):
                nc.scalar.activation(squares[:, i, :].rearrange("p (k n) -> p k n", k=KD), w, ACT.Square,
                                     accum_out=sumsq[:, i:i + 1]).then_inc(n_sq, 1)
            nc.scalar.activation(squares[:, 3, 0:D], b1[:], ACT.Square, accum_out=sumsq[:, 3:4]).then_inc(n_sq, 1)
            act.wait_ge(n_sums, 1)
            act.wait_ge(n_sq, 4)
            nc.scalar.activation(norms[:, 0:3], pt[0][:, 0:3], ACT.Sqrt).then_inc(n_norm, 1)
            nc.scalar.activation(norms[:, 3:4], sumsq[:, 3:4], ACT.Sqrt).then_inc(n_norm, 1)

            def step(s, last=False):
                act.wait_ge(n_xntfree, s + 1)
                for b in range(4):
                    k, half = b // 2, b % 2
                    act.wait_ge(n_tr, 4 * s + b + 1)
                    w = (4, 3)[half] * P
                    nc.scalar.activation(xnt[:, k, half * 4 * P:half * 4 * P + w], pt[half][:, 0:w], ACT.Copy)\
                      .then_inc(n_xnt, 1)
                for j in range(SUP):
                    act.wait_ge(n_yk, s * SUP + (j + 1))
                    nc.scalar.activation(yh[:, bass.ds(s * SUP + j, 1), 0:D].rearrange("p o f -> p (o f)"),
                                         pyk[j % 2][:, 0:D], ACT.Copy, scale=1.0 / LO_SCALE).then_inc(n_yh, 1)
                    nc.scalar.activation(vbuf[:, j, :, 0:P],
                                         pv[j % 2][:, 0:D].rearrange("p (k f) -> p k f", k=KD),
                                         ACT.Copy).then_inc(n_v, 1)
                    act.wait_ge(n_kmin, s * SUP + (j + 1))
                    nc.scalar.activation(kexp[:, j % 2, :], kmin[:, j % 2, :], ACT.Exp).then_inc(n_kexp, 1)
                    if j == NEXT and not last:
                        stdev(s + 1)
            with act.Fori(0, SUPERS - 1) as s:
                step(s)
            step(SUPERS - 1, last=True)

        @block.vector
        def _(dve):
            def layernorm(s):
                dve.wait_ge(n_x, 16 * s + 16)
                for j in range(SUP):
                    last = nc.vector.bn_stats(stats[:, j, :], xb[:, j, :])
                last.then_inc(n_stats, 1)
                dve.wait_ge(n_stats, s + 1)
                dve.sem_inc(keep["turn"], 1)
                for j in range(SUP):
                    last = nc.vector.bn_aggr(meanvar[:, j, :], stats[:, j, :])
                last.then_inc(n_var, 1)
                dve.wait_ge(n_std, s + 1)
                nc.vector.reciprocal(rstd[:], std[:]).then_inc(n_rstd, 1)
                dve.wait_ge(n_rstd, s + 1)
                for j in range(SUP):
                    last = nc.vector.tensor_scalar(xn[:, j, :], xb[:, j, :], meanvar[:, j, 0:1], rstd[:, j:j + 1],
                                                   ALU.subtract, ALU.mult)
                last.then_inc(n_xn, 1)

            def step(s, last=False):
                nc.vector.tensor_copy(vbuf[:, :, :, P:P + 1].rearrange("p j k o -> p j (k o)"),
                                      valid[:, bass.ds(s * SUP, SUP)].unsqueeze(2).to_broadcast([P, SUP, KD]))\
                  .then_inc(n_ones, 1)
                for j in range(SUP):
                    dve.wait_ge(n_yk, s * SUP + (j + 1))
                    dve.wait_ge(n_yh, s * SUP + (j + 1))
                    nc.vector.tensor_scalar(kmin[:, j % 2, :], pyk[j % 2][:, D:2 * D], 0.0, None, ALU.min)\
                      .then_inc(n_kmin, 1)
                    nc.vector.scalar_tensor_tensor(yl[:, bass.ds(s * SUP + j, 1), :].rearrange("p o f -> p (o f)"),
                                                   yh[:, bass.ds(s * SUP + j, 1), 0:D].rearrange("p o f -> p (o f)"),
                                                   -LO_SCALE, pyk[j % 2][:, 0:D], ALU.mult, ALU.add).then_inc(n_yl, 1)
                    dve.wait_ge(n_kexp, s * SUP + (j + 1))
                    nc.vector.scalar_tensor_tensor(kbuf[:, j, :], pyk[j % 2][:, D:2 * D], 0.0, kexp[:, j % 2, :],
                                                   ALU.max, ALU.add).then_inc(n_ykfree, 1)
                    if j == NEXT and not last:
                        layernorm(s + 1)
                dve.wait_ge(n_kv, s + 1)
                nc.vector.tensor_tensor(kvacc[:], pkv[:, 0:KD * (P + 1)].rearrange("p (k n) -> p k n", k=KD),
                                        kvacc[:], ALU.add).then_inc(n_kvacc, 1)
                dve.wait_ge(n_kvacc, s + 1)
            layernorm(0)
            dve.wait_ge(n_norm, 2)
            top = float(D) ** 0.5
            nc.vector.tensor_tensor(tmp[:, 0:1], norms[:, 0:1], norms[:, 1:2], ALU.add).then_inc(n_sc, 1)
            nc.vector.tensor_scalar(bnd[:, 0:1], norms[:, 0:1], top, None, ALU.mult).then_inc(n_sc, 1)
            dve.wait_ge(n_sc, 2)
            nc.vector.scalar_tensor_tensor(tmp[:, 1:2], tmp[:, 0:1], top, norms[:, 3:4], ALU.mult, ALU.add)\
              .then_inc(n_sc, 1)
            dve.wait_ge(n_sc, 3)
            nc.vector.tensor_tensor(bnd[:, 1:2], tmp[:, 1:2], norms[:, 2:3], ALU.mult).then_inc(n_sc, 1)
            dve.wait_ge(n_sc, 4)
            nc.vector.tensor_scalar(bnd[:], bnd[:], 1e-20, None, ALU.max).then_inc(n_sc, 1)
            dve.wait_ge(n_sc, 5)
            nc.vector.reciprocal(scale[:], bnd[:]).then_inc(n_sc, 1)
            dve.wait_ge(n_sc, 6)
            nc.vector.tensor_scalar(scale[:], scale[:], 2.0 ** 15 * LO_SCALE, None, ALU.mult).then_inc(n_sc, 1)
            dve.wait_ge(n_sc, 7)
            nc.vector.tensor_scalar(scale[:].bitcast(I32), scale[:].bitcast(I32), 0x7F800000, None,
                                    ALU.bitwise_and).then_inc(n_sc, 1)
            dve.wait_ge(n_sc, 8)
            nc.vector.reciprocal(rscale[:], scale[:]).then_inc(n_sc, 1)
            nc.vector.tensor_scalar(wyk[:, :, 0:D], wyk[:, :, 0:D], scale[:, 0:1], None, ALU.mult).then_inc(n_sc, 1)
            nc.vector.tensor_scalar(w2lr[:, :, 0:D], w2lr[:, :, 0:D], scale[:, 1:2], None, ALU.mult).then_inc(n_sc, 1)
            dve.wait_ge(n_sc, 11)
            nc.vector.tensor_scalar(unscale[:], rscale[:], LO_SCALE, None, ALU.mult).then_inc(n_sc, 1)
            dve.wait_ge(n_const, 4)
            dve.sem_inc(n_ykfree, 2)
            with dve.Fori(0, SUPERS - 1) as s:
                step(s)
            step(SUPERS - 1, last=True)

        @block.tensor
        def _(pe):
            pe.wait_ge(n_const, 1)
            pe.wait_ge(n_sq, 4)
            nc.tensor.matmul(pt[0][:, 0:3], ones[:], sumsq[:, 0:3], start=True, stop=True).then_inc(n_sums, 1)
            pe.wait_ge(n_norm, 2)
            with pe.Fori(0, SUPERS) as s:
                pe.wait_ge(n_xn, s + 1)
                for b in range(4):
                    k, half = b // 2, b % 2
                    if b >= 2:
                        pe.wait_ge(n_xnt, s * 4 + (b - 1))
                    for j in range(4 * half, min(4 * half + 4, SUP)):
                        last = nc.tensor.transpose(pt[half][:, (j % 4) * P:(j % 4 + 1) * P],
                                                   xn[:, j, k * P:(k + 1) * P], ident[:])
                    last.then_inc(n_tr, 1)
                pe.wait_ge(n_xnt, 4 * s + 4)
                pe.wait_ge(n_sc, 11)
                for j in range(SUP):
                    pe.wait_ge(n_ykfree, s * SUP + (j + 1))
                    for k in range(KD):
                        nc.tensor.matmul(pyk[j % 2][:], xnt[:, k, j * P:(j + 1) * P], wyk[:, k, :],
                                         start=(k == 0), stop=(k == KD - 1))
                    for k in range(KD):
                        last = nc.tensor.matmul(pv[j % 2][:, 0:D], xnt[:, k, j * P:(j + 1) * P],
                                                wv[:, k, :], start=(k == 0), stop=(k == KD - 1))
                    last.then_inc(n_yk, 1)
                pe.wait_ge(n_ykfree, s * SUP + (SUP + 2))
                pe.wait_ge(n_v, s * SUP + SUP)
                pe.wait_ge(n_ones, s + 1)
                for k in range(KD):
                    for j in range(SUP):
                        last = nc.tensor.matmul(pkv[:, k * (P + 1):(k + 1) * (P + 1)], kbuf[:, j, k * P:(k + 1) * P],
                                                vbuf[:, j, k, :], start=(j == 0), stop=(j == SUP - 1))
                last.then_inc(n_kv, 1)


def turn_phase(nc, sem, mem, d, keep):
    def sb(name, shape, dt):
        return mem.enter_context(nc.sbuf_tensor(name, shape, dt))

    ident, gathered, lo_all, key_all = (keep[k] for k in ("ident", "gathered", "lo_all", "key_all"))
    keybase = keep["keybase"]
    late = sb("late", [P, STILES * P], F32)
    missed = sb("missed", [P, 1], F32)
    pt = [mem.enter_context(nc.psum_tensor(f"t_pt{i}", [P, 512], F32)) for i in range(4)]
    c_turned, c_taken = sem("c_turned"), sem("c_taken")
    c_late = sem("c_late")

    with nc.Block() as block:
        @block.sync
        def _(sp):
            pass

        @block.gpsimd
        def _(pool):
            pass

        @block.scalar
        def _(act):
            pass

        @block.tensor
        def _(pe):
            for r in range(STILES):
                if r >= 2:
                    pe.wait_ge(c_taken, r - 1)
                for c in range(CHUNKS):
                    for i in range(2):
                        last = nc.tensor.transpose(pt[2 * (r % 2) + i][:, c * P:(c + 1) * P],
                                                   gathered[:, r, c * P:(c + 1) * P, i], ident[:])
                last.then_inc(c_turned, 1)

        @block.vector
        def _(dve):
            for r in range(STILES):
                dve.wait_ge(c_turned, r + 1)
                here = slice(r * P, (r + 1) * P)
                nc.vector.tensor_copy(lo_all[:, here, :], pt[2 * (r % 2)][:, 0:GE].rearrange("p (c g) -> p g c", g=P))
                nc.vector.tensor_tensor(key_all[:, here, :], pt[2 * (r % 2) + 1][:, 0:GE].rearrange("p (c g) -> p g c", g=P),
                                        keybase[:, here, :], ALU.subtract).then_inc(c_taken, 1)
            dve.wait_ge(c_taken, STILES)
            nc.vector.tensor_scalar(late[:], key_all[:, :, CHUNKS - 1], -(GC - 1) / 2.0, None, ALU.add)\
              .then_inc(c_late, 1)
            dve.wait_ge(c_late, 1)
            nc.vector.tensor_tensor(late[:], late[:], late[:], ALU.mult).then_inc(c_late, 1)
            dve.wait_ge(c_late, 2)
            nc.vector.tensor_scalar(late[:], late[:], (GC / 2.0) ** 2, 0.0, ALU.is_lt, ALU.add,
                                    accum_out=missed[:]).then_inc(c_late, 1)
            dve.wait_ge(c_late, 3)
            nc.vector.scalar_tensor_tensor(keep["uncovered"][:], missed[:], ident[:, P - 1:P], keep["uncovered"][:],
                                           ALU.mult, ALU.add).then_inc(c_late, 1)
            dve.wait_ge(c_late, 4)


def aggregate(pe, nc, keep, s, part, q, ph, pl, yh, yl, cols, t):
    pe.wait_ge(s["part"][q], t * 16 + 16)
    pe.wait_ge(s["bankfree"][q], t + 1)
    pe.sem_inc(keep["turn"], 1)
    h0, h1 = SPLIT[q], SPLIT[q + 1]
    for h in range(h0, h1):
        nc.tensor.matmul(ph[q][:, 0:cols], part[q][:, h - h0, :], yh[:, h, 0:cols], start=(h == h0), stop=(h == h1 - 1))
        last = nc.tensor.matmul(pl[q][:, 0:D], part[q][:, h - h0, :], yl[:, h, :], start=(h == h0), stop=(h == h1 - 1))
    last.then_inc(s["summed"][q], 1)


def load_parts(sp, s, d, part, t):
    for q in range(2):
        sp.wait_ge(s["summed"][q], t + 1)
        sp.dma_start(part[q][:].rearrange("p h n -> p (h n)").bitcast(I32),
                     d["adj"][bass.ds(t, 1), :, SPLIT[q] * P // 4:SPLIT[q + 1] * P // 4].rearrange("o p c -> (o p) c"))\
          .then_inc(s["part"][q], 16)


def aggregation_semaphores(sem, p):
    pair = lambda n: [sem(f"{p}_{n}{q}") for q in range(2)]
    return dict(part=pair("part"), summed=pair("summed"), bankfree=pair("bankfree"),
                comb=sem(f"{p}_comb"))


def combine(dve, nc, s, ph, pl, first, total, cols, t):
    dve.wait_ge(s["summed"][0], t + 2)
    nc.vector.tensor_copy(first[:, 0:cols], ph[0][:, 0:cols]).then_inc(s["comb"], 1)
    dve.wait_ge(s["comb"], t * 4 + 1)
    nc.vector.scalar_tensor_tensor(first[:, 0:D], pl[0][:, 0:D], 1.0 / LO_SCALE, first[:, 0:D], ALU.mult, ALU.add)\
      .then_inc(s["comb"], 1)
    dve.wait_ge(s["comb"], t * 4 + 2)
    dve.sem_inc(s["bankfree"][0], 1)
    dve.wait_ge(s["summed"][1], t + 2)
    nc.vector.tensor_tensor(total[:, 0:cols], ph[1][:, 0:cols], first[:, 0:cols], ALU.add).then_inc(s["comb"], 1)
    dve.wait_ge(s["comb"], t * 4 + 3)
    nc.vector.scalar_tensor_tensor(total[:, 0:D], pl[1][:, 0:D], 1.0 / LO_SCALE, total[:, 0:D], ALU.mult, ALU.add)\
      .then_inc(s["comb"], 1)
    dve.wait_ge(s["comb"], t * 4 + 4)
    dve.sem_inc(s["bankfree"][1], 1)


def layer1_phase(nc, sem, mem, d, keep):
    def sb(name, shape, dt):
        return mem.enter_context(nc.sbuf_tensor(name, shape, dt))

    ident, lo_all, key_all, yh, yl, y2h, y2l, w1r, w2lr, b1, b2, rdeg, unscale = (keep[k] for k in (
        "ident", "lo_all", "key_all", "yh", "yl", "y2h", "y2l", "w1r", "w2lr", "b1", "b2", "rdeg", "unscale"))
    iota_key, iota_lo = keep["iota_key"], keep["iota_lo"]
    key = sb("key", [P, GROUPS, CHUNKS], F32)
    hot_key = sb("hot_key", [P, ONEHOTS, CHUNKS, GC], F16)
    hot_lo = [sb(f"hot_lo{i}", [P, P, GROUPS * CHUNKS], F16) for i in range(2)]
    counts = [sb(f"counts{i}", [P, TILES, P], F8) for i in range(2)]
    total = sb("total", [P, D + 2], F32)
    acc_in, acc_out = sb("acc_in", [P, D], F32), sb("acc_out", [P, D], F32)
    xt = sb("xt", [P, KD, P], F32)
    rsum = sb("rsum", [P, 2], F32)
    h0 = sb("h0", [P, D], F32)
    h = sb("h", [P, D], F32)
    ht = sb("ht", [P, KD, P], F32)
    seen = sb("seen", [P, TILES * P // 4], I32)
    large = hot_lo[0][:].rearrange("p n g -> p (n g)").bitcast(F32)[:, 0:TILES * P // 4]
    faults = sb("faults", [P, 2], F32)
    ones = sb("g_ones", [P, 1], F32)
    ps = lambda n: mem.enter_context(nc.psum_tensor(n, [P, 512], F32))
    pc = [ps(f"pc{i}") for i in range(BANKS)]
    ph, pl, pr, ptr, py2 = ps("ph"), ps("pl"), ps("pr"), ps("ptr"), ps("py2")

    c_keys = sem("c_keys")
    c_hot = sem("c_hot")
    c_group = sem("c_group")
    c_evac = sem("c_evac")
    c_stored = sem("c_stored")
    c_saved, g_seen, g_summed, g_bankfree, g_root, g_accfree, g_y2free, g_outfree = (sem(n) for n in (
        "c_saved", "g_seen", "g_summed", "g_bankfree", "g_root", "g_accfree", "g_y2free", "g_outfree"))
    g_xt, g_acc, g_stored = sem("g_xt"), sem("g_acc"), sem("g_stored")
    g_h, g_tr, g_ht, g_y2, g_y2h, g_out = (sem(f"g_{n}") for n in ("h", "tr", "ht", "y2", "y2h", "out"))
    g_step, g_tail = sem("g_step"), sem("g_tail")
    g_fault, g_sum = sem("g_fault"), sem("g_sum")
    SUMS, TURN, ROOT, PROJECT = 0, 6, 7, 10
    HEAD, LOOK, LOWS = 3, 7, 10
    sums_of = [range(TILES * i // (GROUPS - SUMS), TILES * (i + 1) // (GROUPS - SUMS)) for i in range(GROUPS - SUMS)]

    def over_tiles(eng, step):
        step(0, 0, first=True)
        step(1, 1)
        with eng.Fori(1, TILES // 2) as i:
            step(i * 2, 0)
            step(i * 2 + 1, 1)
        step(TILES - 1, 0, last=True)

    with nc.Block() as block:
        @block.sync
        def _(sp):
            sp.sem_inc(c_saved, 1)
            sp.sem_inc(g_outfree, 1)

            def fetch_xt(t):
                sp.wait_ge(g_root, t + 1)
                sp.dma_start(xt[:], d["xnt"][bass.ds(t, 1)].rearrange("o p k c -> (o p) k c")).then_inc(g_xt, 16)

            def fetch_acc(t):
                sp.wait_ge(g_accfree, t + 1)
                sp.dma_start(acc_in[:], d["acc"][bass.ds(t * P, P), :]).then_inc(g_acc, 16)

            def store_acc(t):
                sp.wait_ge(g_out, t + 1)
                sp.dma_start(d["acc"][bass.ds(t * P, P), :], acc_out[:]).then_inc(g_stored, 16)
                sp.wait_ge(g_stored, t * 16 + 16)
                sp.sem_inc(g_outfree, 1)

            def step(t, b, first=False, last=False):
                sp.wait_ge(c_evac, t * GROUPS + (BANKS + GROUPS))
                sp.dma_start(d["adj"][bass.ds(t, 1)].rearrange("o p c -> (o p) c"),
                             counts[b][:].rearrange("p a b -> p (a b)").bitcast(I32)).then_inc(c_stored, 16)
                sp.wait_ge(c_stored, t * 16 + 16)
                sp.sem_inc(c_saved, 1)
                if not last:
                    fetch_xt(t + 1)
                if not first:
                    store_acc(t - 1)
                    fetch_acc(t)
            fetch_xt(0)
            fetch_acc(0)
            over_tiles(sp, step)
            store_acc(TILES - 1)

        @block.gpsimd
        def _(pool):
            pass

        @block.tensor
        def _(pe):
            pe.sem_inc(c_group, ONEHOTS)
            pe.sem_inc(g_summed, 1)
            pe.sem_inc(g_root, 1)

            def multiply(t, b, g):
                pe.wait_ge(c_hot, t * GROUPS + (g + 1))
                pe.wait_ge(c_evac, t * GROUPS + (g + 1))
                for c in range(CHUNKS):
                    last = nc.tensor.matmul(pc[g % BANKS][:, 0:GC], hot_lo[b][:, :, g * CHUNKS + c],
                                            hot_key[:, g % ONEHOTS, c, :], start=(c == 0), stop=(c == CHUNKS - 1))
                last.then_inc(c_group, 1)

            def sums(t, b, part):
                if part == 0:
                    pe.wait_ge(c_evac, t * GROUPS + (BANKS + GROUPS))
                    pe.wait_ge(g_bankfree, t + 1)
                    pe.sem_inc(keep["turn"], 1)
                for hi in sums_of[part]:
                    nc.tensor.matmul(ph[:, 0:D + 2], counts[b][:, hi, :], yh[:, hi, :], start=(hi == 0), stop=(hi == TILES - 1))
                    last = nc.tensor.matmul(pl[:, 0:D], counts[b][:, hi, :], yl[:, hi, :],
                                            start=(hi == 0), stop=(hi == TILES - 1))
                if part == len(sums_of) - 1:
                    last.then_inc(g_summed, 1)

            def turn(t):
                pe.wait_ge(g_h, t + 1)
                for k in range(KD):
                    last = nc.tensor.transpose(ptr[:, k * P:(k + 1) * P], h[:, k * P:(k + 1) * P], ident[:])
                last.then_inc(g_tr, 1)

            def root(t):
                pe.wait_ge(g_xt, t * 16 + 16)
                for k in range(KD):
                    last = nc.tensor.matmul(pr[:, 0:D], xt[:, k, :], w1r[:, k, :], start=(k == 0), stop=(k == KD - 1))
                last.then_inc(g_root, 1)

            def project(t):
                pe.wait_ge(g_ht, t + 1)
                pe.wait_ge(g_y2free, t + 1)
                for k in range(KD):
                    last = nc.tensor.matmul(py2[:], ht[:, k, :], w2lr[:, k, :], start=(k == 0), stop=(k == KD - 1))
                last.then_inc(g_y2, 1)

            def step(t, b, first=False, last=False):
                for g in range(GROUPS):
                    if not last:
                        multiply(t + 1, 1 - b, g)
                    if g >= SUMS:
                        sums(t, b, g - SUMS)
                    if g == TURN and not first:
                        turn(t - 1)
                    if g == ROOT:
                        root(t)
                    if g == PROJECT and not first:
                        project(t - 1)
            for g in range(GROUPS):
                multiply(0, 0, g)
            over_tiles(pe, step)
            turn(TILES - 1)
            project(TILES - 1)
            pe.wait_ge(g_fault, 5)
            nc.tensor.matmul(pr[0:1, 0:1], faults[:, 1:2], ones[:], start=True, stop=True).then_inc(g_sum, 1)

        @block.scalar
        def _(act):
            act.sem_inc(c_evac, BANKS)

            def evacuate(t, b, groups):
                for g in groups:
                    act.wait_ge(c_group, t * GROUPS + (ONEHOTS + g + 1))
                    act.sem_inc(keep["turn"], 1)
                    nc.scalar.activation(counts[b][:, :, g * GN:(g + 1) * GN].rearrange("p h n -> p n h"),
                                         pc[g % BANKS][:, 0:GC].rearrange("p (n h) -> p n h", n=GN),
                                         ACT.Copy, scale=1.0 / CSCALE, saturate=False).then_inc(c_evac, 1)

            def copy_turned(t):
                act.wait_ge(g_tr, t + 1)
                nc.scalar.activation(ht[:].rearrange("p k c -> p (k c)"), ptr[:, 0:D], ACT.Copy).then_inc(g_ht, 1)

            def high_half(t):
                act.wait_ge(g_y2, t + 1)
                nc.scalar.activation(y2h[:, bass.ds(t, 1), :].rearrange("p o f -> p (o f)"), py2[:, 0:D],
                                     ACT.Copy, scale=1.0 / LO_SCALE).then_inc(g_y2h, 1)

            def step(t, b, first=False, last=False):
                if not last:
                    act.wait_ge(g_summed, t + 1)
                    act.wait_ge(c_saved, t + 1)
                    act.wait_ge(g_seen, t + 1)
                    evacuate(t + 1, 1 - b, range(0, TURN + 1))
                if not first:
                    copy_turned(t - 1)
                if not last:
                    evacuate(t + 1, 1 - b, range(TURN + 1, PROJECT + 1))
                if not first:
                    high_half(t - 1)
                if not last:
                    evacuate(t + 1, 1 - b, range(PROJECT + 1, GROUPS))
            evacuate(0, 0, range(GROUPS))
            over_tiles(act, step)
            copy_turned(TILES - 1)
            high_half(TILES - 1)

        @block.vector
        def _(dve):
            for s in (g_bankfree, g_accfree, g_y2free):
                dve.sem_inc(s, 1)
            nc.vector.memset(ones[:], 1.0).then_inc(g_fault, 1)
            nc.vector.memset(seen[:], 0).then_inc(g_seen, 1)

            def lows(t, b):
                nc.vector.tensor_tensor(hot_lo[b][:], iota_lo[:],
                                        lo_all[:, bass.ds(t * GROUPS, GROUPS), :].rearrange("p g c -> p (g c)")
                                        .unsqueeze(1).to_broadcast([P, P, GROUPS * CHUNKS]), ALU.is_equal)

            def keys(t):
                nc.vector.tensor_copy(key[:], key_all[:, bass.ds(t * GROUPS, GROUPS), :]).then_inc(c_keys, 1)
                dve.wait_ge(c_keys, t + 1)

            def onehots(t, g):
                dve.wait_ge(c_group, t * GROUPS + (g + 1))
                for c in range(CHUNKS):
                    last = nc.vector.tensor_scalar(hot_key[:, g % ONEHOTS, c, :], iota_key[:], key[:, g, c:c + 1],
                                                   None, ALU.is_equal)
                last.then_inc(c_hot, 1)
                if g == GROUPS - 1:
                    dve.wait_ge(c_hot, t * GROUPS + GROUPS)

            def look(t, b):
                dve.wait_ge(c_evac, t * GROUPS + (BANKS + GROUPS))
                dve.wait_ge(g_seen, t + 1)
                nc.vector.tensor_tensor(seen[:], seen[:], counts[b][:].rearrange("p h n -> p (h n)").bitcast(I32),
                                        ALU.bitwise_or).then_inc(g_seen, 1)

            def head(t):
                dve.wait_ge(g_summed, t + 2)
                nc.vector.tensor_copy(total[:], ph[:, 0:D + 2]).then_inc(g_step, 1)
                dve.wait_ge(g_step, t * 8 + 1)
                nc.vector.scalar_tensor_tensor(total[:, 0:D], pl[:, 0:D], 1.0 / LO_SCALE, total[:, 0:D], ALU.mult, ALU.add)\
                  .then_inc(g_step, 1)
                nc.vector.tensor_scalar(rsum[:, 0:1], total[:, D:D + 1], CSCALE, 1.0, ALU.mult, ALU.max).then_inc(g_step, 1)
                dve.wait_ge(g_step, t * 8 + 3)
                dve.sem_inc(g_bankfree, 1)
                nc.vector.reciprocal(rsum[:, 1:2], rsum[:, 0:1]).then_inc(g_step, 1)
                dve.wait_ge(g_step, t * 8 + 4)
                nc.vector.tensor_scalar(rsum[:, 0:1], rsum[:, 1:2], unscale[:, 0:1], CSCALE, ALU.mult, ALU.mult).then_inc(g_step, 1)
                nc.vector.tensor_scalar(rdeg[:, bass.ds(t, 1)], rsum[:, 1:2], unscale[:, 1:2], CSCALE, ALU.mult, ALU.mult)\
                  .then_inc(g_step, 1)
                dve.wait_ge(g_step, t * 8 + 6)
                nc.vector.scalar_tensor_tensor(h0[:], total[:, 0:D], rsum[:, 0:1], b1[:], ALU.mult, ALU.add)\
                  .then_inc(g_step, 1)
                dve.wait_ge(g_step, t * 8 + 7)
                dve.wait_ge(g_root, t + 2)
                nc.vector.tensor_tensor(h0[:], pr[:, 0:D], h0[:], ALU.add).then_inc(g_step, 1)
                dve.wait_ge(g_step, t * 8 + 8)
                nc.vector.tensor_scalar(h[:], h0[:], 0.0, None, ALU.max).then_inc(g_h, 1)

            def tail(t):
                dve.wait_ge(g_y2h, t + 1)
                nc.vector.scalar_tensor_tensor(y2l[:, bass.ds(t, 1), :].rearrange("p o f -> p (o f)"),
                                               y2h[:, bass.ds(t, 1), :].rearrange("p o f -> p (o f)"),
                                               -LO_SCALE, py2[:, 0:D], ALU.mult, ALU.add).then_inc(g_tail, 1)
                dve.wait_ge(g_acc, t * 16 + 16)
                dve.wait_ge(g_outfree, t + 1)
                nc.vector.tensor_tensor(acc_out[:], py2[:, D:2 * D], acc_in[:], ALU.add).then_inc(g_tail, 1)
                dve.wait_ge(g_tail, t * 2 + 2)
                dve.sem_inc(g_accfree, 1)
                dve.sem_inc(g_y2free, 1)
                nc.vector.tensor_tensor(acc_out[:], acc_out[:], b2[:], ALU.add).then_inc(g_out, 1)

            def step(t, b, first=False, last=False):
                if not last:
                    keys(t + 1)
                for g in range(GROUPS):
                    if g == HEAD and not first:
                        head(t - 1)
                    if g == LOOK:
                        look(t, b)
                    if g == LOWS and not last:
                        lows(t + 2, b)
                    if not last:
                        onehots(t + 1, g)
                if not first:
                    tail(t - 1)
            lows(0, 0)
            lows(1, 1)
            keys(0)
            for g in range(GROUPS):
                onehots(0, g)
            over_tiles(dve, step)
            head(TILES - 1)
            tail(TILES - 1)
            dve.wait_ge(g_seen, TILES + 1)
            nc.vector.tensor_scalar(seen[:], seen[:], 0x40404040, None, ALU.bitwise_and).then_inc(g_fault, 1)
            dve.wait_ge(g_fault, 2)
            nc.vector.tensor_copy(large, seen[:]).then_inc(g_fault, 1)
            dve.wait_ge(g_fault, 3)
            nc.vector.tensor_scalar(large, large, 0.0, 0.0, ALU.is_gt, ALU.add,
                                    accum_out=faults[:, 0:1]).then_inc(g_fault, 1)
            dve.wait_ge(g_fault, 4)
            nc.vector.tensor_tensor(faults[:, 1:2], faults[:, 0:1], keep["uncovered"][:], ALU.add).then_inc(g_fault, 1)
            dve.wait_ge(g_sum, 1)
            nc.vector.tensor_scalar(faults[0:1, 0:1], pr[0:1, 0:1], 1.0, None, ALU.min).then_inc(g_fault, 1)
            dve.wait_ge(g_fault, 6)
            nc.vector.tensor_copy(keep["flag"][:], faults[0:1, 0:1]).then_inc(g_fault, 1)
            dve.wait_ge(g_fault, 7)


def layer2_phase(nc, sem, mem, d, keep):
    y2h, y2l, rdeg = keep["y2h"], keep["y2l"], keep["rdeg"]
    part = [mem.enter_context(nc.sbuf_tensor(f"part{q}", [P, SPLIT[q + 1] - SPLIT[q], P], F8)) for q in range(2)]
    first, total, acc_in, acc_out = (mem.enter_context(nc.sbuf_tensor(f"h_{n}", [P, D], F32)) for n in (
        "first", "total", "acc_in", "acc_out"))
    ph, pl = ([mem.enter_context(nc.psum_tensor(f"h_{n}{q}", [P, 512], F32)) for q in range(2)] for n in ("ph", "pl"))
    s = aggregation_semaphores(sem, "h")
    h_acc, h_accfree, h_out, h_outfree = (sem(f"h_{k}") for k in ("acc", "accfree", "out", "outfree"))
    h_stored = sem("h_stored", pool_dma=True)

    with nc.Block() as block:
        @block.sync
        def _(sp):
            with sp.Fori(0, TILES) as t:
                load_parts(sp, s, d, part, t)
                sp.wait_ge(h_accfree, t + 1)
                sp.dma_start(acc_in[:], d["acc"][bass.ds(t * P, P), :]).then_inc(h_acc, 16)

        @block.gpsimd
        def _(pool):
            pool.sem_inc(h_outfree, 1)
            with pool.Fori(0, TILES) as t:
                pool.wait_ge(h_out, t + 1)
                pool.dma_start(d["acc"][bass.ds(t * P, P), :], acc_out[:]).then_inc(h_stored, 16)
                pool.wait_ge(h_stored, t * 16 + 16)
                pool.sem_inc(h_outfree, 1)

        @block.tensor
        def _(pe):
            for q in range(2):
                pe.sem_inc(s["summed"][q], 1)
            with pe.Fori(0, TILES) as t:
                for q in range(2):
                    aggregate(pe, nc, keep, s, part, q, ph, pl, y2h, y2l, D, t)

        @block.vector
        def _(dve):
            for q in range(2):
                dve.sem_inc(s["bankfree"][q], 1)
            dve.sem_inc(h_accfree, 1)
            with dve.Fori(0, TILES) as t:
                combine(dve, nc, s, ph, pl, first, total, D, t)
                dve.wait_ge(h_acc, t * 16 + 16)
                dve.wait_ge(h_outfree, t + 1)
                nc.vector.scalar_tensor_tensor(acc_out[:], total[:, 0:D], rdeg[:, bass.ds(t, 1)], acc_in[:],
                                               ALU.mult, ALU.add).then_inc(h_out, 1)
                dve.wait_ge(h_out, t + 1)
                dve.sem_inc(h_accfree, 1)

        @block.scalar
        def _(act):
            pass


def general_phase(nc, sem, mem, d, t_in, keep):
    def sb(name, shape, dt=F32):
        return mem.enter_context(nc.sbuf_tensor(name, shape, dt))

    ident = keep["ident"]
    src_i = sb("x_src", [EP, ELEN], I32)
    dst_i = sb("x_dst", [EP, ELEN], I32)
    dst_f = sb("x_dstf", [EP, ELEN])
    tbase = sb("x_tbase", [EP, TILES])
    iota_t = sb("x_iota", [EP, P])
    rel = sb("x_rel", [EP, TILES])
    col = sb("x_col", [EP, 1], I32)
    feat = sb("x_feat", [EP, D + 1])
    hot = sb("x_hot", [EP, SUP, P])
    agg = sb("x_agg", [P, TILES, D + 1])
    wl, wr = sb("x_wl", [P, 2, KD, D]), sb("x_wr", [P, 2, KD, D])
    bias = sb("x_bias", [P, 2, D])
    deg = sb("x_deg", [P, TILES])
    mean, own, turned = sb("x_mean", [P, D]), sb("x_own", [P, D]), sb("x_turned", [P, 2 * KD, P])
    xin, base = sb("x_in", [P, D]), sb("x_base", [P, D])
    res = sb("x_res", [P, D])
    bank = [mem.enter_context(nc.psum_tensor(f"x_bank{i}", [P, 512], F32)) for i in range(SUP)]

    x_const, x_load = sem("x_const"), sem("x_load")
    x_in, x_back, x_rows, x_rowst = sem("x_in"), sem("x_back"), sem("x_rows"), sem("x_rowst")
    x_col, x_hot, x_prod, x_sum = ([sem(f"x_{n}{i}") for i in range(2)] for n in ("col", "hot", "prod", "sum"))
    x_gather = [sem(f"x_gather{i}", pool_dma=True) for i in range(2)]
    x_mean, x_tile, x_turn, x_turned, x_out, x_res, x_stored = ([sem(f"x_{n}{i}") for i in range(2)] for n in (
        "mean", "tile", "turn", "turned", "out", "res", "stored"))
    kb = lambda w: w.rearrange("(k p) n -> p k n", p=P)
    rows_of = lambda table, t: table[bass.ds(t * P, P), :]
    tables = [d["feat1"], d["feat2"]]
    results = [d["feat2"], d["acc"]]

    with nc.Block() as block:
        @block.sync
        def _(sp):
            with sp.If(sp.value_load(keep["flag"][0:1, 0:1], min_val=0, max_val=1) > 0):
                sp.dma_start(src_i[:], t_in["src"].rearrange("(p n) -> p n", p=EP)).then_inc(x_load, 16)
                sp.dma_start(dst_i[:], t_in["dst"].rearrange("(p n) -> p n", p=EP)).then_inc(x_load, 16)
                for i, n in enumerate(("1", "2")):
                    sp.dma_start(wl[:, i], kb(t_in[f"gnn_W{n}_l"])).then_inc(x_load, 16)
                    sp.dma_start(wr[:, i], kb(t_in[f"gnn_W{n}_r"])).then_inc(x_load, 16)
                    sp.dma_start(bias[:, i], t_in[f"gnn_b{n}"].unsqueeze(0).to_broadcast([P, D])).then_inc(x_load, 16)
                with sp.Fori(0, TILES) as t:
                    sp.dma_start(turned[:, 0:KD, :], d["xnt"][bass.ds(t, 1)].rearrange("o p k c -> (o p) k c"))\
                      .then_inc(x_in, 16)
                    sp.wait_ge(x_rows, t + 1)
                    sp.sem_inc(keep["turn"], 1)
                    sp.dma_start(rows_of(d["feat1"], t), own[:]).then_inc(x_rowst, 16)
                    sp.wait_ge(x_rowst, t * 16 + 16)
                    sp.sem_inc(keep["turn"], 1)
                for i in range(2):
                    with sp.Fori(0, TILES) as t:
                        sp.wait_ge(x_mean[i], t + 1)
                        sp.sem_inc(keep["turn"], 1)
                        sp.dma_start(own[:], rows_of(tables[i], t)).then_inc(x_tile[i], 16)
                        sp.dma_start(base[:], rows_of(d["feat1"], t)).then_inc(x_tile[i], 16)
                        sp.dma_start(xin[:], rows_of(t_in["x"], t)).then_inc(x_tile[i], 16)
                        sp.wait_ge(x_res[i], t * 3 + 3)
                        sp.sem_inc(keep["turn"], 1)
                        sp.dma_start(rows_of(results[i], t), res[:]).then_inc(x_stored[i], 16)
                        sp.wait_ge(x_stored[i], t * 16 + 16)
                        sp.sem_inc(keep["turn"], 1)

        @block.gpsimd
        def _(pool):
            with pool.If(pool.value_load(keep["flag"][0:1, 0:1], min_val=0, max_val=1) > 0):
                nc.gpsimd.iota(tbase[:], [[-P, TILES]], base=0, channel_multiplier=0,
                               allow_small_or_imprecise_dtypes=True).then_inc(x_const, 1)
                nc.gpsimd.iota(iota_t[:], [[1, P]], base=0, channel_multiplier=0,
                               allow_small_or_imprecise_dtypes=True).then_inc(x_const, 1)
                nc.gpsimd.memset(feat[:, D:D + 1], 1.0).then_inc(x_const, 1)
                pool.wait_ge(x_const, 3)
                pool.wait_ge(x_rowst, 16 * TILES)
                for i in range(2):
                    if i:
                        pool.wait_ge(x_stored[0], 16 * TILES)
                    with pool.Fori(0, ELEN) as c:
                        pool.wait_ge(x_col[i], c + 1)
                        pool.sem_inc(keep["turn"], 1)
                        pool.indirect_dma_start(feat[:, 0:D], None, tables[i],
                                                bass.IndirectOffsetOnAxis(ap=col[:, 0:1], axis=0)).then_inc(x_gather[i], 16)

        @block.tensor
        def _(pe):
            with pe.If(pe.value_load(keep["flag"][0:1, 0:1], min_val=0, max_val=1) > 0):
                with pe.Fori(0, TILES) as t:
                    pe.wait_ge(x_in, t * 16 + 16)
                    for k in range(KD):
                        last = nc.tensor.transpose(bank[0][:, k * P:(k + 1) * P], turned[:, k, :], ident[:])
                    last.then_inc(x_back, 1)
                for i in range(2):
                    with pe.Fori(0, ELEN) as c:
                        pe.wait_ge(x_gather[i], c * 16 + 16)
                        for b in range(SUPERS):
                            pe.wait_ge(x_hot[i], c * SUPERS + (b + 1))
                            for j in range(SUP):
                                last = nc.tensor.matmul(bank[j][:, 0:D + 1], hot[:, j, :], feat[:], start=True, stop=True)
                            last.then_inc(x_prod[i], 1)
                    with pe.Fori(0, TILES) as t:
                        pe.wait_ge(x_mean[i], t + 1)
                        pe.wait_ge(x_tile[i], t * 48 + 48)
                        for k in range(KD):
                            nc.tensor.transpose(bank[0][:, k * P:(k + 1) * P], mean[:, k * P:(k + 1) * P], ident[:])
                            last = nc.tensor.transpose(bank[0][:, (KD + k) * P:(KD + k + 1) * P],
                                                       own[:, k * P:(k + 1) * P], ident[:])
                        last.then_inc(x_turn[i], 1)
                        pe.wait_ge(x_turned[i], t + 1)
                        for k in range(2 * KD):
                            w = wl if k < KD else wr
                            last = nc.tensor.matmul(bank[1][:, 0:D], turned[:, k, :], w[:, i, k % KD, :],
                                                    start=(k == 0), stop=(k == 2 * KD - 1))
                        last.then_inc(x_out[i], 1)

        @block.scalar
        def _(act):
            pass

        @block.vector
        def _(dve):
            with dve.If(dve.value_load(keep["flag"][0:1, 0:1], min_val=0, max_val=1) > 0):
                with dve.Fori(0, TILES) as t:
                    dve.wait_ge(x_back, t + 1)
                    nc.vector.tensor_copy(own[:], bank[0][:, 0:D]).then_inc(x_rows, 1)
                dve.wait_ge(x_rowst, 16 * TILES)
                dve.wait_ge(x_const, 3)
                dve.wait_ge(x_load, 16 * 8)
                nc.vector.tensor_copy(dst_f[:], dst_i[:]).then_inc(x_const, 1)
                for i in range(2):
                    nc.vector.memset(agg[:], 0.0).then_inc(x_const, 1)
                    dve.wait_ge(x_const, 5 + 3 * i)
                    with dve.Fori(0, ELEN) as c:
                        nc.vector.tensor_copy(col[:], src_i[:, bass.ds(c, 1)]).then_inc(x_col[i], 1)
                        nc.vector.tensor_scalar(rel[:], tbase[:], dst_f[:, bass.ds(c, 1)], None, ALU.add)\
                          .then_inc(x_sum[i], 1)
                        dve.wait_ge(x_sum[i], c * (SUPERS + 1) + 1)
                        for b in range(SUPERS):
                            for j in range(SUP):
                                last = nc.vector.tensor_scalar(hot[:, j, :], iota_t[:], rel[:, b * SUP + j:b * SUP + j + 1],
                                                               None, ALU.is_equal)
                            last.then_inc(x_hot[i], 1)
                            dve.wait_ge(x_prod[i], c * SUPERS + (b + 1))
                            for j in range(SUP):
                                last = nc.vector.tensor_tensor(agg[:, b * SUP + j, :], bank[j][:, 0:D + 1],
                                                               agg[:, b * SUP + j, :], ALU.add)
                            last.then_inc(x_sum[i], 1)
                            dve.wait_ge(x_sum[i], c * (SUPERS + 1) + (b + 2))
                        dve.wait_ge(x_col[i], c + 1)
                    nc.vector.tensor_scalar(deg[:], agg[:, :, D], 1.0, None, ALU.max).then_inc(x_const, 1)
                    dve.wait_ge(x_const, 6 + 3 * i)
                    nc.vector.reciprocal(deg[:], deg[:]).then_inc(x_const, 1)
                    dve.wait_ge(x_const, 7 + 3 * i)
                    with dve.Fori(0, TILES) as t:
                        nc.vector.tensor_scalar(mean[:], agg[:, bass.ds(t, 1), 0:D].rearrange("p o f -> p (o f)"),
                                                deg[:, bass.ds(t, 1)], None, ALU.mult).then_inc(x_mean[i], 1)
                        dve.wait_ge(x_turn[i], t + 1)
                        nc.vector.tensor_copy(turned[:].rearrange("p k c -> p (k c)"), bank[0][:]).then_inc(x_turned[i], 1)
                        dve.wait_ge(x_out[i], t + 1)
                        nc.vector.tensor_tensor(res[:], bank[1][:, 0:D], bias[:, i, :], ALU.add).then_inc(x_res[i], 1)
                        dve.wait_ge(x_res[i], t * 3 + 1)
                        if i == 0:
                            nc.vector.tensor_scalar(res[:], res[:], 0.0, None, ALU.max).then_inc(x_res[i], 2)
                        else:
                            nc.vector.tensor_tensor(res[:], res[:], xin[:], ALU.add).then_inc(x_res[i], 1)
                            dve.wait_ge(x_res[i], t * 3 + 2)
                            nc.vector.tensor_tensor(res[:], res[:], base[:], ALU.add).then_inc(x_res[i], 1)
                        dve.wait_ge(x_stored[i], t * 16 + 16)


def mix_phase(nc, sem, mem, d, t_in, keep, out):
    def sb(name, shape, dt=F32):
        return mem.enter_context(nc.sbuf_tensor(name, shape, dt))

    ident, eps, kvacc = keep["ident"], keep["eps"], keep["kvacc"]
    NV = 4 * KD
    wq, wm = sb("wq", [P, KD, D]), sb("wm", [P, KD, D])
    w1, w2 = sb("w1", [P, 2 * KD, 2 * D]), sb("w2", [P, 2 * KD, D])
    we1, we2, be1, be2 = (keep[k] for k in ("we1", "we2", "be1", "be2"))
    wr = sb("wr", [P, KD, EXPERTS])
    g2, b2 = sb("mix_g2", [P, D]), sb("mix_b2", [P, D])
    br = sb("br", [P, EXPERTS])
    rows = sb("vec_rows", [NV, P])
    cols, betab = keep["cols"], keep["betab"]
    G1, B1, GAMMA, BETA = VEC
    ones = sb("ones2", [P, P])
    bdkv, bdks = sb("bdkv", [P, KD, P]), sb("bdks", [P, KD, P])
    c1 = sb("c1", [P, 2 * D // P])
    lb = sb("lb", [P, EXPERTS])
    iota8 = sb("iota8", [P, SUP, EXPERTS])
    xq, xh = sb("xq", [P, KD, R]), sb("xh", [P, KD, R])
    qt, msgt, m1t = (sb(n, [P, KD, R]) for n in ("qt", "msgt", "m1t"))
    x2t = qt
    qmin, qexp = sb("qmin", [P, 2, NW]), sb("qexp", [P, 2, NW])
    den, rden = qmin, qexp
    nrm1 = sb("nrm1", [P, SUP, D])
    nrm = sb("nrm", [P, SUP, D])
    h1t = sb("h1t", [P, 2 * D // P, R])
    filler = h1t[:].rearrange("p m r -> p (m r)")[:, 0:LISTS // P * 4].rearrange("p (n c) -> p n c", c=4)
    acc, x2 = (sb(n, [P, SUP, D]) for n in ("m_acc", "x2"))
    stats, mv = sb("m_stats", [P, SUP, 6]), sb("m_mv", [P, SUP, 2])
    std, rstd, rstd2, var2 = (sb(n, [P, SUP]) for n in ("m_std", "m_rstd", "m_rstd2", "m_var2"))
    lg, top = sb("lg", [P, SUP, EXPERTS]), sb("top", [P, SUP, 8])
    idx, idxf = sb("idx", [P, SUP, 8], U32), sb("idxf", [P, SUP, 8])
    gap, wgt = sb("gap", [P, SUP]), sb("wgt", [P, SUP, 2])
    pick = sb("pick", [P, 2 * SUP * EXPERTS])
    picked = pick[:].rearrange("p (i j e) -> p i j e", i=2, j=SUP)
    before, everyone = sb("before", [P, P]), sb("everyone", [P, P])
    chosen = sb("chosen", [P, CHOICES, EXPERTS])
    upto = [sb(f"upto{i}", [P, CHOICES, EXPERTS]) for i in range(2)]
    place = sb("place", [P, CHOICES, EXPERTS])
    place_f, place_i = sb("place_f", [P, CHOICES]), sb("place_i", [P, CHOICES], I32)
    entry = sb("entry", [P, CHOICES, 4])
    node = sb("node", [P, CHOICES])
    zeros = sb("zeros", [P, D])
    ends = keep["ends"]
    bank = [mem.enter_context(nc.psum_tensor(f"bank{i}", [P, 512], F32)) for i in range(8)]

    m_w, m_row = sem("m_w"), sem("m_row")
    m_const, m_cols, m_colst, m_fold, m_scaled, m_bd, m_setup = (sem(f"m_{k}") for k in (
        "const", "cols", "colst", "fold", "scaled", "bd", "setup"))
    m_xq, m_xh = sem("m_xq"), sem("m_xh")
    m_accin, m_accb, m_accfree = sem("m_accin"), sem("m_accb"), sem("m_accfree")
    m_q, m_qmin, m_qexp, m_qt = sem("m_q"), sem("m_qmin"), sem("m_qexp"), sem("m_qt")
    m_att, m_den, m_msg = sem("m_att"), sem("m_den"), sem("m_msg")
    m_m1, m_tr1, m_m1t = sem("m_m1"), sem("m_tr1"), sem("m_m1t")
    m_h1, m_h1t, m_h2, m_x2 = sem("m_h1"), sem("m_h1t"), sem("m_h2"), sem("m_x2")
    m_tr2, m_x2t = sem("m_tr2"), sem("m_x2t")
    m_lg, m_route, m_gap, m_exp = (sem(f"m_{k}") for k in ("lg", "route", "gap", "exp"))
    m_pick, m_count, m_place, m_entry = sem("m_pick"), sem("m_count"), sem("m_place"), sem("m_entry")
    m_listfree = sem("m_listfree")
    m_beta, m_bias, m_folded = sem("m_beta"), sem("m_bias"), sem("m_folded")
    m_counted, m_x2free, m_nrmfree = sem("m_counted"), sem("m_x2free"), sem("m_nrmfree")
    m_listed = sem("m_listed", pool_dma=True)
    m_ew, m_fill, m_filled, m_x2st, m_nrmst = (sem(f"m_{k}") for k in ("ew", "fill", "filled", "x2st", "nrmst"))
    ln = [{k: sem(f"m_ln{i}_{k}") for k in ("stats", "var", "std", "rstd", "done") + ("step",) * (i == 2)} for i in range(3)]

    kb = lambda w: w.rearrange("(k p) n -> p k n", p=P)
    acc_s = d["acc"].rearrange("(s j p) f -> s p j f", p=P, j=SUP)
    out_s = out[0:NPAD, :].rearrange("(s j p) f -> s p j f", p=P, j=SUP)
    table_s = d["table"].rearrange("(s j p) f -> s p j f", p=P, j=SUP)
    xnt_s = d["xnt"].rearrange("(s j) p k c -> s p k j c", j=SUP)
    tile_cols = lambda b, j: b[j // 2][:, (j % 2) * D:(j % 2 + 1) * D]
    row_vec = lambda v, n: v.rearrange("(k p) -> k p", p=P)

    def wait(eng, signal, value):
        if not isinstance(value, int) or value > 0:
            eng.wait_ge(signal, value)

    with nc.Block() as block:
        @block.sync
        def _(sp):
            r = 0
            for v, n in ((row_vec(t_in["mix_g1"], KD), KD), (row_vec(t_in["mix_b1"], KD), KD),
                         (row_vec(t_in["ffn_gamma"], KD), KD), (row_vec(t_in["ffn_beta"], KD), KD)):
                sp.dma_start(rows[r:r + n, :], v).then_inc(m_row, 16)
                r += n
            sp.dma_start(w1[:], kb(t_in["mix_W1"])).then_inc(m_w, 16)
            sp.dma_start(wr[:], kb(t_in["ffn_Wr"])).then_inc(m_w, 16)
            sp.dma_start(br[:], t_in["ffn_br"].unsqueeze(0).to_broadcast([P, EXPERTS])).then_inc(m_w, 16)
            sp.dma_start(wq[:], kb(t_in["mix_Wq"])).then_inc(m_w, 16)
            sp.dma_start(wm[:], kb(t_in["mix_Wm"])).then_inc(m_w, 16)
            sp.dma_start(w2[:], kb(t_in["mix_W2"])).then_inc(m_w, 16)
            sp.dma_start(g2[:], t_in["mix_g2"].unsqueeze(0).to_broadcast([P, D])).then_inc(m_w, 16)
            sp.dma_start(b2[:], t_in["mix_b2"].unsqueeze(0).to_broadcast([P, D])).then_inc(m_w, 16)

            def fetch(buf, signal, s):
                for k in range(KD):
                    sp.dma_start(buf[:, k, :].rearrange("p (j c) -> p j c", j=SUP),
                                 xnt_s[bass.ds(s, 1), :, k].rearrange("o p j c -> (o p) j c")).then_inc(signal, 16)

            def fetch_acc(s):
                wait(sp, m_accfree, s)
                sp.dma_start(acc[:], acc_s[bass.ds(s, 1)].rearrange("o p j f -> (o p) j f")).then_inc(m_accin, 16)
            fetch(xq, m_xq, 0)
            fetch(xh, m_xh, 0)
            fetch_acc(0)
            sp.wait_ge(m_fill, 2)
            sp.dma_start(d["lists"].rearrange("(p n) c -> p n c", p=P), filler).then_inc(m_filled, 16)
            sp.dma_start(out[NPAD:NPAD + P, :], zeros[:]).then_inc(m_filled, 16)
            for e in range(EXPERTS):
                sp.dma_start(we1[:, e], kb(t_in["ffn_W1"][e])).then_inc(m_ew, 16)
                sp.dma_start(we2[:, e], kb(t_in["ffn_W2"][e])).then_inc(m_ew, 16)
            sp.dma_start(be1[:], t_in["ffn_b1"].rearrange("e h -> (e h)").unsqueeze(0).to_broadcast([P, EXPERTS * HID]))\
              .then_inc(m_ew, 16)
            sp.dma_start(be2[:], t_in["ffn_b2"].rearrange("e h -> (e h)").unsqueeze(0).to_broadcast([P, EXPERTS * D]))\
              .then_inc(m_ew, 16)
            sp.wait_ge(m_filled, 32)

            sp.wait_ge(m_q, 4)
            fetch(xq, m_xq, 1)

            def step(s, first=False, more=2):
                if more > 1:
                    sp.wait_ge(m_q, (s + 1) * 4 + 4)
                    fetch(xq, m_xq, s + 2)
                if not first:
                    sp.wait_ge(m_x2, (s - 1) * 2 + 2)
                    sp.dma_start(out_s[bass.ds(s - 1, 1)].rearrange("o p j f -> (o p) j f"), x2[:]).then_inc(m_x2st, 16)
                    fetch_acc(s)
                    sp.wait_ge(ln[2]["done"], s)
                    sp.dma_start(table_s[bass.ds(s - 1, 1)].rearrange("o p j f -> (o p) j f"), nrm[:])\
                      .then_inc(m_nrmst, 16)
                    sp.wait_ge(m_x2st, s * 16)
                    sp.sem_inc(m_x2free, 1)
                    sp.wait_ge(m_nrmst, s * 16)
                    sp.sem_inc(m_nrmfree, 1)
                if more:
                    sp.wait_ge(m_h1, s * 8 + 8)
                    fetch(xh, m_xh, s + 1)
            step(0, first=True)
            with sp.Fori(1, SUPERS - 2) as s:
                step(s)
            step(SUPERS - 2, more=1)
            step(SUPERS - 1, more=0)
            sp.wait_ge(m_x2, SUPERS * 2)
            sp.dma_start(out_s[SUPERS - 1], x2[:]).then_inc(m_x2st, 16)
            sp.wait_ge(ln[2]["done"], SUPERS)
            sp.dma_start(table_s[SUPERS - 1], nrm[:]).then_inc(m_nrmst, 16)
            sp.wait_ge(m_x2st, 16 * SUPERS)
            sp.wait_ge(m_nrmst, 16 * SUPERS)
            sp.wait_ge(m_ew, 16 * (2 * EXPERTS + 2))

        @block.gpsimd
        def _(pool):
            nc.gpsimd.memset(bdkv[:], 0.0).then_inc(m_const, 1)
            nc.gpsimd.memset(bdks[:], 0.0).then_inc(m_const, 1)
            nc.gpsimd.memset(ones[:], 1.0).then_inc(m_const, 1)
            nc.gpsimd.memset(filler, 0.0).then_inc(m_const, 1)
            nc.gpsimd.memset(zeros[:], 0.0).then_inc(m_fill, 1)
            nc.gpsimd.memset(before[:], 1.0).then_inc(m_const, 1)
            nc.gpsimd.memset(everyone[:], 1.0).then_inc(m_const, 1)
            nc.gpsimd.memset(entry[:], 0.0).then_inc(m_const, 1)
            nc.gpsimd.iota(node[:], [[0, 2], [P, SUP]], base=0, channel_multiplier=1,
                           allow_small_or_imprecise_dtypes=True).then_inc(m_const, 1)
            nc.gpsimd.iota(ends[:], [[REGION, EXPERTS]], base=0, channel_multiplier=0,
                           allow_small_or_imprecise_dtypes=True).then_inc(m_const, 1)
            nc.gpsimd.iota(iota8[:], [[0, SUP], [1, EXPERTS]], base=0, channel_multiplier=0,
                           allow_small_or_imprecise_dtypes=True).then_inc(m_const, 1)
            pool.wait_ge(m_const, 10)
            nc.gpsimd.iota(filler[:, :, 2], [[0, LISTS // P // P], [1, P]], base=NPAD, channel_multiplier=0,
                           allow_small_or_imprecise_dtypes=True).then_inc(m_fill, 1)
            nc.gpsimd.affine_select(out=before[:], in_=before[:], compare_op=ALU.is_ge, fill=0.0,
                                    base=-1, pattern=[[1, P]], channel_multiplier=-1).then_inc(m_const, 1)
            pool.wait_ge(m_w, 16 * 8)

            def add_bias(s):
                pool.wait_ge(m_accin, s * 16 + 16)
                nc.gpsimd.tensor_tensor(acc[:], acc[:], b2[:].unsqueeze(1).to_broadcast([P, SUP, D]), ALU.add)\
                  .then_inc(m_accb, 1)

            def enter(s):
                pool.wait_ge(m_entry, s * ENTRY_STEPS + ENTRY_STEPS)
                pool.wait_ge(m_filled, 32)
                pool.sem_inc(keep["turn"], 1)
                for b in range(CHOICES):
                    pool.indirect_dma_start(d["lists"], bass.IndirectOffsetOnAxis(ap=place_i[:, b:b + 1], axis=0),
                                            entry[:, b, :], None).then_inc(m_listed, 16)
                pool.wait_ge(m_listed, s * (16 * CHOICES) + 16 * CHOICES)
                pool.sem_inc(m_listfree, 1)
            add_bias(0)
            with pool.Fori(0, SUPERS - 1) as s:
                add_bias(s + 1)
                enter(s)
            enter(SUPERS - 1)
            pool.wait_ge(m_listed, 16 * CHOICES * SUPERS)

        @block.scalar
        def _(act):
            act.wait_ge(m_cols, 1)
            nc.scalar.activation(cols[:], bank[0][:, 0:NV], ACT.Copy).then_inc(m_colst, 1)

            def stdev(l, src, s, per, k):
                act.wait_ge(ln[l]["var"], s * per + (k + 1))
                nc.scalar.activation(std[:], src, ACT.Sqrt, bias=eps[:]).then_inc(ln[l]["std"], 1)
            act.wait_ge(m_filled, 32)

            def exps(s):
                for i in range(4):
                    act.wait_ge(m_qmin, s * 4 + (i + 1))
                    nc.scalar.activation(qexp[:, i % 2, :], qmin[:, i % 2, :], ACT.Exp).then_inc(m_qexp, 1)

            def copies(to, turned, done, s):
                for b in range(4):
                    k, half, w = b // 2, b % 2, (4, 3)[b % 2] * P
                    act.wait_ge(turned, s * 4 + (b + 1))
                    nc.scalar.activation(to[:, k, half * 4 * P:half * 4 * P + w], bank[4 + b][:, 0:w], ACT.Copy)\
                      .then_inc(done, 1)

            def relus(s, blocks):
                for i in blocks:
                    m, n = i // 2, i % 2
                    act.wait_ge(m_h1, s * 8 + (i + 1))
                    nc.scalar.activation(h1t[:, m, n * NW:(n + 1) * NW], bank[4 + i % 4][:, 0:NW], ACT.Relu,
                                         bias=c1[:, m:m + 1]).then_inc(m_h1t, 1)

            def stdevs_x2(s):
                stdev(2, mv[:, :, 1], s, 2, 0)
                stdev(2, var2[:], s, 2, 1)

            def route(s):
                act.wait_ge(m_gap, s + 1)
                nc.scalar.activation(gap[:], gap[:], ACT.Exp).then_inc(m_exp, 1)

            def step(s, first=False, last=False):
                if not first:
                    stdev(1, mv[:, :, 1], s - 1, 1, 0)
                copies(m1t, m_tr1, m_m1t, s)
                if not last:
                    exps(s + 1)
                relus(s, range(4))
                if not first:
                    stdevs_x2(s - 1)
                relus(s, (4,))
                if not last:
                    stdev(0, mv[:, :, 1], s + 1, 1, 0)
                relus(s, (5, 6))
                if not first:
                    copies(x2t, m_tr2, m_x2t, s - 1)
                relus(s, (7,))
                if not first:
                    route(s - 1)
            exps(0)
            stdev(0, mv[:, :, 1], 0, 1, 0)
            step(0, first=True)
            with act.Fori(1, SUPERS - 1) as s:
                step(s)
            step(SUPERS - 1, last=True)
            stdev(1, mv[:, :, 1], SUPERS - 1, 1, 0)
            stdevs_x2(SUPERS - 1)
            copies(x2t, m_tr2, m_x2t, SUPERS - 1)
            route(SUPERS - 1)
            for e in range(EXPERTS):
                act.wait_ge(m_beta, e + 1)
                for k in range(KD):
                    last = nc.scalar.activation(we1[:, e, k, :], we1[:, e, k, :], ACT.Copy,
                                                scale=cols[:, GAMMA + k:GAMMA + k + 1])
            last.then_inc(m_folded, 1)
            act.wait_ge(m_folded, 1)

        @block.tensor
        def _(pe):
            pe.wait_ge(m_row, 64)
            nc.tensor.transpose(bank[0][:, 0:NV], rows[:], ident[0:NV, 0:NV]).then_inc(m_cols, 1)
            pe.wait_ge(m_colst, 1)
            pe.wait_ge(m_bd, 1)
            pe.wait_ge(m_w, 16 * 8)
            for m in range(2 * D // P):
                for k in range(KD):
                    nc.tensor.matmul(bank[1][:, m:m + 1], w1[:, KD + k, m * P:(m + 1) * P], cols[:, B1 + k:B1 + k + 1],
                                     start=(k == 0), stop=(k == KD - 1))
            for k in range(KD):
                last = nc.tensor.matmul(bank[3][:, 0:EXPERTS], betab[:, k, :], wr[:, k, :],
                                        start=(k == 0), stop=(k == KD - 1))
            last.then_inc(m_fold, 1)
            pe.wait_ge(m_setup, 1)
            pe.wait_ge(m_const, 11)

            def queries(s, first=False):
                pe.wait_ge(m_xq, s * 32 + 32)
                for i in range(4):
                    m, n = i // 2, i % 2
                    if not first:
                        pe.wait_ge(m_m1t, (s - 1) * 4 + (i + 1))
                    for k in range(KD):
                        last = nc.tensor.matmul(bank[4 + i][:, 0:NW], wq[:, k, m * P:(m + 1) * P],
                                                xq[:, k, n * NW:(n + 1) * NW], start=(k == 0), stop=(k == KD - 1))
                    last.then_inc(m_q, 1)

            def attend(s, blocks, first=False):
                for i in blocks:
                    if i == 0 and not first:
                        wait(pe, ln[1]["done"], s - 1)
                    m, n = i // 2, i % 2
                    pe.wait_ge(m_qt, s * 4 + (i + 1))
                    if i >= 2:
                        pe.wait_ge(m_msg, s * 4 + (i - 1))
                    nc.tensor.matmul(bank[2 * (i % 2)][:, 0:NW], bdkv[:, m, :], qt[:, m, n * NW:(n + 1) * NW],
                                     start=True, stop=True)
                    nc.tensor.matmul(bank[1 + 2 * (i % 2)][:, 0:NW], bdks[:, m, :], qt[:, m, n * NW:(n + 1) * NW],
                                     start=True, stop=True).then_inc(m_att, 1)

            def project(s):
                pe.wait_ge(m_msg, s * 4 + 4)
                for j in range(SUP):
                    for k in range(KD):
                        last = nc.tensor.matmul(tile_cols(bank[0:4], j), msgt[:, k, j * P:(j + 1) * P], wm[:, k, :],
                                                start=(k == 0), stop=(k == KD - 1))
                last.then_inc(m_m1, 1)

            def turn(src, done, s, free=None, value=0, at=0):
                for b in range(4):
                    k, half = b // 2, b % 2
                    if free and b == at:
                        wait(pe, free, value)
                    for j in range(4 * half, min(4 * half + 4, SUP)):
                        last = nc.tensor.transpose(bank[4 + b][:, (j % 4) * P:(j % 4 + 1) * P],
                                                   src[:, j, k * P:(k + 1) * P], ident[:])
                    last.then_inc(done, 1)

            def hidden(s, blocks, last_step=False):
                for i in blocks:
                    m, n = i // 2, i % 2
                    if i == 0:
                        pe.wait_ge(m_xh, s * 32 + 32)
                        pe.wait_ge(m_m1t, s * 4 + 4)
                    if i >= 4:
                        pe.wait_ge(m_h1t, s * 8 + (i - 3))
                    elif not last_step:
                        pe.wait_ge(m_qt, (s + 1) * 4 + (i + 1))
                    for k in range(2 * KD):
                        src = xh if k < KD else m1t
                        last = nc.tensor.matmul(bank[4 + i % 4][:, 0:NW], w1[:, k, m * P:(m + 1) * P],
                                                src[:, k % KD, n * NW:(n + 1) * NW],
                                                start=(k == 0), stop=(k == 2 * KD - 1))
                    last.then_inc(m_h1, 1)

            def feed(s, last_step=False):
                pe.wait_ge(m_h1t, s * 8 + 8)
                if last_step:
                    pe.wait_ge(ln[1]["done"], s)
                else:
                    pe.wait_ge(ln[0]["done"], s + 2)
                for j in range(SUP):
                    for k in range(2 * KD):
                        last = nc.tensor.matmul(tile_cols(bank[0:4], j), h1t[:, k, j * P:(j + 1) * P], w2[:, k, :],
                                                start=(k == 0), stop=(k == 2 * KD - 1))
                last.then_inc(m_h2, 1)

            def logits(s, free):
                pe.wait_ge(ln[2]["done"], s + 1)
                turn(nrm, m_tr2, s, *free)
                pe.wait_ge(m_x2t, s * 4 + 4)
                for j in range(SUP):
                    for k in range(KD):
                        last = nc.tensor.matmul(bank[4][:, j * EXPERTS:(j + 1) * EXPERTS], x2t[:, k, j * P:(j + 1) * P],
                                                wr[:, k, :], start=(k == 0), stop=(k == KD - 1))
                last.then_inc(m_lg, 1)

            def counts(s):
                pe.wait_ge(m_pick, s + 1)
                nc.tensor.matmul(bank[6][:, 0:CHOICES * EXPERTS], before[:], pick[:], start=True, stop=True)
                nc.tensor.matmul(bank[7][:, 0:CHOICES * EXPERTS], everyone[:], pick[:], start=True, stop=True)\
                  .then_inc(m_count, 1)

            def step(s, first=False, last=False):
                pe.wait_ge(ln[0]["done"], s + 1)
                if first:
                    turn(nrm1, m_tr1, s)
                else:
                    turn(nrm1, m_tr1, s, m_counted, s, 2)
                if not last:
                    queries(s + 1)
                for i in range(4):
                    hidden(s, (i,), last)
                    if not last:
                        attend(s + 1, ((0, 1), (2,), (3,), ())[i], first)
                hidden(s, (4,), last)
                if not last:
                    project(s + 1)
                hidden(s, (5, 6), last)
                if not first:
                    logits(s - 1, (m_h1t, s * 8 + 7))
                hidden(s, (7,), last)
                feed(s, last)
                if not first:
                    counts(s - 1)
            queries(0, True)
            attend(0, range(4), True)
            project(0)
            step(0, first=True)
            with pe.Fori(1, SUPERS - 1) as s:
                step(s)
            step(SUPERS - 1, last=True)
            pe.wait_ge(m_counted, SUPERS)
            logits(SUPERS - 1, (None, 0))
            counts(SUPERS - 1)
            pe.wait_ge(m_ew, 16 * (2 * EXPERTS + 2))
            pe.wait_ge(ln[1]["done"], SUPERS)
            for e in range(EXPERTS):
                if e >= 2:
                    pe.wait_ge(m_bias, e - 1)
                for k in range(KD):
                    last = nc.tensor.matmul(bank[e % 2][:], betab[:, k, :], we1[:, e, k, :],
                                            start=(k == 0), stop=(k == KD - 1))
                last.then_inc(m_beta, 1)

        @block.vector
        def _(dve):
            dve.wait_ge(m_colst, 1)
            dve.wait_ge(m_const, 11)
            for k in range(KD):
                last = nc.vector.tensor_scalar(betab[:, k, :], ones[:], cols[:, BETA + k:BETA + k + 1], None, ALU.mult)
            last.then_inc(m_bd, 1)
            for k in range(KD):
                for b in range(P // HD):
                    q = slice(b * HD, (b + 1) * HD)
                    nc.vector.tensor_copy(bdkv[q, k, q], kvacc[q, k, q])
                    last = nc.vector.tensor_scalar(bdks[q, k, q], ones[q, q], kvacc[q, k, P:P + 1], None, ALU.mult)
            last.then_inc(m_bd, 1)
            dve.wait_ge(m_w, 16 * 8)
            dve.wait_ge(m_fold, 1)
            nc.vector.tensor_copy(c1[:], bank[1][:, 0:2 * D // P])
            nc.vector.tensor_tensor(lb[:], bank[3][:, 0:EXPERTS], br[:], ALU.add)
            for k in range(KD):
                nc.vector.tensor_scalar(w1[:, KD + k, :], w1[:, KD + k, :], cols[:, G1 + k:G1 + k + 1], None, ALU.mult)
                last = nc.vector.tensor_scalar(wr[:, k, :], wr[:, k, :], cols[:, GAMMA + k:GAMMA + k + 1],
                                               None, ALU.mult)
            last.then_inc(m_setup, 1)
            for signal in (m_listfree, m_counted, m_x2free, m_nrmfree):
                dve.sem_inc(signal, 1)

            def moments(l, src, s, per):
                for j in range(SUP):
                    last = nc.vector.bn_stats(stats[:, j, :], src(j))
                last.then_inc(ln[l]["stats"], 1)
                dve.wait_ge(ln[l]["stats"], s + 1)
                dve.sem_inc(keep["turn"], 1)
                for j in range(SUP):
                    last = nc.vector.bn_aggr(mv[:, j, :], stats[:, j, :])
                last.then_inc(ln[l]["var"], 1)
                dve.wait_ge(ln[l]["std"], s * per + 1)
                nc.vector.reciprocal(rstd[:], std[:]).then_inc(ln[l]["rstd"], 1)
                dve.wait_ge(ln[l]["rstd"], s * per + 1)

            def normalise(l, src, s, by):
                to = nrm if l else nrm1
                for j in range(SUP):
                    last = nc.vector.tensor_scalar(to[:, j, :], src(j), mv[:, j, 0:1], by[:, j:j + 1],
                                                   ALU.subtract, ALU.mult)
                last.then_inc(ln[l]["done"], 1)
            low = lambda j: tile_cols(bank[0:4], j)
            rows_of = lambda j: x2[:, j, :]

            def elus(s):
                for i in range(4):
                    m, n = i // 2, i % 2
                    dve.wait_ge(m_q, s * 4 + (i + 1))
                    nc.vector.tensor_scalar(qmin[:, i % 2, :], bank[4 + i][:, 0:NW], 0.0, None, ALU.min).then_inc(m_qmin, 1)
                    dve.wait_ge(m_qexp, s * 4 + (i + 1))
                    nc.vector.scalar_tensor_tensor(qt[:, m, n * NW:(n + 1) * NW], bank[4 + i][:, 0:NW], 0.0,
                                                   qexp[:, i % 2, :], ALU.max, ALU.add).then_inc(m_qt, 1)

            def messages(s):
                for i in range(4):
                    m, n = i // 2, i % 2
                    dve.wait_ge(m_att, s * 4 + (i + 1))
                    nc.vector.tensor_scalar(den[:, i % 2, :], bank[1 + 2 * (i % 2)][:, 0:NW], ATT_EPS, None, ALU.add)\
                      .then_inc(m_den, 1)
                    dve.wait_ge(m_den, s * 8 + (2 * i + 1))
                    nc.vector.reciprocal(rden[:, i % 2, :], den[:, i % 2, :]).then_inc(m_den, 1)
                    dve.wait_ge(m_den, s * 8 + (2 * i + 2))
                    nc.vector.tensor_tensor(msgt[:, m, n * NW:(n + 1) * NW], bank[2 * (i % 2)][:, 0:NW],
                                            rden[:, i % 2, :], ALU.mult).then_inc(m_msg, 1)

            def norm_messages(s):
                dve.wait_ge(m_m1, s + 1)
                moments(0, low, s, 1)
                normalise(0, low, s, rstd)

            def norm_feed(s):
                dve.wait_ge(m_h2, s + 1)
                moments(1, low, s, 1)
                dve.wait_ge(m_nrmfree, s + 1)
                normalise(1, low, s, rstd)

            def residual(s):
                dve.wait_ge(ln[1]["done"], s + 1)
                nc.vector.tensor_tensor(nrm[:], nrm[:], g2[:].unsqueeze(1).to_broadcast([P, SUP, D]), ALU.mult)\
                  .then_inc(m_x2, 1)
                dve.wait_ge(m_x2, s * 2 + 1)
                dve.wait_ge(m_accb, s + 1)
                dve.wait_ge(m_x2free, s + 1)
                nc.vector.tensor_tensor(x2[:], nrm[:], acc[:], ALU.add).then_inc(m_x2, 1)
                dve.wait_ge(m_x2, s * 2 + 2)
                dve.sem_inc(m_accfree, 1)
                moments(2, rows_of, s, 2)
                nc.vector.tensor_tensor(var2[:], rstd[:], rstd[:], ALU.mult).then_inc(ln[2]["step"], 1)
                dve.wait_ge(ln[2]["step"], s * 2 + 1)
                nc.vector.tensor_tensor(var2[:], var2[:], mv[:, :, 1], ALU.mult).then_inc(ln[2]["var"], 1)
                dve.wait_ge(ln[2]["std"], s * 2 + 2)
                nc.vector.reciprocal(rstd2[:], std[:]).then_inc(ln[2]["rstd"], 1)
                dve.wait_ge(ln[2]["rstd"], s * 2 + 2)
                nc.vector.tensor_tensor(rstd2[:], rstd2[:], rstd[:], ALU.mult).then_inc(ln[2]["step"], 1)
                dve.wait_ge(ln[2]["step"], s * 2 + 2)
                normalise(2, rows_of, s, rstd2)

            def route(s):
                dve.wait_ge(m_lg, s + 1)
                nc.vector.tensor_tensor(lg[:], bank[4][:, 0:SUP * EXPERTS].rearrange("p (j e) -> p j e", j=SUP),
                                        lb[:].unsqueeze(1).to_broadcast([P, SUP, EXPERTS]), ALU.add).then_inc(m_route, 1)
                dve.wait_ge(m_route, s * 7 + 1)
                dve.sem_inc(keep["turn"], 1)
                for j in range(SUP):
                    last = nc.vector.max(top[:, j, :], lg[:, j, :])
                last.then_inc(m_route, 1)
                dve.wait_ge(m_route, s * 7 + 2)
                nc.vector.tensor_tensor(gap[:], top[:, :, 1], top[:, :, 0], ALU.subtract).then_inc(m_gap, 1)
                for j in range(SUP):
                    last = nc.vector.max_index(idx[:, j, :], top[:, j, :], lg[:, j, :])
                last.then_inc(m_route, 1)
                dve.wait_ge(m_route, s * 7 + 3)
                nc.vector.tensor_copy(idxf[:], idx[:]).then_inc(m_route, 1)
                dve.wait_ge(m_exp, s + 1)
                nc.vector.tensor_scalar(wgt[:, :, 1], gap[:], 1.0, None, ALU.add).then_inc(m_route, 1)
                dve.wait_ge(m_route, s * 7 + 5)
                nc.vector.reciprocal(wgt[:, :, 0], wgt[:, :, 1]).then_inc(m_route, 1)
                dve.wait_ge(m_route, s * 7 + 6)
                nc.vector.tensor_tensor(wgt[:, :, 1], gap[:], wgt[:, :, 0], ALU.mult).then_inc(m_route, 1)
                for i in range(2):
                    last = nc.vector.tensor_tensor(picked[:, i], iota8[:],
                                                   idxf[:, :, i:i + 1].to_broadcast([P, SUP, EXPERTS]), ALU.is_equal)
                last.then_inc(m_pick, 1)

            def enter(s):
                dve.wait_ge(m_count, s + 1)
                count = bank[7][:, 0:CHOICES * EXPERTS].rearrange("p (b e) -> p b e", b=CHOICES)
                ahead = bank[6][:, 0:CHOICES * EXPERTS].rearrange("p (b e) -> p b e", b=CHOICES)
                nc.vector.tensor_copy(chosen[:], count).then_inc(m_place, 1)
                nc.vector.tensor_copy(upto[0][:, 1:, :], count[:, 1:, :]).then_inc(m_place, 1)
                nc.vector.tensor_tensor(upto[0][:, 0, :], count[:, 0, :], ends[:], ALU.add).then_inc(m_place, 1)
                dve.wait_ge(m_place, s * PLACE_STEPS + 3)
                n, w, done = 0, 1, 3
                while w < CHOICES:
                    nc.vector.tensor_copy(upto[1 - n][:, 0:w, :], upto[n][:, 0:w, :]).then_inc(m_place, 1)
                    nc.vector.tensor_tensor(upto[1 - n][:, w:, :], upto[n][:, w:, :], upto[n][:, :CHOICES - w, :], ALU.add)\
                      .then_inc(m_place, 1)
                    n, w, done = 1 - n, 2 * w, done + 2
                    dve.wait_ge(m_place, s * PLACE_STEPS + done)
                nc.vector.tensor_copy(ends[:], upto[n][:, CHOICES - 1, :]).then_inc(m_place, 1)
                nc.vector.tensor_tensor(place[:], ahead, upto[n][:], ALU.add).then_inc(m_place, 1)
                dve.wait_ge(m_place, s * PLACE_STEPS + done + 2)
                dve.sem_inc(m_counted, 1)
                nc.vector.tensor_tensor(place[:], place[:], chosen[:], ALU.subtract).then_inc(m_place, 1)
                dve.wait_ge(m_place, s * PLACE_STEPS + done + 3)
                nc.vector.tensor_tensor(place[:], place[:], pick[:].rearrange("p (b e) -> p b e", b=CHOICES), ALU.mult)\
                  .then_inc(m_place, 1)
                dve.wait_ge(m_place, s * PLACE_STEPS + done + 4)
                nc.vector.tensor_reduce(place_f[:], place[:], mybir.AxisListType.X, ALU.add).then_inc(m_place, 1)
                dve.wait_ge(m_place, s * PLACE_STEPS + done + 5)
                assert done + 5 == PLACE_STEPS
                dve.wait_ge(m_listfree, s + 1)
                nc.vector.tensor_copy(place_i[:], place_f[:]).then_inc(m_entry, 1)
                for i in (0, 2):
                    nc.vector.tensor_copy(entry[:, :, i], node[:]).then_inc(m_entry, 1)
                nc.vector.tensor_copy(entry[:, :, 1].rearrange("p (i j) -> p i j", i=2), wgt[:].rearrange("p j i -> p i j"))\
                  .then_inc(m_entry, 1)
                dve.wait_ge(m_entry, s * ENTRY_STEPS + 4)
                nc.vector.tensor_scalar(node[:], node[:], float(R), None, ALU.add).then_inc(m_entry, 1)
                dve.wait_ge(m_entry, s * ENTRY_STEPS + ENTRY_STEPS)

            def step(s, first=False, last=False):
                if not first:
                    norm_feed(s - 1)
                if not last:
                    elus(s + 1)
                if not last:
                    messages(s + 1)
                if not first:
                    residual(s - 1)
                if not last:
                    norm_messages(s + 1)
                if not first:
                    route(s - 1)
                    enter(s - 1)
            elus(0)
            messages(0)
            norm_messages(0)
            step(0, first=True)
            with dve.Fori(1, SUPERS - 1) as s:
                step(s)
            step(SUPERS - 1, last=True)
            norm_feed(SUPERS - 1)
            residual(SUPERS - 1)
            route(SUPERS - 1)
            enter(SUPERS - 1)
            for e in range(EXPERTS):
                dve.wait_ge(m_beta, e + 1)
                nc.vector.tensor_tensor(be1[:, e * HID:(e + 1) * HID], bank[e % 2][:], be1[:, e * HID:(e + 1) * HID],
                                        ALU.add).then_inc(m_bias, 1)
            dve.wait_ge(m_bias, EXPERTS)


def expert_phase(nc, sem, mem, d, keep, out):
    def sb(name, shape, dt=F32):
        return mem.enter_context(nc.sbuf_tensor(f"moe_{name}", shape, dt))

    ident, we1, we2, be1, be2, ends = (keep[k] for k in ("ident", "we1", "we2", "be1", "be2", "ends"))
    region = sb("region", [1, EXPERTS])
    cum = [sb(f"cum{i}", [1, EXPERTS]) for i in range(2)]
    need, need_i = sb("need", [1, EXPERTS]), sb("need_i", [1, EXPERTS], I32)
    tile_no = sb("tile_no", [1, LTILES, EXPERTS])
    past, behind = sb("past", [1, LTILES, EXPERTS]), sb("behind", [1, LTILES, EXPERTS])
    expert_f, gone, row_f = sb("expert_f", [1, LTILES]), sb("gone", [1, LTILES]), sb("row_f", [1, LTILES])
    expert_i, row_i = sb("expert_i", [1, LTILES], I32), sb("row_i", [1, LTILES], I32)
    ents = sb("ents", [P, LTILES, 4])
    source = [sb(f"source{i}", [P, 1], I32) for i in range(2)]
    target = [sb(f"target{i}", [P, 1], I32) for i in range(2)]
    weight = [sb(f"weight{i}", [P, 1]) for i in range(2)]
    rows = [sb(f"rows{i}", [P, D]) for i in range(2)]
    rows_t = sb("rows_t", [P, KD * P])
    hid, hid_act, hid_t = sb("hid", [P, HID]), sb("hid_act", [P, HID]), sb("hid_t", [P, HB * P])
    yb, yw = sb("yb", [P, D]), [sb(f"yw{i}", [P, D]) for i in range(2)]
    ps = lambda n: mem.enter_context(nc.psum_tensor(n, [P, 512], F32))
    p_rows, p_hid, p_hidt, p_y = ps("p_rows"), ps("p_hid"), ps("p_hidt"), ps("p_y")

    y_const, y_plan = sem("y_const"), sem("y_plan")
    y_ents = [sem(f"y_ents{i}") for i in range(2)]
    y_rows = [sem(f"y_rows{i}", pool_dma=True) for i in range(2)]
    y_added = sem("y_added", pool_dma=True)
    y_addfree = sem("y_addfree")
    y_source = sem("y_source")
    y_tr = sem("y_tr")
    y_rowst, y_hid, y_biased, y_gelu, y_htr, y_hidt, y_out, y_yb, y_yw = (sem(f"y_{k}") for k in (
        "rowst", "hid", "biased", "gelu", "htr", "hidt", "out", "yb", "yw"))
    PLAN = 19

    with nc.Block() as block:
        @block.sync
        def _(sp):
            sp.wait_ge(y_plan, PLAN)

            def load(half, b):
                i = half * 2 + b
                row = sp.value_load(row_i[0:1, bass.ds(i, 1)], min_val=0, max_val=EXPERTS * REGION)
                sp.dma_start(ents[:, bass.ds(i, 1), :].rearrange("p o c -> p (o c)"), d["lists"][bass.ds(row, P), :])\
                  .then_inc(y_ents[b], 16)
            load(0, 0)
            load(0, 1)
            with sp.Fori(1, LTILES // 2) as half:
                for b in range(2):
                    sp.wait_ge(y_ents[b], half * 16)
                    sp.sem_inc(keep["turn"], 1)
                    load(half, b)
            sp.wait_ge(y_ents[0], LTILES // 2 * 16)
            load(LTILES // 2, 0)

        @block.gpsimd
        def _(pool):
            nc.gpsimd.iota(region[:], [[REGION, EXPERTS]], base=0, channel_multiplier=0,
                           allow_small_or_imprecise_dtypes=True).then_inc(y_const, 1)
            nc.gpsimd.iota(tile_no[:], [[1, LTILES], [0, EXPERTS]], base=0, channel_multiplier=0,
                           allow_small_or_imprecise_dtypes=True).then_inc(y_const, 1)
            pool.sem_inc(y_addfree, 2)

            def gather(half, b):
                pool.wait_ge(y_source, half * 2 + (b + 1))
                pool.sem_inc(keep["turn"], 1)
                pool.indirect_dma_start(rows[b][:], None, d["table"],
                                        bass.IndirectOffsetOnAxis(ap=source[b][:, 0:1], axis=0)).then_inc(y_rows[b], 16)

            def added(half, b):
                pool.wait_ge(y_added, half * 32 + (b + 1) * 16)
                pool.sem_inc(y_addfree, 1)

            def add(half, b):
                pool.wait_ge(y_yw, half * 2 + (b + 2))
                pool.sem_inc(keep["turn"], 1)
                pool.indirect_dma_start(out, bass.IndirectOffsetOnAxis(ap=target[b][:, 0:1], axis=0),
                                        yw[b][:], None, compute_op=ALU.add).then_inc(y_added, 16)

            def step(half, b, last=None, first=False):
                if last is None or last + AHEAD < LTILES:
                    gather(half + (b + AHEAD) // 2, (b + AHEAD) % 2)
                if not first:
                    added(half + (b - 1) // 2, (b - 1) % 2)
                add(half, b)
            for i in range(AHEAD):
                gather(i // 2, i % 2)
            step(0, 0, first=True)
            step(0, 1)
            with pool.Fori(1, LOOPED // 2) as half:
                step(half, 0)
                step(half, 1)
            for i in range(LOOPED, LTILES):
                step(i // 2, i % 2, i)
            added((LTILES - 1) // 2, (LTILES - 1) % 2)

        @block.tensor
        def _(pe):
            pe.sem_inc(y_tr, 2)
            for s in (y_hid, y_htr, y_out):
                pe.sem_inc(s, 1)

            def turn_rows(half, b):
                i = half * 2 + b
                pe.wait_ge(y_rows[b], half * 16 + 16)
                pe.wait_ge(y_rowst, i + 1)
                for k in range(KD):
                    last = nc.tensor.transpose(p_rows[:, k * P:(k + 1) * P], rows[b][:, k * P:(k + 1) * P], ident[:])
                last.then_inc(y_tr, 1)

            def expert(i):
                return pe.value_load(expert_i[0:1, bass.ds(i, 1)], min_val=0, max_val=EXPERTS - 1)

            def up(i, e):
                pe.wait_ge(y_rowst, i + 2)
                pe.wait_ge(y_biased, i + 1)
                for k in range(KD):
                    last = nc.tensor.matmul(p_hid[:], rows_t[:, k * P:(k + 1) * P],
                                            we1[:, bass.ds(e, 1), k, :].rearrange("p o h -> p (o h)"),
                                            start=(k == 0), stop=(k == KD - 1))
                last.then_inc(y_hid, 1)

            def turn_hidden(half, b):
                i = half * 2 + b
                pe.wait_ge(y_gelu, i + 2)
                pe.wait_ge(y_hidt, i + 1)
                for k in range(HB):
                    last = nc.tensor.transpose(p_hidt[:, k * P:(k + 1) * P], hid_act[:, k * P:(k + 1) * P], ident[:])
                last.then_inc(y_htr, 1)

            def down(i, e):
                pe.wait_ge(y_hidt, i + 2)
                pe.wait_ge(y_yb, i + 1)
                for k in range(HB):
                    last = nc.tensor.matmul(p_y[:, 0:D], hid_t[:, k * P:(k + 1) * P],
                                            we2[:, bass.ds(e, 1), k, :].rearrange("p o f -> p (o f)"),
                                            start=(k == 0), stop=(k == HB - 1))
                last.then_inc(y_out, 1)

            def step(half, b, now, after, last=None):
                turn_hidden(half, b)
                if last is None or last + 1 < LTILES:
                    up(half * 2 + (b + 1), after)
                if last is None or last + 2 < LTILES:
                    turn_rows(half + 1, b)
                down(half * 2 + b, now)
            pe.wait_ge(y_plan, PLAN)
            turn_rows(0, 0)
            up(0, expert(0))
            turn_rows(0, 1)
            with pe.Fori(0, LOOPED // 2) as half:
                now, after = expert(half * 2), expert(half * 2 + 1)
                step(half, 0, now, after)
                now = expert(half * 2 + 2)
                step(half, 1, after, now)
            for i in range(LOOPED, LTILES):
                step(i // 2, i % 2, expert(i), expert(min(i + 1, LTILES - 1)), i)

        @block.scalar
        def _(act):
            for s in (y_rowst, y_gelu, y_hidt, y_yw):
                act.sem_inc(s, 1)

            def copy_rows(i):
                act.wait_ge(y_tr, i + 3)
                act.wait_ge(y_hid, i + 1)
                nc.scalar.activation(rows_t[:], p_rows[:, 0:KD * P], ACT.Copy).then_inc(y_rowst, 1)

            def gelu(i):
                act.wait_ge(y_biased, i + 2)
                act.wait_ge(y_htr, i + 1)
                nc.scalar.activation(hid_act[:], hid[:], ACT.Gelu).then_inc(y_gelu, 1)

            def copy_hidden(i):
                act.wait_ge(y_htr, i + 2)
                act.wait_ge(y_out, i + 1)
                nc.scalar.activation(hid_t[:], p_hidt[:], ACT.Copy).then_inc(y_hidt, 1)

            def weigh(i, b):
                act.wait_ge(y_yb, i + 2)
                act.wait_ge(y_addfree, i + 1)
                nc.scalar.activation(yw[b][:], yb[:], ACT.Copy, scale=weight[b][:]).then_inc(y_yw, 1)

            def step(half, b, last=None):
                i = half * 2 + b
                copy_hidden(i)
                if last is None or last + 2 < LTILES:
                    copy_rows(i + 2)
                if last is None or last + 1 < LTILES:
                    gelu(i + 1)
                weigh(i, b)
            copy_rows(0)
            copy_rows(1)
            gelu(0)
            with act.Fori(0, LOOPED // 2) as half:
                step(half, 0)
                step(half, 1)
            for i in range(LOOPED, LTILES):
                step(i // 2, i % 2, i)

        @block.vector
        def _(dve):
            for s in (y_biased, y_yb):
                dve.sem_inc(s, 1)
            steps = [0]

            def plan(instruction):
                instruction.then_inc(y_plan, 1)
                steps[0] += 1
                dve.wait_ge(y_plan, steps[0])
            dve.wait_ge(y_const, 2)
            plan(nc.vector.tensor_tensor(need[:], ends[0:1, :], region[:], ALU.subtract))
            plan(nc.vector.tensor_scalar(need[:], need[:], float(P - 1), None, ALU.add))
            plan(nc.vector.tensor_copy(need_i[:], need[:]))
            plan(nc.vector.tensor_scalar(need_i[:], need_i[:], 7, None, ALU.logical_shift_right))
            plan(nc.vector.tensor_copy(need[:], need_i[:]))
            plan(nc.vector.tensor_copy(cum[0][:], need[:]))
            n, w = 0, 1
            while w < EXPERTS:
                nc.vector.tensor_copy(cum[1 - n][:, 0:w], cum[n][:, 0:w])
                plan(nc.vector.tensor_tensor(cum[1 - n][:, w:], cum[n][:, w:], cum[n][:, :EXPERTS - w], ALU.add))
                n, w = 1 - n, 2 * w
            plan(nc.vector.tensor_tensor(past[:], tile_no[:], cum[n][:].unsqueeze(1).to_broadcast([1, LTILES, EXPERTS]),
                                         ALU.is_ge))
            plan(nc.vector.tensor_reduce(expert_f[:], past[:], mybir.AxisListType.X, ALU.add))
            plan(nc.vector.tensor_tensor(behind[:], past[:], need[:].unsqueeze(1).to_broadcast([1, LTILES, EXPERTS]),
                                         ALU.mult))
            plan(nc.vector.tensor_reduce(gone[:], behind[:], mybir.AxisListType.X, ALU.add))
            plan(nc.vector.tensor_tensor(gone[:], tile_no[:, :, 0], gone[:], ALU.subtract))
            plan(nc.vector.tensor_scalar(gone[:], gone[:], float(P), None, ALU.mult))
            plan(nc.vector.scalar_tensor_tensor(row_f[:], expert_f[:], float(REGION), gone[:], ALU.mult, ALU.add))
            plan(nc.vector.tensor_scalar(row_f[:], row_f[:], float(EXPERTS * REGION), None, ALU.min))
            nc.vector.tensor_scalar(expert_f[:], expert_f[:], float(EXPERTS - 1), None, ALU.min)
            plan(nc.vector.tensor_copy(row_i[:], row_f[:]))
            plan(nc.vector.tensor_copy(expert_i[:], expert_f[:]))
            assert steps[0] == PLAN, steps

            def sources(half, b):
                i = half * 2 + b
                dve.wait_ge(y_ents[b], half * 16 + 16)
                dve.wait_ge(y_tr, i + 1)
                nc.vector.tensor_copy(source[b][:], ents[:, bass.ds(i, 1), 0]).then_inc(y_source, 1)

            def bias(i):
                e = dve.value_load(expert_i[0:1, bass.ds(i, 1)], min_val=0, max_val=EXPERTS - 1)
                dve.wait_ge(y_hid, i + 2)
                dve.wait_ge(y_gelu, i + 1)
                nc.vector.tensor_tensor(hid[:], p_hid[:], be1[:, bass.ds(e * HID, HID)], ALU.add).then_inc(y_biased, 1)
                return e

            def finish(i, b):
                e = dve.value_load(expert_i[0:1, bass.ds(i, 1)], min_val=0, max_val=EXPERTS - 1)
                dve.wait_ge(y_addfree, i + 1)
                dve.wait_ge(y_yw, i + 1)
                dve.sem_inc(keep["turn"], 1)
                nc.vector.tensor_copy(target[b][:], ents[:, bass.ds(i, 1), 2])
                nc.vector.tensor_copy(weight[b][:], ents[:, bass.ds(i, 1), 1])
                dve.wait_ge(y_out, i + 2)
                nc.vector.tensor_tensor(yb[:], p_y[:, 0:D], be2[:, bass.ds(e * D, D)], ALU.add).then_inc(y_yb, 1)

            def step(half, b, last=None):
                i = half * 2 + b
                if last is None or last + AHEAD < LTILES:
                    sources(half + (b + AHEAD) // 2, (b + AHEAD) % 2)
                if last is None or last + 1 < LTILES:
                    bias(i + 1)
                finish(i, b)
            for i in range(AHEAD):
                sources(i // 2, i % 2)
            bias(0)
            with dve.Fori(0, LOOPED // 2) as half:
                step(half, 0)
                step(half, 1)
            for i in range(LOOPED, LTILES):
                step(i // 2, i % 2, i)


INPUTS = ["x", "src", "dst",
          "gnn_W1_l", "gnn_b1", "gnn_W1_r", "gnn_W2_l", "gnn_b2", "gnn_W2_r",
          "mix_Wq", "mix_Wk", "mix_Wv", "mix_Wm", "mix_W1", "mix_W2", "mix_g1", "mix_b1", "mix_g2", "mix_b2",
          "ffn_gamma", "ffn_beta", "ffn_Wr", "ffn_br", "ffn_W1", "ffn_b1", "ffn_W2", "ffn_b2"]


def kernel(**inputs):
    import numpy as np
    import concourse.bacc as bacc
    from concourse.bass_utils import run_bass_kernel_spmd

    nc = bacc.Bacc("TRN2", target_bir_lowering=False, num_devices=1)
    arrays, t_in = {}, {}
    for name in INPUTS:
        a = np.ascontiguousarray(inputs[name if name in inputs else "L0_" + name])
        if name == "x":
            padded = np.zeros((NPAD, D), a.dtype)
            padded[:N_NODES] = a
            a = padded
        arrays[f"in_{name}"] = a
        t_in[name] = nc.dram_tensor(f"in_{name}", a.shape, mybir.dt.from_np(a.dtype), kind="ExternalInput").ap()
    out = nc.dram_tensor("out", (NPAD + P, D), F32, kind="ExternalOutput").ap()
    program(nc, t_in, out)
    r = run_bass_kernel_spmd(nc, [arrays], core_ids=[0])
    return r.results[0]["out"][:N_NODES]
```
